# Optimizing a Trainium2 kernel written in Bass

```python
import numpy as np
import jax
import jax.numpy as jnp

def _softmax(x, axis=-1):
    return jax.nn.softmax(x, axis=axis)

def _gelu(x):
    return jax.nn.gelu(x, approximate=True)

def _silu(x):
    return jax.nn.silu(x)

def _sigmoid(x):
    return jax.nn.sigmoid(x)

def _layernorm(x, axis=-1, eps=1e-05):
    m = jnp.mean(x, axis=axis, keepdims=True)
    v = jnp.var(x, axis=axis, keepdims=True)
    return (x - m) / jnp.sqrt(v + eps)

def _scatter_add(tgt, idx, src, axis=0):
    return tgt.at[idx].add(src)

def _segment_sum(src, seg, n):
    return jax.ops.segment_sum(src, seg, n)
kernel_name = 'mk_decoder_preln_d2_seqx_r8_9a8519'

def setup_inputs(seed: int=0):
    np.random.seed(seed)
    _w = jnp.asarray

    def _rec_inputs():
        import jax
        import jax.numpy as jnp
        _rk = jax.random.key(seed)
        x = -0.000125 + 0.9999 * jax.random.normal(jax.random.fold_in(_rk, 1), (16, 256, 128), jnp.float32)
        _lenS = 256 - jax.random.randint(jax.random.fold_in(_rk, 7), (16,), 0, max(1, 256 // 4) + 1, jnp.int32)
        _lenS2 = 64 - jax.random.randint(jax.random.fold_in(_rk, 8), (16,), 0, max(1, 64 // 4) + 1, jnp.int32)
        _ctx_1024P = jax.random.normal(jax.random.fold_in(_rk, 11), (16, 16, 128), jnp.float32)
        _ctx_1024c = jax.random.dirichlet(jax.random.fold_in(_rk, 511), 0.3 * jnp.ones((16,), jnp.float32), (16, 64))
        _ctx_1024t = jnp.einsum('bsk,bkd->bsd', _ctx_1024c, _ctx_1024P)
        _ctx_1024t = _ctx_1024t * jax.lax.rsqrt(jnp.mean(jnp.square(_ctx_1024t)) + 1e-12) * 0.953939
        ctx_1024 = -5.72187e-05 + 0.999849 * (_ctx_1024t + 0.3 * jax.random.normal(jax.random.fold_in(_rk, 611), (16, 64, 128), jnp.float32))
        return (x, ctx_1024)
    x, ctx_1024 = _rec_inputs()

    def _L0_attn_setup():
        import jax, jax.numpy as jnp
        import numpy as np
        B, N, D, H, DH = (2, 256, 128, 16, 64)
        key = jax.random.key(seed)
        ks = jax.random.split(key, 5)
        x = jax.random.normal(ks[0], (B, N, D), dtype=jnp.float32)
        Wq = jax.random.normal(ks[1], (D, H * DH), dtype=jnp.float32) * 0.02
        Wk = jax.random.normal(ks[2], (D, H * DH), dtype=jnp.float32) * 0.02
        Wv = jax.random.normal(ks[3], (D, H * DH), dtype=jnp.float32) * 0.02
        Wo = jax.random.normal(ks[4], (H * DH, D), dtype=jnp.float32) * 0.02
        bo = jnp.zeros((D,), dtype=jnp.float32)
        return {'x': x, 'Wq': Wq, 'Wk': Wk, 'Wv': Wv, 'Wo': Wo, 'bo': bo}
    _L0_attn_all = _L0_attn_setup()
    _L0_attn_in = {k: v for k, v in _L0_attn_all.items() if k in ('Wq', 'Wk', 'Wv', 'Wo', 'bo')}
    del _L0_attn_all

    def _L0_xattn_setup():
        import jax, jax.numpy as jnp
        import numpy as np
        EPS = 1e-08
        B, Q, S, D = (128, 32, 64, 128)

        def l2norm(x, axis):
            norm = jnp.sqrt(jnp.sum(x * x, axis=axis, keepdims=True) + EPS) + EPS
            return x / norm
        key = jax.random.key(seed)
        ks = jax.random.split(key, 4)
        return {'query': jax.random.normal(ks[0], (B, Q, D), jnp.float32), 'context': jax.random.normal(ks[1], (B, S, D), jnp.float32), 'W_lin': jax.random.normal(ks[2], (2 * D, D), jnp.float32) * 0.02, 'b_lin': jnp.zeros((D,), jnp.float32), 'W_gate': jax.random.normal(ks[3], (2 * D, D), jnp.float32) * 0.02, 'b_gate': jnp.zeros((D,), jnp.float32), 'smooth': 9}
    _L0_xattn_all = _L0_xattn_setup()
    _L0_xattn_in = {k: v for k, v in _L0_xattn_all.items() if k in ('W_lin', 'b_lin', 'W_gate', 'b_gate')}
    del _L0_xattn_all

    def _L0_ffn_setup():
        import jax, jax.numpy as jnp
        import numpy as np
        B, S, D, F, E, K = (4, 256, 128, 512, 8, 2)
        FS = 128
        LN_EPS = 1e-05

        def _swiglu(x, gu_w, dn_w):
            gate, up = jnp.split(x @ gu_w, 2, axis=-1)
            gate = jnp.clip(gate, -10.0, 10.0)
            return jax.nn.silu(gate) * up @ dn_w
        key = jax.random.key(seed)
        ks = jax.random.split(key, 6)
        s = 0.02
        return {'x': jax.random.normal(ks[0], (B, S, D), jnp.float32), 'ln_gamma': jnp.ones((D,), jnp.float32), 'ln_beta': jnp.zeros((D,), jnp.float32), 'router_w': jax.random.normal(ks[1], (D, E), jnp.float32) * s, 'gate_up_w': jax.random.normal(ks[2], (E, D, 2 * F), jnp.float32) * s, 'down_w': jax.random.normal(ks[3], (E, F, D), jnp.float32) * s, 'shared_gate_up_w': jax.random.normal(ks[4], (D, 2 * FS), jnp.float32) * s, 'shared_down_w': jax.random.normal(ks[5], (FS, D), jnp.float32) * s}
    _L0_ffn_all = _L0_ffn_setup()
    _L0_ffn_in = {k: v for k, v in _L0_ffn_all.items() if k in ('ln_gamma', 'ln_beta', 'router_w', 'gate_up_w', 'down_w', 'shared_gate_up_w', 'shared_down_w')}
    del _L0_ffn_all

    def _L1_attn_setup():
        import jax, jax.numpy as jnp
        import numpy as np
        D_MODEL = 128
        N_HEADS = 16
        D_HEAD = D_MODEL // N_HEADS
        M_SLOPE = 0.5
        BATCH = 2
        SEQ = 256

        def _alibi_bias(n_heads, seq_len, m, dtype):
            slopes = m ** jnp.arange(n_heads, dtype=dtype)
            pos = jnp.arange(seq_len, dtype=dtype)
            dist = jnp.abs(pos[:, None] - pos[None, :])
            return -dist[None, :, :] * slopes[:, None, None]
        key = jax.random.key(seed)
        k1, k2, k3 = jax.random.split(key, 3)
        x = jax.random.normal(k1, (BATCH, SEQ, D_MODEL), dtype=jnp.float32)
        qkv_w = jax.random.normal(k2, (3 * D_MODEL, D_MODEL), dtype=jnp.float32) * (1.0 / np.sqrt(D_MODEL))
        qkv_b = jnp.zeros((3 * D_MODEL,), dtype=jnp.float32)
        out_w = jax.random.normal(k3, (D_MODEL, D_MODEL), dtype=jnp.float32) * (1.0 / np.sqrt(D_MODEL))
        out_b = jnp.zeros((D_MODEL,), dtype=jnp.float32)
        return {'x': x, 'qkv_w': qkv_w, 'qkv_b': qkv_b, 'out_w': out_w, 'out_b': out_b}
    _L1_attn_all = _L1_attn_setup()
    _L1_attn_in = {k: v for k, v in _L1_attn_all.items() if k in ('qkv_w', 'qkv_b', 'out_w', 'out_b')}
    del _L1_attn_all

    def _L1_xattn_setup():
        import jax, jax.numpy as jnp
        import numpy as np
        DIM = 128
        NUM_HEADS = 16
        HEAD_DIM = DIM // NUM_HEADS
        SCALE = HEAD_DIM ** (-0.5)
        key = jax.random.key(seed)
        k1, k2, k3, k4, k5, k6 = jax.random.split(key, 6)
        B, S, L = (4, 1024, 64)
        x = jax.random.normal(k1, (B, S, DIM), dtype=jnp.float32)
        latents = jax.random.normal(k2, (B, L, DIM), dtype=jnp.float32)
        w_q = jax.random.normal(k3, (DIM, DIM), dtype=jnp.float32) * DIM ** (-0.5)
        w_kv = jax.random.normal(k4, (2 * DIM, DIM), dtype=jnp.float32) * DIM ** (-0.5)
        w_out = jax.random.normal(k5, (DIM, DIM), dtype=jnp.float32) * DIM ** (-0.5)
        b_out = jax.random.normal(k6, (DIM,), dtype=jnp.float32) * 0.01
        return {'x': x, 'latents': latents, 'w_q': w_q, 'w_kv': w_kv, 'w_out': w_out, 'b_out': b_out}
    _L1_xattn_all = _L1_xattn_setup()
    _L1_xattn_in = {k: v for k, v in _L1_xattn_all.items() if k in ('w_q', 'w_kv', 'w_out', 'b_out')}
    del _L1_xattn_all

    def _L1_ffn_setup():
        import jax, jax.numpy as jnp
        import numpy as np
        TOP_K = 2
        key = jax.random.key(seed)
        ks = jax.random.split(key, 8)
        B, S, H, I, E = (2, 256, 128, 64, 8)
        SI = 2 * I
        scale = 0.02
        return {'x': jax.random.normal(ks[0], (B, S, H), jnp.float32), 'gate_w': jax.random.normal(ks[1], (H, E), jnp.float32) * scale, 'wg': jax.random.normal(ks[2], (E, H, I), jnp.float32) * scale, 'wu': jax.random.normal(ks[3], (E, H, I), jnp.float32) * scale, 'wd': jax.random.normal(ks[4], (E, I, H), jnp.float32) * scale, 'sg': jax.random.normal(ks[5], (H, SI), jnp.float32) * scale, 'su': jax.random.normal(ks[6], (H, SI), jnp.float32) * scale, 'sd': jax.random.normal(ks[7], (SI, H), jnp.float32) * scale}
    _L1_ffn_all = _L1_ffn_setup()
    _L1_ffn_in = {k: v for k, v in _L1_ffn_all.items() if k in ('gate_w', 'wg', 'wu', 'wd', 'sg', 'su', 'sd')}
    del _L1_ffn_all
    return {'x': x, 'ctx_1024': ctx_1024, 'L0_attn_Wq': _L0_attn_in['Wq'], 'L0_attn_Wk': _L0_attn_in['Wk'], 'L0_attn_Wv': _L0_attn_in['Wv'], 'L0_attn_Wo': _L0_attn_in['Wo'], 'L0_attn_bo': _L0_attn_in['bo'], 'L0_xattn_W_lin': _L0_xattn_in['W_lin'], 'L0_xattn_b_lin': _L0_xattn_in['b_lin'], 'L0_xattn_W_gate': _L0_xattn_in['W_gate'], 'L0_xattn_b_gate': _L0_xattn_in['b_gate'], 'L0_ffn_ln_gamma': _L0_ffn_in['ln_gamma'], 'L0_ffn_ln_beta': _L0_ffn_in['ln_beta'], 'L0_ffn_router_w': _L0_ffn_in['router_w'], 'L0_ffn_gate_up_w': _L0_ffn_in['gate_up_w'], 'L0_ffn_down_w': _L0_ffn_in['down_w'], 'L0_ffn_shared_gate_up_w': _L0_ffn_in['shared_gate_up_w'], 'L0_ffn_shared_down_w': _L0_ffn_in['shared_down_w'], 'L1_attn_qkv_w': _L1_attn_in['qkv_w'], 'L1_attn_qkv_b': _L1_attn_in['qkv_b'], 'L1_attn_out_w': _L1_attn_in['out_w'], 'L1_attn_out_b': _L1_attn_in['out_b'], 'L1_xattn_w_q': _L1_xattn_in['w_q'], 'L1_xattn_w_kv': _L1_xattn_in['w_kv'], 'L1_xattn_w_out': _L1_xattn_in['w_out'], 'L1_xattn_b_out': _L1_xattn_in['b_out'], 'L1_ffn_gate_w': _L1_ffn_in['gate_w'], 'L1_ffn_wg': _L1_ffn_in['wg'], 'L1_ffn_wu': _L1_ffn_in['wu'], 'L1_ffn_wd': _L1_ffn_in['wd'], 'L1_ffn_sg': _L1_ffn_in['sg'], 'L1_ffn_su': _L1_ffn_in['su'], 'L1_ffn_sd': _L1_ffn_in['sd']}

def reference(x, ctx_1024, L0_attn_Wq, L0_attn_Wk, L0_attn_Wv, L0_attn_Wo, L0_attn_bo, L0_xattn_W_lin, L0_xattn_b_lin, L0_xattn_W_gate, L0_xattn_b_gate, L0_ffn_ln_gamma, L0_ffn_ln_beta, L0_ffn_router_w, L0_ffn_gate_up_w, L0_ffn_down_w, L0_ffn_shared_gate_up_w, L0_ffn_shared_down_w, L1_attn_qkv_w, L1_attn_qkv_b, L1_attn_out_w, L1_attn_out_b, L1_xattn_w_q, L1_xattn_w_kv, L1_xattn_w_out, L1_xattn_b_out, L1_ffn_gate_w, L1_ffn_wg, L1_ffn_wu, L1_ffn_wd, L1_ffn_sg, L1_ffn_su, L1_ffn_sd):
    import jax
    import jax.numpy as jnp

    def _L0_attn_ref(x, Wq, Wk, Wv, Wo, bo):
        import jax, jax.numpy as jnp
        import numpy as np
        B, N, D, H, DH = (2, 256, 128, 16, 64)
        b, n, _ = x.shape
        scale = DH ** (-0.5)
        q = (x @ Wq).reshape(b, n, H, DH)
        k = (x @ Wk).reshape(b, n, H, DH)
        v = (x @ Wv).reshape(b, n, H, DH)
        base = (2.0 ** 8) ** (1.0 / H)
        slope = 1.0 / base ** jnp.arange(1, H + 1, dtype=jnp.float32)
        pos = jnp.arange(n, dtype=jnp.float32)
        bias = slope[:, None, None] * (pos[:, None] - pos[None, :])
        scores = jnp.einsum('bihd,bjhd->bhij', q, k) * scale + bias[None]
        causal = pos[:, None] >= pos[None, :]
        scores = jnp.where(causal[None, None], scores, jnp.float32(-1e+30))
        attn = jax.nn.softmax(scores, axis=-1)
        out = jnp.einsum('bhij,bjhd->bihd', attn, v).reshape(b, n, H * DH)
        return out @ Wo + bo

    def _L0_xattn_ref(query, context, W_lin, b_lin, W_gate, b_gate, smooth):
        import jax, jax.numpy as jnp
        import numpy as np
        EPS = 1e-08
        B, Q, S, D = (128, 32, 64, 128)

        def l2norm(x, axis):
            norm = jnp.sqrt(jnp.sum(x * x, axis=axis, keepdims=True) + EPS) + EPS
            return x / norm
        attn = jnp.einsum('bsd,bqd->bsq', context, query)
        attn = jax.nn.leaky_relu(attn, negative_slope=0.1)
        attn = l2norm(attn, axis=2)
        a = jax.nn.softmax(jnp.swapaxes(attn, 1, 2) * smooth, axis=2)
        weighted_ctx = jnp.einsum('bqs,bsd->bqd', a, context)
        cat = jnp.concatenate([query, weighted_ctx], axis=2)
        h = jnp.tanh(cat @ W_lin + b_lin)
        g = jax.nn.sigmoid(cat @ W_gate + b_gate)
        return query * g + h * (1.0 - g)

    def _L0_ffn_ref(x, ln_gamma, ln_beta, router_w, gate_up_w, down_w, shared_gate_up_w, shared_down_w):
        import jax, jax.numpy as jnp
        import numpy as np
        B, S, D, F, E, K = (4, 256, 128, 512, 8, 2)
        FS = 128
        LN_EPS = 1e-05

        def _swiglu(x, gu_w, dn_w):
            gate, up = jnp.split(x @ gu_w, 2, axis=-1)
            gate = jnp.clip(gate, -10.0, 10.0)
            return jax.nn.silu(gate) * up @ dn_w
        b, s, d = x.shape
        xf = x.reshape(-1, d)
        mu = jnp.mean(xf, axis=-1, keepdims=True)
        var = jnp.var(xf, axis=-1, keepdims=True)
        xn = (xf - mu) * jax.lax.rsqrt(var + LN_EPS) * ln_gamma + ln_beta
        logits = xn @ router_w
        probs = jax.nn.softmax(logits, axis=-1)
        topv, topi = jax.lax.top_k(probs, K)
        topv = topv / jnp.sum(topv, axis=-1, keepdims=True)
        comb = jnp.sum(jax.nn.one_hot(topi, E, dtype=xn.dtype) * topv[..., None], axis=1)
        out = jnp.zeros_like(xf)
        for e in range(E):
            out = out + comb[:, e:e + 1] * _swiglu(xn, gate_up_w[e], down_w[e])
        out = out + _swiglu(xn, shared_gate_up_w, shared_down_w)
        return out.reshape(b, s, d)

    def _L1_attn_ref(x, qkv_w, qkv_b, out_w, out_b):
        import jax, jax.numpy as jnp
        import numpy as np
        D_MODEL = 128
        N_HEADS = 16
        D_HEAD = D_MODEL // N_HEADS
        M_SLOPE = 0.5
        BATCH = 2
        SEQ = 256

        def _alibi_bias(n_heads, seq_len, m, dtype):
            slopes = m ** jnp.arange(n_heads, dtype=dtype)
            pos = jnp.arange(seq_len, dtype=dtype)
            dist = jnp.abs(pos[:, None] - pos[None, :])
            return -dist[None, :, :] * slopes[:, None, None]
        batch, seq_len, d_model = x.shape
        qkv = x @ qkv_w.T + qkv_b
        qkv = qkv.reshape(batch, seq_len, N_HEADS, 3 * D_HEAD).transpose(0, 2, 1, 3)
        q, k, v = jnp.split(qkv, 3, axis=-1)
        scale = jnp.sqrt(jnp.asarray(D_HEAD, dtype=x.dtype))
        scores = jnp.einsum('bhid,bhjd->bhij', q, k) / scale
        scores = scores + _alibi_bias(N_HEADS, seq_len, M_SLOPE, x.dtype)[None]
        attn = jax.nn.softmax(scores, axis=-1)
        out = jnp.einsum('bhij,bhjd->bhid', attn, v)
        out = out.transpose(0, 2, 1, 3).reshape(batch, seq_len, d_model)
        return out @ out_w.T + out_b

    def _L1_xattn_ref(x, latents, w_q, w_kv, w_out, b_out):
        import jax, jax.numpy as jnp
        import numpy as np
        DIM = 128
        NUM_HEADS = 16
        HEAD_DIM = DIM // NUM_HEADS
        SCALE = HEAD_DIM ** (-0.5)
        B, L, _ = latents.shape
        S = x.shape[1]
        q = latents @ w_q.T
        kv = x @ w_kv.T
        k, v = jnp.split(kv, 2, axis=-1)
        q = q.reshape(B, L, NUM_HEADS, HEAD_DIM)
        k = k.reshape(B, S, NUM_HEADS, HEAD_DIM)
        v = v.reshape(B, S, NUM_HEADS, HEAD_DIM)
        attn = jnp.einsum('blhd,bshd->bhls', q, k) * SCALE
        attn = jax.nn.softmax(attn, axis=-1)
        out = jnp.einsum('bhls,bshd->blhd', attn, v)
        out = out.reshape(B, L, DIM)
        return out @ w_out.T + b_out

    def _L1_ffn_ref(x, gate_w, wg, wu, wd, sg, su, sd):
        import jax, jax.numpy as jnp
        import numpy as np
        TOP_K = 2
        B, S, H = x.shape
        E = gate_w.shape[1]
        T = B * S
        xt = x.reshape(T, H)
        logits = xt @ gate_w
        scores = jax.nn.softmax(logits, axis=-1)
        top_w, top_i = jax.lax.top_k(scores, TOP_K)
        top_w = top_w / jnp.sum(top_w, axis=-1, keepdims=True)
        cw = jnp.zeros((T, E), x.dtype).at[jnp.arange(T)[:, None], top_i].set(top_w)
        g = jnp.einsum('th,ehi->eti', xt, wg)
        u = jnp.einsum('th,ehi->eti', xt, wu)
        h = jax.nn.silu(g) * u
        eo = jnp.einsum('eti,eih->eth', h, wd)
        moe = jnp.einsum('eth,te->th', eo, cw)
        gs = xt @ sg
        us = xt @ su
        shared = jax.nn.silu(gs) * us @ sd
        return (moe + shared).reshape(B, S, H)
    x = x + _L0_attn_ref(_layernorm(x, axis=-1), L0_attn_Wq, L0_attn_Wk, L0_attn_Wv, L0_attn_Wo, L0_attn_bo)
    x = x + _L0_xattn_ref(_layernorm(x, axis=-1), ctx_1024, L0_xattn_W_lin, L0_xattn_b_lin, L0_xattn_W_gate, L0_xattn_b_gate, 9)
    x = x + _L0_ffn_ref(_layernorm(x, axis=-1), L0_ffn_ln_gamma, L0_ffn_ln_beta, L0_ffn_router_w, L0_ffn_gate_up_w, L0_ffn_down_w, L0_ffn_shared_gate_up_w, L0_ffn_shared_down_w)
    x = x + _L1_attn_ref(_layernorm(x, axis=-1), L1_attn_qkv_w, L1_attn_qkv_b, L1_attn_out_w, L1_attn_out_b)
    x = x + _L1_xattn_ref(ctx_1024, _layernorm(x, axis=-1), L1_xattn_w_q, L1_xattn_w_kv, L1_xattn_w_out, L1_xattn_b_out)
    x = x + _L1_ffn_ref(_layernorm(x, axis=-1), L1_ffn_gate_w, L1_ffn_wg, L1_ffn_wu, L1_ffn_wd, L1_ffn_sg, L1_ffn_su, L1_ffn_sd)
    return x

_drawn_inputs = setup_inputs


def setup_inputs(seed=0):
    import zlib

    import numpy as np

    out = dict(_drawn_inputs(seed))
    spreads = {'L0_attn_bo': (0.0, 0.1),
     'L0_xattn_b_lin': (0.0, 0.1),
     'L0_xattn_b_gate': (0.0, 0.457),
     'L0_ffn_ln_gamma': (1.0, 0.6),
     'L0_ffn_ln_beta': (0.0, 0.8),
     'L1_attn_qkv_b': (0.0, 0.8),
     'L1_attn_out_b': (0.0, 0.8)}
    factors = {'L0_attn_Wq': 8.0,
     'L0_attn_Wk': 8.0,
     'L0_ffn_router_w': 8.0,
     'L0_ffn_gate_up_w': 8.0,
     'L0_ffn_down_w': 8.0,
     'L0_ffn_shared_gate_up_w': 8.0,
     'L0_ffn_shared_down_w': 8.0,
     'L1_xattn_b_out': 63.72,
     'L1_ffn_gate_w': 8.0,
     'L1_ffn_wg': 8.0,
     'L1_ffn_wu': 8.0,
     'L1_ffn_wd': 8.0,
     'L1_ffn_sg': 8.0,
     'L1_ffn_su': 8.0,
     'L1_ffn_sd': 8.0,
     'L1_attn_qkv_w': 3.197,
     'L1_attn_out_w': 2.806,
     'L1_xattn_w_q': 4.407}
    for name, (base, spread) in spreads.items():
        noise = np.random.default_rng([zlib.crc32(name.encode()), seed]).standard_normal(out[name].shape)
        drawn = base * np.exp(spread * noise) if base else spread * noise
        out[name] = jnp.asarray(drawn.astype(out[name].dtype))
    for name, factor in factors.items():
        out[name] = (out[name] * factor).astype(out[name].dtype)
    return out
```

```python
from contextlib import ExitStack

import numpy as np
import concourse.bass as bass
from concourse import mybir

F32 = mybir.dt.float32
F32R = mybir.dt.float32r
BF16 = mybir.dt.bfloat16
I32 = mybir.dt.int32
ALU = mybir.AluOpType
ACT = mybir.ActivationFunctionType
AX = mybir.AxisListType

P = 128
B = 16
S = 256
D = 128
L = 64
H = 16
T = B * S
NT = T // P
BT = S // P
DH0 = 64
PAIRS = H // 2
E = 8
F0 = 512
CAUSAL = P + 2 * P
MOE_BLOCKS = -(-(2 * T + E * (P - 1)) // P // 4) * 4
CLIP = 10.0
LN_EPS = 1e-5
MASKED = 1e30
LEAST = 3e38
START = 1


class Phase:

    def __init__(self, nc, ctx, tag):
        self.nc, self.ctx, self.tag = nc, ctx, tag
        self.sems = []
        ctx.callback(self.release)

    def sb(self, name, shape, dt=F32):
        return self.ctx.enter_context(self.nc.sbuf_tensor(f"{self.tag}_{name}", shape, dt))

    def ps(self, name, shape, dt=F32):
        return self.ctx.enter_context(self.nc.psum_tensor(f"{self.tag}_{name}", shape, dt))

    def sem(self, name):
        self.sems.append(self.nc.alloc_semaphore(f"{self.tag}_{name}"))
        return self.sems[-1]

    def release(self):
        self.nc.clear_and_free_semaphores(self.sems)
        self.nc.all_engine_barrier()


class LayerNorm:

    def __init__(self, ph, g, tag, keep_rows=False, source=None, scale=None, shift=None):
        self.g, self.keep_rows = g, keep_rows
        self.source, self.scale, self.shift = g.x if source is None else source, scale, shift
        if scale is not None:
            self.plain = ph.sb(f"{tag}_plain", [P, 2, BT, D])
            self.scaled = ph.sb(f"{tag}_scaled", [P, 2, BT, D])
            self.plain_done = ph.sem(f"{tag}_plain_done")
            self.scaled_done = ph.sem(f"{tag}_scaled_done")
        self.nc = ph.nc
        self.partial = ph.sb(f"{tag}_partial", [P, 2, BT, 6])
        self.moments = ph.sb(f"{tag}_moments", [P, 2, BT, 2])
        self.shifted = ph.sb(f"{tag}_shifted", [P, 2, BT])
        self.power = ph.sb(f"{tag}_power", [P, 2, BT])
        self.rows = ph.sb(f"{tag}_rows", [P, 2, BT, D])
        self.halves_done = ph.sem(f"{tag}_halves_done")
        self.moments_done = ph.sem(f"{tag}_moments_done")
        self.shift_done = ph.sem(f"{tag}_shift_done")
        self.rstd_done = ph.sem(f"{tag}_rstd_done")
        self.rows_done = ph.sem(f"{tag}_rows_done")
        self.turned = ph.sem(f"{tag}_turned")
        self.kept = ph.sem(f"{tag}_kept")

    def stats(self, dve, b, j=0):
        nc, g = self.nc, self.g
        for k in range(BT):
            nc.vector.bn_stats(self.partial[:, j, k, :], self.source[:, bass.ds(b * BT + k, 1), :]).then_inc(self.halves_done, 1)

    def stats_landed(self, dve, b):
        dve.wait_ge(self.halves_done, b * BT + BT)

    def aggregate(self, dve, b, j=0):
        nc = self.nc
        for k in range(BT):
            nc.vector.bn_aggr(self.moments[:, j, k, :], self.partial[:, j, k, :]).then_inc(self.moments_done, 1)

    def rstd(self, pool, b, j=0):
        nc, g = self.nc, self.g
        pool.wait_ge(self.moments_done, b * BT + BT)
        nc.gpsimd.tensor_tensor(self.shifted[:, j, :], self.moments[:, j, :, 1], g.eps[:, 0:BT],
                                ALU.add).then_inc(self.shift_done, 1)
        pool.wait_ge(self.shift_done, b + 1)
        nc.gpsimd.tensor_tensor(self.power[:, j, :], self.shifted[:, j, :], g.minus_half[:, 0:BT],
                                ALU.pow).then_inc(self.rstd_done, 1)

    def apply(self, dve, b, j=0, ahead=1):
        nc, g = self.nc, self.g
        dve.wait_ge(self.rstd_done, b + 1)
        if not (isinstance(b, int) and b < ahead):
            dve.wait_ge(self.turned, START + b - ahead + 1)
        out, done = (self.rows, self.rows_done) if self.scale is None else (self.plain, self.plain_done)
        kept = g.rows[:, bass.ds(b * BT, BT), :]
        for k in range(BT):
            args = (self.source[:, bass.ds(b * BT + k, 1), :], self.moments[:, j, k, 0:1], self.power[:, j, k:k + 1],
                    ALU.subtract, ALU.mult)
            nc.vector.tensor_scalar(out[:, j, k, :], *args).then_inc(done, 1)
            if self.keep_rows and self.scale is None:
                nc.vector.tensor_scalar(g.rows[:, bass.ds(b * BT + k, 1), :], *args)
        if self.scale is not None:
            dve.wait_ge(self.plain_done, b * BT + BT)
            nc.vector.tensor_tensor(self.scaled[:, j, :, :], self.plain[:, j, :, :], self.scale, ALU.mult).then_inc(self.scaled_done, 1)
            dve.wait_ge(self.scaled_done, b + 1)
            nc.vector.tensor_tensor(self.rows[:, j, :, :], self.scaled[:, j, :, :], self.shift, ALU.add).then_inc(self.rows_done, BT)
            if self.keep_rows:
                nc.vector.tensor_tensor(kept, self.scaled[:, j, :, :], self.shift, ALU.add)

    def turn(self, pe, b, out, j=0):
        pe.wait_ge(self.rows_done, b * BT + BT)
        for k in range(BT):
            mm = pe.transpose(out[:, k * P:(k + 1) * P], self.rows[:, j, k, :], self.g.ident[:])
        mm.then_inc(self.turned, 1)

    def start_turned(self, pe):
        pe.sem_inc(self.turned, START)

    def start_kept(self, act):
        act.sem_inc(self.kept, START)

    def wait_kept(self, pe, count):
        pe.wait_ge(self.kept, START + count)

    def keep(self, act, b, turned):
        act.wait_ge(self.turned, START + b + 1)
        self.nc.scalar.copy(self.g.xnT[:, bass.ds(b * S, S)], turned).then_inc(self.kept, 1)

    def all_turns(self, pe, psN):
        self.start_turned(pe)
        for j in range(2):
            self.turn(pe, j, psN[:, j, :], j)
        with pe.Fori(1, B // 2) as h:
            for j in range(2):
                self.wait_kept(pe, h * 2 + j - 1)
                self.turn(pe, h * 2 + j, psN[:, j, :], j)

    def all_keeps(self, act, psN):
        self.start_kept(act)
        with act.Fori(0, B // 2) as h:
            for j in range(2):
                self.keep(act, h * 2 + j, psN[:, j, 0:S])

    def all_rstds(self, pool):
        with pool.Fori(0, B // 2) as h:
            for j in range(2):
                self.rstd(pool, h * 2 + j, j)

    def all_rows(self, dve):
        def step(b, j):
            self.stats(dve, b + 1, 1 - j)
            self.stats_landed(dve, b + 1)
            self.apply(dve, b, j, 2)
            self.aggregate(dve, b + 1, 1 - j)

        self.stats(dve, 0, 0)
        self.stats_landed(dve, 0)
        self.aggregate(dve, 0, 0)
        for j in range(2):
            step(j, j)
        with dve.Fori(1, B // 2 - 1) as h:
            for j in range(2):
                step(h * 2 + j, j)
        step(B - 2, 0)
        self.apply(dve, B - 1, 1, 2)


def rounds(eng, new, count=B):
    new(0, True, lambda p, lag: p >= lag)
    with eng.Fori(1, count) as r:
        new(r, True, lambda p, lag: True)
    new(count, False, lambda p, lag: p < lag)


def load_and_prepare(nc, g, d, rest):
    with ExitStack() as ctx:
        ph = Phase(nc, ctx, "prep")
        wqT = ph.sb("wqT", [P, PAIRS, D])
        wkT = ph.sb("wkT", [P, PAIRS, D])
        psG = ph.ps("psG", [P, 4, 512])
        psN = ph.ps("psN", [P, 2, 512])
        psC = ph.ps("psC", [P, 2, 512])
        x_in = [ph.sem(f"x_in{i}") for i in range(8)]
        qk_in = ph.sem("qk_in")
        ident_in = ph.sem("ident_in")
        ctx_in = ph.sem("ctx_in")
        rest_in = ph.sem("rest_in")
        half_set = ph.sem("half_set")
        g_done = ph.sem("g_done")
        c_done = ph.sem("c_done")
        ln = LayerNorm(ph, g, "ln")
        block = ctx.enter_context(nc.Block())
        XB = NT // len(x_in)
        zero_set = ph.sem("zero_set")
        slots_cleared = ph.sem("slots_cleared")
        zero = ph.sb("zero", [P, MOE_BLOCKS * D // 8])
        by_part = g.sorted_in.rearrange("(p r) d -> p (r d)", p=P)

        @block.sync
        def _(sp):
            sp.dma_start(g.ident[:], d["ident"]).then_inc(ident_in, 16)
            for i, sem in enumerate(x_in):
                sp.dma_start(g.x[:, i * XB:(i + 1) * XB, :],
                             d["x"][i * XB * P:(i + 1) * XB * P, :].rearrange("(t p) d -> p t d", p=P)).then_inc(sem, 16)
                if i == 0:
                    sp.dma_start(wqT[:], d["wqT"]).then_inc(qk_in, 16)
                    sp.dma_start(wkT[:], d["wkT"]).then_inc(qk_in, 16)
                if i == 3:
                    sp.dma_start(g.ctx[:], d["ctx"]).then_inc(ctx_in, 16)
            for dst, src in rest:
                sp.dma_start(dst, src).then_inc(rest_in, 16)
            sp.wait_ge(zero_set, 1)
            for i in range(8):
                w = MOE_BLOCKS * D // 8
                sp.dma_start(by_part[:, i * w:(i + 1) * w], zero[:]).then_inc(slots_cleared, 16)
            sp.wait_ge(rest_in, 16 * len(rest))
            sp.wait_ge(slots_cleared, 16 * 8)

        @block.gpsimd
        def _(pool):
            nc.gpsimd.memset(zero[:], 0.0).then_inc(zero_set, 1)
            nc.gpsimd.memset(g.eps[:], LN_EPS).then_inc(half_set, 1)
            nc.gpsimd.memset(g.minus_half[:], -0.5).then_inc(half_set, 1)
            pool.wait_ge(half_set, 2)
            ln.all_rstds(pool)

        @block.tensor
        def _(pe):
            pe.wait_ge(ident_in, 16)
            pe.wait_ge(qk_in, 32)
            for h in range(H):
                k, q, j = h % 2, h // 8, (h % 8) // 2
                mm = pe.matmul(psG[:, 2 * q + k, j * P:(j + 1) * P], wqT[k * DH0:(k + 1) * DH0, h // 2, :],
                               wkT[k * DH0:(k + 1) * DH0, h // 2, :], start=True, stop=True)
                mm.then_inc(g_done, 1)
            pe.wait_ge(ctx_in, 16)
            for c in range(B * L // P):
                mm = pe.transpose(psC[:, c // 4, (c % 4) * P:(c % 4 + 1) * P], g.ctx[:, c, :], g.ident[:])
            mm.then_inc(c_done, 1)
            ln.all_turns(pe, psN)

        @block.scalar
        def _(act):
            for q in range(2):
                act.wait_ge(g_done, 8 * q + 8)
                for k in range(2):
                    nc.scalar.copy(g.G[:, 8 * q + k:8 * q + 8:2, :], psG[:, 2 * q + k, :].rearrange("p (h d) -> p h d", h=4))
            act.wait_ge(c_done, 1)
            nc.scalar.copy(g.ctxT[:].rearrange("p (a c) -> p a c", a=2), psC[:])
            ln.all_keeps(act, psN)

        @block.vector
        def _(dve):
            for sem in x_in:
                dve.wait_ge(sem, 16)
            ln.all_rows(dve)


def layer0_attention(nc, g, d):
    with ExitStack() as ctx:
        ph = Phase(nc, ctx, "a0")
        psA = ph.ps("psA", [P, 2, S])
        psS = ph.ps("psS", [P, 4, 512])
        psT = ph.ps("psT", [P, 512])
        psO = ph.ps("psO", [P, 512])
        psM = ph.ps("psM", [P, 512])
        cur = ph.sb("cur", [P, S])
        a_sb = ph.sb("a", [P, 2, 2, S])
        prob = ph.sb("prob", [P, 8, CAUSAL])
        probT = ph.sb("probT", [P, 4, CAUSAL])
        low = ph.sb("low", [P, 4, 2])
        total = ph.sb("total", [P, 4, 2])
        inv = ph.sb("inv", [P, 4, 2])
        v_sb = ph.sb("v", [P, BT, H * DH0])
        o_sb = ph.sb("o", [P, PAIRS, S])
        resid = ph.sb("resid", [P, BT, D])
        cur_ready = ph.sem("cur_ready")
        a_done = ph.sem("a_done")
        a_kept = ph.sem("a_kept")
        s_done = ph.sem("s_done")
        low_done = ph.sem("low_done")
        exp_done = ph.sem("exp_done")
        inv_done = ph.sem("inv_done")
        norm_done = ph.sem("norm_done")
        t_done = ph.sem("t_done")
        t_kept = ph.sem("t_kept")
        v_done = ph.sem("v_done")
        v_kept = ph.sem("v_kept")
        pv_done = ph.sem("pv_done")
        o_kept = ph.sem("o_kept")
        y_done = ph.sem("y_done")
        y_used = ph.sem("y_used")
        x_done = ph.sem("x_done")
        seen = ph.sem("seen")
        ln = LayerNorm(ph, g, "ln", keep_rows=True)
        block = ctx.enter_context(nc.Block())
        blocks = [(0, 0, P), (1, P, 3 * P)]

        @block.tensor
        def _(pe):
            ln.start_turned(pe)
            def project(b, p):
                pe.wait_ge(a_kept, b * PAIRS + p)
                for k in range(2):
                    mm = pe.matmul(psA[:, k, :], g.G[:, 2 * p + k, :], g.xnT[:, bass.ds(b * S, S)], start=True, stop=True)
                mm.then_inc(a_done, 1)

            def scores(b, p, has_unit):
                pe.wait_ge(a_kept, b * PAIRS + p + 1)
                if has_unit(p, 2):
                    pe.wait_ge(exp_done, b * 32 + 4 * p - 4)
                for k in range(2):
                    for i, lo, hi in blocks:
                        mm = pe.matmul(psS[:, 2 * (p % 2) + k, lo:hi], a_sb[:, p % 2, k, i * P:(i + 1) * P],
                                       g.xnT[:, bass.ds(b * S, hi - lo)], start=True, stop=True)
                    mm.then_inc(s_done, 1)

            def values_in(b, p, has_unit):
                if p == 4 and has_unit(p, 8):
                    pe.wait_ge(y_used, b)
                elif p or has_unit(p, 8):
                    pe.wait_ge(v_kept, b * PAIRS + p)
                if p == 0 and has_unit(p, 8):
                    ln.wait_kept(pe, b - 1)
                if p == 0:
                    pe.wait_ge(cur_ready, b + 1)
                mm = pe.matmul(psM[:, 0:S], cur[:, (p % 2) * P:(p % 2 + 1) * P], g.wv[:, (p // 2) * S:(p // 2 + 1) * S],
                               start=True, stop=True)
                mm.then_inc(v_done, 1)

            def values(b, p):
                pe.wait_ge(t_kept, b * H + 2 * p - 4)
                pe.wait_ge(v_kept, b * PAIRS + 2 * ((p - 3) // 2) + 2)
                pe.wait_ge(o_kept, b * PAIRS + p - 3)
                q = (p - 3) % PAIRS
                for j, lo, hi in ((0, 0, S), (1, P, S)):
                    for k in range(2):
                        h = 2 * q + k
                        pt = probT[:, 2 * (q % 2) + k, 0:S] if j == 0 else probT[:, 2 * (q % 2) + k, S:CAUSAL]
                        mm = pe.matmul(psO[k * DH0:(k + 1) * DH0, lo:hi], v_sb[:, j, h * DH0:(h + 1) * DH0], pt,
                                       start=(j == 0), stop=(j == 1), skip_group_check=True)
                mm.then_inc(pv_done, 1)

            def turn(b, p, k):
                pe.wait_ge(norm_done, b * 32 + 4 * p - 6 + 2 * k)
                pe.wait_ge(t_kept, b * H + 2 * p - 4 + k)
                q = (p - 2) % PAIRS
                for c in range(3):
                    mm = pe.transpose(psT[:, c * P:(c + 1) * P], prob[:, 2 * (q % 4) + k, c * P:(c + 1) * P], g.ident[:])
                mm.then_inc(t_done, 1)

            def output(b):
                pe.wait_ge(o_kept, b * PAIRS)
                for i in range(BT):
                    for q in range(PAIRS):
                        mm = pe.matmul(psM[:, i * P:(i + 1) * P], o_sb[:, q, i * P:(i + 1) * P], g.wo[:, q, :],
                                       start=(q == 0), stop=(q == PAIRS - 1))
                mm.then_inc(y_done, 1)

            def tail_of_batch_before(b, p, new):
                if new:
                    pe.wait_ge(v_kept, b * PAIRS + p + 1)
                elif p == 7:
                    pe.wait_ge(y_used, b)
                else:
                    pe.wait_ge(v_kept, b * PAIRS)
                    ln.wait_kept(pe, b - 1)
                if p == 3:
                    output(b)
                else:
                    ln.turn(pe, b - 1, psM)

            def slots(b, new, has_unit):
                for p in range(PAIRS):
                    if new and p == 0:
                        project(b, 0)
                    elif new:
                        scores(b, p, has_unit)
                    if has_unit(p, 2):
                        turn(b, p, 0)
                    if new and p == 0:
                        values_in(b, p, has_unit)
                    if new and 0 < p < PAIRS - 1:
                        project(b, p + 1)
                    elif new and p == PAIRS - 1:
                        values_in(b, p, has_unit)
                    if has_unit(p, 2):
                        turn(b, p, 1)
                    if new and p == 0:
                        project(b, 1)
                    elif new and p < PAIRS - 1:
                        values_in(b, p, has_unit)
                    if p == 3 and has_unit(p, 8):
                        tail_of_batch_before(b, p, new)
                    if has_unit(p, 3):
                        values(b, p)
                    if p == 7 and has_unit(p, 8):
                        tail_of_batch_before(b, p, new)
                    if new and p == 0:
                        scores(b, p, has_unit)

            rounds(pe, slots)

        @block.scalar
        def _(act):
            ln.start_kept(act)
            def keep_a(b, p):
                act.wait_ge(a_done, b * PAIRS + p + 1)
                if p >= 2:
                    act.wait_ge(s_done, b * H + 2 * p - 2)
                nc.scalar.activation(a_sb[:, p % 2, :, :], psA[:], ACT.Copy, scale=-(DH0 ** -0.5)).then_inc(a_kept, 1)

            def keep_t(b, p, k):
                q = (p - 2) % PAIRS
                if not (isinstance(b, int) and b == 0 and p < 4):
                    act.wait_ge(pv_done, b * PAIRS + p - 3)
                act.wait_ge(t_done, b * H + 2 * p - 3 + k)
                nc.scalar.copy(probT[:, 2 * (q % 2) + k, :], psT[:, 0:CAUSAL]).then_inc(t_kept, 1)

            def exps(b, p, has_unit):
                if has_unit(p, 4):
                    act.wait_ge(t_done, b * H + 2 * p - 6)
                for k in range(2):
                    u = 2 * (p % 2) + k
                    act.wait_ge(low_done, b * 32 + 4 * p + 2 * k + 2)
                    for i, lo, hi in blocks:
                        nc.scalar.activation(prob[:, 2 * (p % 4) + k, lo:hi], psS[:, u, lo:hi], ACT.Exp, bias=low[:, u, i:i + 1],
                                             scale=-1.0, accum_out=total[:, u, i:i + 1]).then_inc(exp_done, 1)

            def slots(b, new, has_unit):
                for p in range(PAIRS):
                    if new and p == 0:
                        if has_unit(p, 8):
                            act.wait_ge(v_done, b * PAIRS)
                        nc.scalar.copy(cur[:], g.xnT[:, bass.ds(b * S, S)]).then_inc(cur_ready, 1)
                    if new and p == 0:
                        keep_a(b, 0)
                    if has_unit(p, 2):
                        keep_t(b, p, 0)
                    if new and 0 < p < PAIRS - 1:
                        keep_a(b, p + 1)
                    if has_unit(p, 2):
                        keep_t(b, p, 1)
                    if new and p == 0:
                        keep_a(b, 1)
                    if new:
                        exps(b, p, has_unit)
                    if p == 7 and has_unit(p, 8):
                        ln.keep(act, b - 1, psM[:, 0:S])

            rounds(act, slots)

        @block.vector
        def _(dve):
            def lows(b, p, has_unit):
                if has_unit(p, 2):
                    dve.wait_ge(exp_done, b * 32 + 4 * p - 4)
                for k in range(2):
                    u = 2 * (p % 2) + k
                    dve.wait_ge(s_done, b * H + 2 * p + k + 1)
                    dve.sem_inc(seen, 1)
                    for i, lo, hi in blocks:
                        nc.vector.tensor_tensor_reduce(psS[:, u, lo:hi], psS[:, u, lo:hi], g.bias0[:, 2 * p + k, lo:hi],
                                                       1.0, LEAST, ALU.add, ALU.min, low[:, u, i:i + 1]).then_inc(low_done, 1)

            def norm(b, p):
                q = (p - 1) % PAIRS
                u = slice(2 * (q % 2), 2 * (q % 2) + 2)
                dve.wait_ge(exp_done, b * 32 + 4 * p)
                nc.vector.reciprocal(inv[:, u, :], total[:, u, :]).then_inc(inv_done, 1)
                dve.wait_ge(inv_done, b * PAIRS + p)
                for k in range(2):
                    for i, lo, hi in blocks:
                        w = prob[:, 2 * (q % 4) + k, lo:hi]
                        nc.vector.tensor_scalar(w, w, inv[:, 2 * (q % 2) + k, i:i + 1], None, ALU.mult).then_inc(norm_done, 1)

            def keep_o(b, p):
                q = (p - 3) % PAIRS
                if p == 3 and not (isinstance(b, int) and b == 0):
                    dve.wait_ge(y_done, b)
                dve.wait_ge(pv_done, b * PAIRS + p - 2)
                nc.vector.tensor_copy(o_sb[:, q, :], psO[:, 0:S]).then_inc(o_kept, 1)

            def slots(b, new, has_unit):
                for p in range(PAIRS):
                    if p == 5 and has_unit(p, 8):
                        ln.stats_landed(dve, b - 1)
                    if p == 6 and has_unit(p, 8):
                        ln.apply(dve, b - 1)
                    if new:
                        lows(b, p, has_unit)
                    if has_unit(p, 1):
                        norm(b, p)
                    if new:
                        dve.wait_ge(v_done, b * PAIRS + p + 1)
                        nc.vector.tensor_copy(v_sb[:, p % 2, (p // 2) * S:(p // 2 + 1) * S], psM[:, 0:S]).then_inc(v_kept, 1)
                    if p == 3 and has_unit(p, 8):
                        dve.wait_ge(y_done, b)
                        nc.vector.tensor_tensor(resid[:], psM[:, 0:S].rearrange("p (t d) -> p t d", t=BT),
                                                g.x[:, bass.ds((b - 1) * BT, BT), :], ALU.add).then_inc(y_used, 1)
                        dve.wait_ge(y_used, b)
                        nc.vector.tensor_tensor(g.x[:, bass.ds((b - 1) * BT, BT), :], resid[:], g.bo[:], ALU.add).then_inc(x_done, 1)
                    if has_unit(p, 3):
                        keep_o(b, p)
                    if p == 4 and has_unit(p, 8):
                        dve.wait_ge(x_done, b)
                        dve.sem_inc(seen, 1)
                        ln.stats(dve, b - 1)
                    if p == 5 and has_unit(p, 8):
                        if not new:
                            dve.sem_inc(seen, 1)
                        ln.aggregate(dve, b - 1)

            rounds(dve, slots)

        @block.gpsimd
        def _(pool):
            with pool.Fori(0, B) as b:
                ln.rstd(pool, b)


def layer0_context(nc, g, d):
    UQ = 2 * S
    UB = UQ // P
    EPS = 1e-8
    SMOOTH = 9.0
    with ExitStack() as ctx:
        ph = Phase(nc, ctx, "c0")
        psX = ph.ps("psX", [P, 512])
        psW = ph.ps("psW", [P, 2, 512])
        psV = ph.ps("psV", [P, 512])
        psC = ph.ps("psC", [P, UB, 2 * D])
        psN = ph.ps("psN", [P, 2, 512])
        q_cur = ph.sb("q_cur", [P, 2, UQ])
        ctxT_cur = ph.sb("ctxT_cur", [P, 2, 2 * L])
        ctx1_cur = ph.sb("ctx1_cur", [P, 2, D + 1])
        tenth = ph.sb("tenth", [P, S])
        leaky = ph.sb("leaky", [P, 2, S])
        square = ph.sb("square", [P, S])
        norm2 = ph.sb("norm2", [P, 1])
        norm2e = ph.sb("norm2e", [P, 1])
        root = ph.sb("root", [P, 1])
        length = ph.sb("length", [P, 1])
        inv = ph.sb("inv", [P, 1])
        sharp = ph.sb("sharp", [P, 1])
        consts = ph.sb("consts", [P, 2])
        e_bd = ph.sb("e_bd", [P, 2, UQ])
        invz = ph.sb("invz", [P, UB])
        w_rows = ph.sb("w_rows", [P, UB, D])
        w_sb = ph.sb("w", [P, UQ])
        pre = ph.sb("pre", [P, UB, 2 * D])
        hid = ph.sb("hid", [P, UB, D])
        gate = ph.sb("gate", [P, UB, D])
        diff = ph.sb("diff", [P, UB, D])
        part = ph.sb("part", [P, UB, D])
        mix = ph.sb("mix", [P, UB, D])
        consts_set = ph.sem("consts_set")
        cur_ready = ph.sem("cur_ready")
        ctx_ready = ph.sem("ctx_ready")
        x_scores = ph.sem("x_scores")
        tenth_done = ph.sem("tenth_done")
        leaky_done = ph.sem("leaky_done")
        square_done = ph.sem("square_done")
        root_steps = ph.sem("root_steps")
        sharp_steps = ph.sem("sharp_steps")
        e_done = ph.sem("e_done")
        w_done = ph.sem("w_done")
        invz_done = ph.sem("invz_done")
        rows_done = ph.sem("rows_done")
        w_turned = ph.sem("w_turned")
        w_kept = ph.sem("w_kept")
        c_done = ph.sem("c_done")
        pre_done = ph.sem("pre_done")
        tanh_done = ph.sem("tanh_done")
        mix_steps = ph.sem("mix_steps")
        x_done = ph.sem("x_done")
        ln = LayerNorm(ph, g, "ln", keep_rows=True)
        block = ctx.enter_context(nc.Block())
        ROUNDS = B // 4
        experts_in = ph.sem("experts_in")

        @block.sync
        def _(sp):
            for i in range(4):
                n = 2 * E // 4
                sp.dma_start(g.gate_up[:, i * n:(i + 1) * n, :], d["gate_up"][:, i * n:(i + 1) * n, :]).then_inc(experts_in, 16)
            sp.dma_start(g.down[:], d["down"]).then_inc(experts_in, 16)
            sp.wait_ge(experts_in, 16 * 5)

        @block.tensor
        def _(pe):
            ln.start_turned(pe)
            pe.wait_ge(consts_set, 4)
            def slots(r, new, has_unit):
                for p in range(2):
                    n = r * 2 + p
                    if new:
                        pe.wait_ge(cur_ready, n + 1)
                        pe.wait_ge(ctx_ready, n * 2 + 2)
                        if has_unit(p, 1):
                            pe.wait_ge(leaky_done, n)
                        for j in range(2):
                            mm = pe.matmul(psX[j * L:(j + 1) * L, 0:S], ctxT_cur[:, p, j * L:(j + 1) * L],
                                           q_cur[:, p, j * S:(j + 1) * S], start=True, stop=True)
                        mm.then_inc(x_scores, 1)
                    if has_unit(p, 1):
                        pe.wait_ge(e_done, n * 2)
                        pe.wait_ge(rows_done, n - 1)
                        for k in range(UB):
                            mm = pe.matmul(psW[:, k // 2, (k % 2) * 256:(k % 2) * 256 + D + 1], e_bd[:, 1 - p, k * P:(k + 1) * P],
                                           ctx1_cur[:, 1 - p, :], start=True, stop=True)
                        mm.then_inc(w_done, 1)
                    if has_unit(p, 2):
                        ln.wait_kept(pe, n * 2 - 4)
                        for j in range(2):
                            ln.turn(pe, n * 2 - 4 + j, psN[:, j, :], j)
                    if has_unit(p, 1):
                        pe.wait_ge(rows_done, n)
                        for k in range(UB):
                            mm = pe.transpose(psV[:, k * P:(k + 1) * P], w_rows[:, k, :], g.ident[:])
                        mm.then_inc(w_turned, 1)
                        pe.wait_ge(pre_done, n - 1)
                        for k in range(UB):
                            pe.matmul(psC[:, k, :], q_cur[:, 1 - p, k * P:(k + 1) * P], g.wcat[:, 0, :], start=True, stop=False)
                            if k == 0:
                                pe.wait_ge(w_kept, n)
                            mm = pe.matmul(psC[:, k, :], w_sb[:, k * P:(k + 1) * P], g.wcat[:, 1, :], start=False, stop=True)
                        mm.then_inc(c_done, 1)

            rounds(pe, slots, ROUNDS)

        @block.scalar
        def _(act):
            ln.start_kept(act)
            def slots(r, new, has_unit):
                for p in range(2):
                    n = r * 2 + p
                    if new:
                        if has_unit(p, 2):
                            act.wait_ge(c_done, n - 1)
                        nc.scalar.copy(q_cur[:, p, :], g.xnT[:, bass.ds(n * UQ, UQ)]).then_inc(cur_ready, 1)
                    if new:
                        act.wait_ge(sharp_steps, n * 3 + 3)
                        for j in range(2):
                            rows = slice(j * L, (j + 1) * L)
                            nc.scalar.activation(e_bd[rows, p, j * S:(j + 1) * S], leaky[rows, p, :], ACT.Exp,
                                                 scale=sharp[rows, 0:1]).then_inc(e_done, 1)
                    if has_unit(p, 2):
                        for j in range(2):
                            ln.keep(act, n * 2 - 4 + j, psN[:, j, 0:S])
                    if has_unit(p, 1):
                        act.wait_ge(w_turned, n)
                        if has_unit(p, 2):
                            act.wait_ge(c_done, n - 1)
                        nc.scalar.copy(w_sb[:], psV[:]).then_inc(w_kept, 1)
                        act.wait_ge(pre_done, n)
                        nc.scalar.activation(hid[:], pre[:, :, 0:D], ACT.Tanh).then_inc(tanh_done, 1)
                        nc.scalar.activation(gate[:], pre[:, :, D:2 * D], ACT.Tanh, scale=0.5).then_inc(tanh_done, 1)

            rounds(act, slots, ROUNDS)

        @block.gpsimd
        def _(pool):
            nc.gpsimd.memset(ctx1_cur[:, :, D:D + 1], 1.0).then_inc(consts_set, 1)
            nc.gpsimd.memset(consts[:, 0:1], EPS).then_inc(consts_set, 1)
            nc.gpsimd.memset(consts[:, 1:2], 0.5).then_inc(consts_set, 1)
            nc.gpsimd.memset(e_bd[:], 0.0).then_inc(consts_set, 1)
            pool.wait_ge(consts_set, 4)

            def slots(r, new, has_unit):
                for p in range(2):
                    n = r * 2 + p
                    if new:
                        pool.wait_ge(square_done, n + 1)
                        nc.gpsimd.tensor_tensor(norm2e[:], norm2[:], consts[:, 0:1], ALU.add).then_inc(root_steps, 1)
                        pool.wait_ge(root_steps, n * 2 + 1)
                        nc.gpsimd.tensor_tensor(root[:], norm2e[:], consts[:, 1:2], ALU.pow).then_inc(root_steps, 1)
                    if has_unit(p, 1):
                        for j in range(2):
                            ln.rstd(pool, n * 2 - 2 + j, j)

            rounds(pool, slots, ROUNDS)

        @block.vector
        def _(dve):
            dve.wait_ge(consts_set, 4)

            def slots(r, new, has_unit):
                for p in range(2):
                    n = r * 2 + p
                    if new:
                        if has_unit(p, 2):
                            dve.wait_ge(w_done, n - 1)
                        nc.vector.tensor_copy(ctxT_cur[:, p, :], g.ctxT[:, bass.ds(n * 2 * L, 2 * L)]).then_inc(ctx_ready, 1)
                        nc.vector.tensor_copy(ctx1_cur[:, p, 0:D], g.ctx[:, bass.ds(n, 1), :]).then_inc(ctx_ready, 1)
                        dve.wait_ge(x_scores, n + 1)
                        nc.vector.tensor_scalar(tenth[:], psX[:, 0:S], 0.1, None, ALU.mult).then_inc(tenth_done, 1)
                        dve.wait_ge(tenth_done, n + 1)
                        if has_unit(p, 2):
                            dve.wait_ge(e_done, n * 2 - 2)
                        nc.vector.tensor_tensor(leaky[:, p, :], psX[:, 0:S], tenth[:], ALU.max).then_inc(leaky_done, 1)
                        dve.wait_ge(leaky_done, n + 1)
                        nc.vector.tensor_tensor_reduce(square[:], leaky[:, p, :], leaky[:, p, :], 1.0, 0.0, ALU.mult, ALU.add,
                                                       norm2[:]).then_inc(square_done, 1)
                    if has_unit(p, 1):
                        dve.wait_ge(w_done, n)
                        nc.vector.reciprocal(invz[:], psW[:].rearrange("p b (k c) -> p (b k) c", c=256)[:, :, D]).then_inc(invz_done, 1)
                        dve.wait_ge(invz_done, n)
                        if has_unit(p, 2):
                            dve.wait_ge(w_turned, n - 1)
                        for k in range(UB):
                            at = psW[:, k // 2, (k % 2) * 256:(k % 2) * 256 + D]
                            i = nc.vector.tensor_scalar(w_rows[:, k, :], at, invz[:, k:k + 1], None, ALU.mult)
                        i.then_inc(rows_done, 1)
                    if new:
                        dve.wait_ge(root_steps, n * 2 + 2)
                        if has_unit(p, 1):
                            dve.wait_ge(e_done, n * 2)
                        nc.vector.tensor_scalar(length[:], root[:], EPS, None, ALU.add).then_inc(sharp_steps, 1)
                        dve.wait_ge(sharp_steps, n * 3 + 1)
                        nc.vector.reciprocal(inv[:], length[:]).then_inc(sharp_steps, 1)
                        dve.wait_ge(sharp_steps, n * 3 + 2)
                        nc.vector.tensor_scalar(sharp[:], inv[:], SMOOTH, None, ALU.mult).then_inc(sharp_steps, 1)
                    if has_unit(p, 2):
                        for j in range(2):
                            ln.apply(dve, n * 2 - 4 + j, j)
                    if has_unit(p, 1):
                        dve.wait_ge(c_done, n)
                        if has_unit(p, 2):
                            dve.wait_ge(tanh_done, n * 2 - 2)
                        nc.vector.tensor_tensor(pre[:], psC[:], g.bcat[:], ALU.add).then_inc(pre_done, 1)
                    if has_unit(p, 1):
                        m = n - 1
                        rows = bass.ds(m * UB, UB)
                        dve.wait_ge(tanh_done, m * 2 + 2)
                        nc.vector.tensor_tensor(diff[:], g.rows[:, rows, :], hid[:], ALU.subtract).then_inc(mix_steps, 1)
                        dve.wait_ge(mix_steps, m * 3 + 1)
                        nc.vector.scalar_tensor_tensor(out=part[:], in0=gate[:], scalar=1.0, in1=diff[:], op0=ALU.add,
                                                       op1=ALU.mult).then_inc(mix_steps, 1)
                        dve.wait_ge(mix_steps, m * 3 + 2)
                        nc.vector.scalar_tensor_tensor(out=mix[:], in0=part[:], scalar=0.5, in1=hid[:], op0=ALU.mult,
                                                       op1=ALU.add).then_inc(mix_steps, 1)
                        dve.wait_ge(mix_steps, m * 3 + 3)
                        nc.vector.tensor_tensor(g.x[:, rows, :], g.x[:, rows, :], mix[:], ALU.add).then_inc(x_done, 1)
                        dve.wait_ge(x_done, m + 1)
                        for j in range(2):
                            ln.stats(dve, m * 2 + j, j)
                        ln.stats_landed(dve, m * 2 + 1)
                        dve.sem_inc(seen, 1)
                        for j in range(2):
                            ln.aggregate(dve, m * 2 + j, j)

            seen = ph.sem("seen")
            rounds(dve, slots, ROUNDS)


class Routing:

    def __init__(self, ph, g, tag):
        self.g, self.nc = g, ph.nc
        full = lambda name: ph.sb(f"{tag}_{name}", [P, NT, E])
        col = lambda name: ph.sb(f"{tag}_{name}", [P, NT])
        self.logits, self.hit, self.score, self.rest = full("logits"), full("hit"), full("score"), full("rest")
        self.best, self.first, self.second, self.pick = col("best"), col("first"), col("second"), col("pick")
        self.gap, self.e_gap, self.one_plus = col("gap"), col("e_gap"), col("one_plus")
        self.step = ph.sem(f"{tag}_step")
        self.gap_done = ph.sem(f"{tag}_gap_done")
        self.exp_done = ph.sem(f"{tag}_exp_done")
        self.count = 0

    def then(self, dve, instruction):
        instruction.then_inc(self.step, 1)
        self.count += 1
        dve.wait_ge(self.step, self.count)

    def choose(self, dve, psum, top, weight):
        v, g = self.nc.vector, self.g
        wide = lambda t: t[:].unsqueeze(2).to_broadcast([P, NT, E])
        self.then(dve, v.tensor_copy(self.logits[:], psum))
        source, bests = self.logits, (self.first, self.second)
        for k in range(2):
            self.then(dve, v.tensor_reduce(bests[k][:], source[:], AX.X, ALU.max))
            self.then(dve, v.tensor_tensor(self.hit[:], source[:], wide(bests[k]), ALU.is_ge))
            self.then(dve, v.tensor_tensor(self.score[:], self.hit[:], g.countdown[:], ALU.mult))
            self.then(dve, v.tensor_reduce(self.pick[:], self.score[:], AX.X, ALU.max))
            self.then(dve, v.tensor_tensor(top[:, k, :, :], g.countdown[:], wide(self.pick), ALU.is_equal))
            if k == 0:
                self.then(dve, v.tensor_scalar(self.hit[:], top[:, 0, :, :], -LEAST, None, ALU.mult))
                self.then(dve, v.tensor_tensor(self.rest[:], self.logits[:], self.hit[:], ALU.add))
                source = self.rest
        v.tensor_tensor(self.gap[:], self.second[:], self.first[:], ALU.subtract).then_inc(self.gap_done, 1)
        dve.wait_ge(self.exp_done, 1)
        self.then(dve, v.tensor_scalar(self.one_plus[:], self.e_gap[:], 1.0, None, ALU.add))
        self.then(dve, v.reciprocal(weight[:, 0, :], self.one_plus[:]))
        self.then(dve, v.tensor_tensor(weight[:, 1, :], self.e_gap[:], weight[:, 0, :], ALU.mult))

    def exponent(self, act):
        act.wait_ge(self.gap_done, 1)
        self.nc.scalar.activation(self.e_gap[:], self.gap[:], ACT.Exp).then_inc(self.exp_done, 1)


def layer0_route(nc, g, d):
    with ExitStack() as ctx:
        ph = Phase(nc, ctx, "r0")
        psN = ph.ps("psN", [P, 2, 512])
        psL = ph.ps("psL", [P, NT, E])
        psR = ph.ps("psR", [P, NT, E])
        psK = ph.ps("psK", [P, NT, E])
        top_sum = ph.sb("top_sum", [P, NT, E], BF16)
        zeros = ph.sb("zeros", [P, NT])
        upto = ph.sb("upto", [P, NT, E])
        before = ph.sb("before", [P, NT, E])
        rank = ph.sb("rank", [P, NT, E])
        padded = ph.sb("padded", [P, E])
        padded_i = ph.sb("padded_i", [P, E], I32)
        blocks_i = ph.sb("blocks_i", [P, E], I32)
        blocks = ph.sb("blocks", [P, E])
        ends = ph.sb("ends", [P, E])
        base = ph.sb("base", [P, E])
        place = ph.sb("place", [P, NT, E])
        chosen = ph.sb("chosen", [P, NT, E])
        slot_f = ph.sb("slot_f", [P, NT])
        late = ph.sb("late", [P, MOE_BLOCKS, E])
        expert_f = ph.sb("expert_f", [P, MOE_BLOCKS])
        expert_c = ph.sb("expert_c", [P, MOE_BLOCKS])
        logits_done = ph.sem("logits_done")
        top_ready = ph.sem("top_ready")
        ranks_done = ph.sem("ranks_done")
        ln = LayerNorm(ph, g, "ln", keep_rows=True, source=g.rows, scale=g.gamma[:], shift=g.beta[:])
        route = Routing(ph, g, "rt")
        block = ctx.enter_context(nc.Block())

        @block.tensor
        def _(pe):
            ln.all_turns(pe, psN)
            ln.wait_kept(pe, B)
            for t in range(NT):
                mm = pe.matmul(psL[:, t, :], g.xnT[:, t * P:(t + 1) * P], g.router[:], start=True, stop=True)
            mm.then_inc(logits_done, 1)
            pe.wait_ge(top_ready, 1)
            pe.matmul(psR[:], g.before_mask[:], top_sum[:], start=True, stop=True)
            pe.matmul(psK[:], g.ones_bf[:], top_sum[:], start=True, stop=True).then_inc(ranks_done, 1)

        @block.scalar
        def _(act):
            ln.all_keeps(act, psN)
            route.exponent(act)

        @block.gpsimd
        def _(pool):
            ln.all_rstds(pool)

        @block.vector
        def _(dve):
            v = nc.vector
            v.memset(zeros[:], 0.0)
            ln.all_rows(dve)
            dve.wait_ge(logits_done, 1)
            route.choose(dve, psL[:], g.top, g.weight)
            then = lambda i: route.then(dve, i)
            v.tensor_tensor(top_sum[:], g.top[:, 0, :, :], g.top[:, 1, :, :], ALU.add).then_inc(top_ready, 1)
            dve.wait_ge(ranks_done, 1)
            for e in range(E):
                i = v.tensor_tensor_scan(upto[:, :, e], psK[:, :, e], zeros[:], 0.0, ALU.add, ALU.add)
            then(i)
            then(v.tensor_tensor(before[:], upto[:], psK[:], ALU.subtract))
            then(v.tensor_tensor(rank[:], before[:], psR[:], ALU.add))
            then(v.tensor_scalar(padded[:], upto[:, NT - 1, :], float(P - 1), None, ALU.add))
            then(v.tensor_copy(padded_i[:], padded[:]))
            then(v.tensor_scalar(blocks_i[:], padded_i[:], 7, None, ALU.logical_shift_right))
            then(v.tensor_copy(blocks[:], blocks_i[:]))
            then(v.tensor_tensor_scan(ends[:], blocks[:], zeros[:, 0:E], 0.0, ALU.add, ALU.add))
            then(v.tensor_tensor(padded[:], ends[:], blocks[:], ALU.subtract))
            then(v.tensor_scalar(base[:], padded[:], float(P), None, ALU.mult))
            then(v.tensor_tensor(place[:], rank[:], base[:].unsqueeze(1).to_broadcast([P, NT, E]), ALU.add))
            for k in range(2):
                then(v.tensor_tensor(chosen[:], place[:], g.top[:, k, :, :], ALU.mult))
                then(v.tensor_reduce(slot_f[:], chosen[:], AX.X, ALU.add))
                then(v.tensor_copy(g.slot[:, k, :], slot_f[:]))
            then(v.tensor_tensor(late[:], g.block_index[:].unsqueeze(2).to_broadcast([P, MOE_BLOCKS, E]),
                                 ends[:].unsqueeze(1).to_broadcast([P, MOE_BLOCKS, E]), ALU.is_ge))
            then(v.tensor_reduce(expert_f[:], late[:], AX.X, ALU.add))
            then(v.tensor_scalar(expert_c[:], expert_f[:], float(E - 1), None, ALU.min))
            then(v.tensor_copy(g.expert[:], expert_c[:]))


class SharedExpert:

    def __init__(self, ph, g, tag, w_in, w_out, clip):
        self.g, self.nc, self.w_in, self.w_out, self.clip = g, ph.nc, w_in, w_out, clip
        self.psG = ph.ps(f"{tag}_psG", [P, 512])
        self.psU = ph.ps(f"{tag}_psU", [P, 512])
        self.psY = ph.ps(f"{tag}_psY", [P, 4, D])
        self.gate = ph.sb(f"{tag}_gate", [P, 2, 512])
        self.act = ph.sb(f"{tag}_act", [P, 2, 512])
        self.hid = ph.sb(f"{tag}_hid", [P, 2, 512])
        self.in_done, self.clipped = ph.sem(f"{tag}_in_done"), ph.sem(f"{tag}_clipped")
        self.silu_done, self.hid_done = ph.sem(f"{tag}_silu_done"), ph.sem(f"{tag}_hid_done")
        self.y_done, self.x_done = ph.sem(f"{tag}_y_done"), ph.sem(f"{tag}_x_done")

    def tensor(self, pe, n, p, new, lagging):
        g = self.g
        if new:
            pe.wait_ge(self.hid_done, n)
            pe.matmul(self.psG[:], self.w_in[:, 0:P], g.xnT[:, bass.ds(n * 512, 512)], start=True, stop=True)
            pe.matmul(self.psU[:], self.w_in[:, P:2 * P], g.xnT[:, bass.ds(n * 512, 512)], start=True, stop=True).then_inc(self.in_done, 1)
        if lagging:
            pe.wait_ge(self.hid_done, n)
            pe.wait_ge(self.x_done, n - 1)
            for k in range(4):
                mm = pe.matmul(self.psY[:, k, :], self.hid[:, 1 - p, k * P:(k + 1) * P], self.w_out, start=True, stop=True)
            mm.then_inc(self.y_done, 1)

    def scalar(self, act, n, p, new, lagging):
        if new:
            act.wait_ge(self.clipped if self.clip else self.in_done, n + 1)
            src = self.gate[:, p, :] if self.clip else self.psG[:]
            self.nc.scalar.activation(self.act[:, p, :], src, ACT.Silu).then_inc(self.silu_done, 1)

    def vector(self, dve, n, p, new, lagging):
        v, g = self.nc.vector, self.g
        if new:
            dve.wait_ge(self.in_done, n + 1)
            if self.clip:
                v.tensor_scalar(self.gate[:, p, :], self.psG[:], CLIP, -CLIP, ALU.min, ALU.max).then_inc(self.clipped, 1)
            dve.wait_ge(self.silu_done, n + 1)
            v.tensor_tensor(self.hid[:, p, :], self.act[:, p, :], self.psU[:], ALU.mult).then_inc(self.hid_done, 1)
        if lagging:
            rows = bass.ds((n - 1) * 4, 4)
            dve.wait_ge(self.y_done, n)
            v.tensor_tensor(g.x[:, rows, :], g.x[:, rows, :], self.psY[:], ALU.add).then_inc(self.x_done, 1)

    def slots(self, step):
        def body(r, new, has_unit):
            for p in range(2):
                step(r * 2 + p, p, new, has_unit(p, 1))
        return body


def layer0_shared_and_dispatch(nc, g, d):
    with ExitStack() as ctx:
        ph = Phase(nc, ctx, "s0")
        shared = SharedExpert(ph, g, "sh", g.shared_in0, g.shared_out0[:], True)
        sent = ph.sem("sent")
        block = ctx.enter_context(nc.Block())

        @block.gpsimd
        def _(pool):
            for k in range(2):
                for t in range(NT):
                    nc.gpsimd.indirect_dma_start(out=g.sorted_in, out_offset=bass.IndirectOffsetOnAxis(ap=g.slot[:, k, t:t + 1], axis=0),
                                                 in_=g.rows[:, t, :], in_offset=None).then_inc(sent, 16)
            pool.wait_ge(sent, 16 * 2 * NT)

        @block.tensor
        def _(pe):
            rounds(pe, shared.slots(lambda *a: shared.tensor(pe, *a)), T // 1024)

        @block.scalar
        def _(act):
            rounds(act, shared.slots(lambda *a: shared.scalar(act, *a)), T // 1024)

        @block.vector
        def _(dve):
            rounds(dve, shared.slots(lambda *a: shared.vector(dve, *a)), T // 1024)


def layer0_experts(nc, g, d):
    FC = F0 // P
    with ExitStack() as ctx:
        ph = Phase(nc, ctx, "e0")
        psX = ph.ps("psX", [P, 512])
        psG = ph.ps("psG", [P, 2, 512])
        psU = ph.ps("psU", [P, 2, 512])
        psH = ph.ps("psH", [P, 512])
        psY = ph.ps("psY", [P, 512])
        rows = ph.sb("rows", [P, 4, D])
        cols = ph.sb("cols", [P, 2, P])
        gate = ph.sb("gate", [P, F0])
        act_sb = ph.sb("act", [P, F0])
        hid = ph.sb("hid", [P, 4, F0])
        hidT = ph.sb("hidT", [P, F0])
        y_sb = ph.sb("y", [P, 2, D])
        rows_in = [ph.sem(f"rows_in{i}") for i in range(4)]
        turned = ph.sem("turned")
        cols_kept = ph.sem("cols_kept")
        gate_in = ph.sem("gate_in")
        in_done = ph.sem("in_done")
        clipped = ph.sem("clipped")
        silu_done = ph.sem("silu_done")
        hid_done = ph.sem("hid_done")
        h_turned = ph.sem("h_turned")
        h_kept = ph.sem("h_kept")
        y_done = ph.sem("y_done")
        y_kept = ph.sem("y_kept")
        y_out = [ph.sem(f"y_out{i}") for i in range(2)]
        block = ctx.enter_context(nc.Block())
        N = MOE_BLOCKS
        src = g.sorted_in.rearrange("(n p) d -> p n d", p=P)
        dst = g.sorted_out.rearrange("(n p) d -> p n d", p=P)

        @block.sync
        def _(sp):
            for n in range(4):
                sp.dma_start(rows[:, n, :], src[:, n, :]).then_inc(rows_in[n], 16)
            with sp.Fori(0, N // 4 - 1) as r:
                for k in range(4):
                    n = r * 4 + k
                    sp.wait_ge(turned, n + 1)
                    sp.dma_start(rows[:, k, :], src[:, bass.ds(n + 4, 1), :]).then_inc(rows_in[k], 16)

        @block.gpsimd
        def _(pool):
            with pool.Fori(0, N // 2) as r:
                for k in range(2):
                    pool.wait_ge(y_kept, r * 2 + k + 1)
                    nc.gpsimd.dma_start(dst[:, bass.ds(r * 2 + k, 1), :], y_sb[:, k, :]).then_inc(y_out[k], 16)
            for k in range(2):
                pool.wait_ge(y_out[k], 16 * (N // 2))

        def each(eng, slot):
            def body(r, new, has_unit):
                for p in range(4):
                    slot(r * 4 + p, p, new, has_unit(p, 2))
            rounds(eng, body, N // 4)

        @block.tensor
        def _(pe):
            def slot(n, p, new, lagging):
                if new:
                    pe.wait_ge(rows_in[p], (n - p) * 4 + 16)
                    pe.wait_ge(cols_kept, n)
                    pe.transpose(psX[:, 0:P], rows[:, p, :], g.ident[:]).then_inc(turned, 1)
                if lagging:
                    pe.wait_ge(hid_done, n - 1)
                    pe.wait_ge(h_kept, n - 2)
                    for c in range(FC):
                        mm = pe.transpose(psH[:, c * P:(c + 1) * P], hid[:, (p + 2) % 4, c * P:(c + 1) * P], g.ident[:])
                    mm.then_inc(h_turned, 1)
                if new:
                    e = pe.value_load(g.expert[0:1, bass.ds(n, 1)], min_val=0, max_val=E - 1)
                    pe.wait_ge(cols_kept, n + 1)
                    pe.matmul(psG[:, p % 2, :], cols[:, p % 2, :], g.gate_up[:, bass.ds(e * 2, 1), :], start=True,
                              stop=True).then_inc(gate_in, 1)
                    pe.matmul(psU[:, p % 2, :], cols[:, p % 2, :], g.gate_up[:, bass.ds(e * 2 + 1, 1), :], start=True,
                              stop=True).then_inc(in_done, 1)
                if lagging:
                    e = pe.value_load(g.expert[0:1, bass.ds(n - 2, 1)], min_val=0, max_val=E - 1)
                    pe.wait_ge(h_kept, n - 1)
                    pe.wait_ge(y_kept, n - 2)
                    for c in range(FC):
                        mm = pe.matmul(psY[:, 0:D], hidT[:, c * P:(c + 1) * P], g.down[:, bass.ds(e * FC + c, 1), :],
                                       start=(c == 0), stop=(c == FC - 1))
                    mm.then_inc(y_done, 1)

            each(pe, slot)

        @block.scalar
        def _(act):
            def slot(n, p, new, lagging):
                if new:
                    act.wait_ge(turned, n + 1)
                    if lagging:
                        act.wait_ge(in_done, n - 1)
                    nc.scalar.copy(cols[:, p % 2, :], psX[:, 0:P]).then_inc(cols_kept, 1)
                if lagging:
                    act.wait_ge(h_turned, n - 1)
                    act.wait_ge(y_done, n - 2)
                    nc.scalar.copy(hidT[:], psH[:]).then_inc(h_kept, 1)
                if new:
                    act.wait_ge(clipped, n + 1)
                    nc.scalar.activation(act_sb[:], gate[:], ACT.Silu).then_inc(silu_done, 1)

            each(act, slot)

        @block.vector
        def _(dve):
            def slot(n, p, new, lagging):
                if new:
                    dve.wait_ge(gate_in, n + 1)
                    nc.vector.tensor_scalar(gate[:], psG[:, p % 2, :], CLIP, -CLIP, ALU.min, ALU.max).then_inc(clipped, 1)
                    dve.wait_ge(silu_done, n + 1)
                    dve.wait_ge(in_done, n + 1)
                    if not (isinstance(n, int) and n < 4):
                        dve.wait_ge(h_turned, n - 3)
                    nc.vector.tensor_tensor(hid[:, p, :], act_sb[:], psU[:, p % 2, :], ALU.mult).then_inc(hid_done, 1)
                if lagging:
                    dve.wait_ge(y_done, n - 1)
                    if not (isinstance(n, int) and n < 4):
                        dve.wait_ge(y_out[p % 2], (n - 2 - p % 2) * 8)
                    nc.vector.tensor_copy(y_sb[:, p % 2, :], psY[:, 0:D]).then_inc(y_kept, 1)

            each(dve, slot)


def layer0_combine(nc, g, d):
    with ExitStack() as ctx:
        ph = Phase(nc, ctx, "m0")
        psN = ph.ps("psN", [P, 2, 512])
        RB = 4
        back = ph.sb("back", [P, RB, 2, D])
        fetched = [ph.sem(f"fetched{i}") for i in range(RB)]
        added = ph.sem("added")
        seen = ph.sem("seen")
        ln = LayerNorm(ph, g, "ln")
        block = ctx.enter_context(nc.Block())

        @block.gpsimd
        def _(pool):
            for b in range(B + 1):
                for t in range(b * BT, min(b * BT + BT, NT)):
                    if t >= RB:
                        pool.wait_ge(added, 2 * (t - RB) + 2)
                    for k in range(2):
                        nc.gpsimd.indirect_dma_start(out=back[:, t % RB, k, :], out_offset=None, in_=g.sorted_out,
                                                     in_offset=bass.IndirectOffsetOnAxis(ap=g.slot[:, k, t:t + 1], axis=0)).then_inc(fetched[t % RB], 16)
                if b:
                    ln.rstd(pool, b - 1, (b - 1) % 2)

        @block.vector
        def _(dve):
            for b in range(B + 1):
                for t in range(b * BT, min(b * BT + BT, NT)):
                    dve.wait_ge(fetched[t % RB], 32 * (t // RB + 1))
                    for k in range(2):
                        if k:
                            dve.wait_ge(added, 2 * t + 1)
                        nc.vector.scalar_tensor_tensor(out=g.x[:, t, :], in0=back[:, t % RB, k, :], scalar=g.weight[:, k, t:t + 1],
                                                       in1=g.x[:, t, :], op0=ALU.mult, op1=ALU.add).then_inc(added, 1)
                if b < B:
                    dve.wait_ge(added, 2 * BT * (b + 1))
                    ln.stats(dve, b, b % 2)
                    ln.stats_landed(dve, b)
                    ln.aggregate(dve, b, b % 2)
                if b:
                    ln.apply(dve, b - 1, (b - 1) % 2, 2)

        @block.tensor
        def _(pe):
            ln.all_turns(pe, psN)

        @block.scalar
        def _(act):
            ln.all_keeps(act, psN)


def layer1_attention(nc, g, d):
    G4 = H // 4
    DH1 = D // H
    SCALAR_TURNS = (6,)
    VW = 32
    SCALE = float(np.float32(DH1) ** np.float32(-0.5))
    with ExitStack() as ctx:
        ph = Phase(nc, ctx, "a1")
        psA = ph.ps("psA", [P, 512])
        psS = ph.ps("psS", [P, 4, 512])
        psT = ph.ps("psT", [P, 512])
        psO = ph.ps("psO", [P, 512])
        psM = ph.ps("psM", [P, 512])
        cur = ph.sb("cur", [P, S])
        sel = ph.sb("sel", [P, 4, G4, P], F32R)
        sel_in = ph.sb("sel_in", [P, 4, G4, P])
        qk = ph.sb("qk", [P, 2, S])
        qk_hi = ph.sb("qk_hi", [P, 2, S], F32R)
        qk_lo = ph.sb("qk_lo", [P, 2, S], F32R)
        q4 = ph.sb("q4", [P, 2, S], F32R)
        k4 = ph.sb("k4", [P, 2, 4, S], F32R)
        prob = ph.sb("prob", [P, 8, BT * S])
        probT = ph.sb("probT", [P, 8, BT * S])
        low = ph.sb("low", [P, 2, 4])
        v_aug = ph.sb("v_aug", [P, BT, H, VW])
        oT = ph.sb("oT", [P, S])
        inv = ph.sb("inv", [P, BT, 4])
        o_rows = ph.sb("o_rows", [P, BT, D])
        o_cols = ph.sb("o_cols", [P, S])
        resid = ph.sb("resid", [P, BT, D])
        sem = {name: ph.sem(name) for name in (
            "sel_loaded", "sel_ready", "v_zero", "v_one", "cur_ready", "proj_done", "qk_ready", "hi_done", "lo_done",
            "spread_done", "k4_kept", "q4_kept", "s_done", "low_done", "exp_done", "t_done", "t0_kept", "t1_kept",
            "v_done", "v_kept", "pv_done", "o_kept", "ot_done", "inv_done", "o_norm", "oc_done", "oc_kept", "y_done",
            "y_used", "x_done")}
        (sel_loaded, sel_ready, v_zero, v_one, cur_ready, proj_done, qk_ready, hi_done, lo_done, spread_done, k4_kept,
         q4_kept, s_done, low_done, exp_done, t_done, t0_kept, t1_kept, v_done, v_kept, pv_done, o_kept, ot_done,
         inv_done, o_norm, oc_done, oc_kept, y_done, y_used, x_done) = sem.values()
        bq_scaled = ph.sb("bq_scaled", [P, 1])
        bq_ready = ph.sem("bq_ready")
        pool_seen = ph.sem("pool_seen")
        ln = LayerNorm(ph, g, "ln")
        block = ctx.enter_context(nc.Block())

        def all_rounds(eng, first, slots):
            first()
            slots(0, True, True, lambda p, lag: p >= lag)
            with eng.Fori(1, B - 1) as b:
                slots(b, True, True, lambda p, lag: True)
            slots(B - 1, True, False, lambda p, lag: True)
            slots(B, False, False, lambda p, lag: p < lag)

        @block.sync
        def _(sp):
            sp.dma_start(sel_in[:], d["sel"]).then_inc(sel_loaded, 16)

        @block.tensor
        def _(pe):
            ln.start_turned(pe)
            def project(b):
                pe.wait_ge(cur_ready, b + 1)
                for k in range(2):
                    mm = pe.matmul(psA[:, k * S:(k + 1) * S], g.wqkv1[:, k, :], cur[:], start=True, stop=True)
                mm.then_inc(proj_done, 1)

            def spread_parts(b, G):
                pe.wait_ge(lo_done, b + 1)
                for k in range(2):
                    for j, part in enumerate((qk_hi, qk_lo)):
                        mm = pe.matmul(psA[:, k * S:(k + 1) * S], sel[:, 2 * k + j, G, :], part[:, k, :], start=(j == 0), stop=(j == 1))
                mm.then_inc(spread_done, 1)

            def scores(b, p, k, has_unit):
                G = p // 2
                if k == 0:
                    pe.wait_ge(q4_kept, b * G4 + G + 1)
                if has_unit(p, 2):
                    pe.wait_ge(exp_done, b * 32 + 4 * p - 6 + 2 * k)
                for i in range(BT):
                    at = psS[:, 2 * (p % 2) + k, i * S:(i + 1) * S]
                    pe.matmul(at, q4[:, G % 2, i * P:(i + 1) * P], k4[:, G % 2, (2 * p + k) % 4, :], start=True, stop=False)
                    mm = pe.matmul(at, g.slopes[:, 2 * p + k, :], g.distance[:, i, :], start=False, stop=True)
                mm.then_inc(s_done, 1)

            def turn(b, p, k):
                pe.wait_ge(exp_done, b * 32 + 4 * p - 6 + 2 * k)
                if k == 0:
                    pe.wait_ge(t1_kept, b * PAIRS + p - 2)
                else:
                    pe.wait_ge(t0_kept, b * PAIRS + p - 1)
                u = 2 * ((p - 2) % 4) + k
                for j in range(BT):
                    for i in range(BT):
                        mm = pe.transpose(psT[:, j * S + i * P:j * S + (i + 1) * P], prob[:, u, i * S + j * P:i * S + (j + 1) * P], g.ident[:])
                mm.then_inc(t_done, 1)

            def values(b, p):
                gamma = b * G4 + (p - 4) // 2
                pe.wait_ge(t0_kept, gamma * 2 + 2)
                pe.wait_ge(t1_kept, gamma * 2 + 2)
                pe.wait_ge(v_kept, b + 1 if p >= 4 else b)
                pe.wait_ge(o_kept, gamma)
                for j in range(BT):
                    for hh in range(4):
                        h = 4 * (((p - 4) // 2) % G4) + hh
                        mm = pe.matmul(psO[hh * VW:(hh + 1) * VW, 0:S], v_aug[:, j, h, :], probT[:, h % 8, j * S:(j + 1) * S],
                                       start=(j == 0), stop=(j == BT - 1))
                mm.then_inc(pv_done, 1)

            def values_to_rows(gamma):
                pe.wait_ge(o_kept, gamma + 1)
                for i in range(BT):
                    mm = pe.transpose(psM[:, i * P:(i + 1) * P], oT[:, i * P:(i + 1) * P], g.ident[:])
                mm.then_inc(ot_done, 1)

            def first():
                project(0)
                spread_parts(0, 0)

            def slots(b, new, prep, has_unit):
                for p in range(PAIRS):
                    old = has_unit(p, 8)
                    if new:
                        scores(b, p, 0, has_unit)
                    if has_unit(p, 2):
                        turn(b, p, 0)
                    if new:
                        scores(b, p, 1, has_unit)
                    if p == 3 and old:
                        pe.wait_ge(o_norm, b * G4 - 1)
                        values_to_rows(b * G4 - 1)
                    if p == 7 and old:
                        if new:
                            pe.wait_ge(o_norm, b * G4 + 1)
                        else:
                            pe.wait_ge(y_used, b)
                        ln.turn(pe, b - 1, psM)
                    if new and p in (0, 2, 4):
                        pe.wait_ge(v_kept, b + 1) if p == 4 else pe.wait_ge(q4_kept, b * G4 + p // 2 + 1)
                        spread_parts(b, p // 2 + 1)
                    if prep and p == 5:
                        pe.wait_ge(q4_kept, b * G4 + 4)
                        project(b + 1)
                    if has_unit(p, 2):
                        turn(b, p, 1)
                    if p == 1 and old:
                        pe.wait_ge(o_norm, b * G4 - 2)
                        values_to_rows(b * G4 - 2)
                    if p == 4 and old:
                        pe.wait_ge(oc_kept, b)
                        for i in range(BT):
                            mm = pe.matmul(psM[:, i * P:(i + 1) * P], o_cols[:, i * P:(i + 1) * P], g.wo1[:], start=True, stop=True)
                        mm.then_inc(y_done, 1)
                    if p == 5 and new:
                        if old:
                            pe.wait_ge(y_used, b)
                        values_to_rows(b * G4)
                    if p % 2 == 0 and has_unit(p, 4):
                        values(b, p)
                    if new and p == 3:
                        pe.wait_ge(q4_kept, b * G4 + 3)
                        for j in range(BT):
                            mm = pe.matmul(psA[:, j * P:(j + 1) * P], cur[:, j * P:(j + 1) * P], g.wqkv1[:, 2, :], start=True, stop=True)
                        mm.then_inc(v_done, 1)
                    if p == 3 and old:
                        pe.wait_ge(o_norm, b * G4)
                        for i in range(BT):
                            mm = pe.transpose(psM[:, i * P:(i + 1) * P], o_rows[:, i, :], g.ident[:])
                        mm.then_inc(oc_done, 1)
                    if p == 7 and new:
                        if old:
                            ln.wait_kept(pe, b)
                        else:
                            pe.wait_ge(o_norm, 1)
                        values_to_rows(b * G4 + 1)
                    if prep and p == 6:
                        spread_parts(b + 1, 0)

            pe.wait_ge(sel_ready, 1)
            all_rounds(pe, first, slots)

        @block.scalar
        def _(act):
            ln.start_kept(act)
            def copy_cur(b):
                nc.scalar.copy(cur[:], g.xnT[:, bass.ds(b * S, S)]).then_inc(cur_ready, 1)

            def keep_qk(b):
                act.wait_ge(proj_done, b + 1)
                nc.scalar.activation(qk[:, 0, :], psA[:, 0:S], ACT.Identity, bias=bq_scaled[:], scale=-SCALE).then_inc(qk_ready, 1)
                nc.scalar.activation(qk[:, 1, :], psA[:, S:2 * S], ACT.Identity, bias=g.bqk1[:, 1:2]).then_inc(qk_ready, 1)

            def keep_q4(b, G):
                act.wait_ge(k4_kept, b * G4 + G + 1)
                nc.scalar.copy(q4[:, G % 2, :], psA[:, 0:S]).then_inc(q4_kept, 1)

            def keep_t(b, p, k):
                if not (isinstance(b, int) and b == 0 and p < 6):
                    act.wait_ge(pv_done, b * G4 + (p - 4) // 2)
                act.wait_ge(t_done, b * H + 2 * p - 3 + k)
                nc.scalar.copy(probT[:, (2 * (p - 2) + k) % 8, :], psT[:]).then_inc(t1_kept if k else t0_kept, 1)

            def exps(b, p, has_unit):
                if has_unit(p, 4):
                    act.wait_ge(t_done, b * H + 2 * p - 6)
                for k in range(2):
                    act.wait_ge(low_done, b * H + 2 * p + k + 1)
                    for i in range(BT):
                        u = 2 * (p % 2) + k
                        nc.scalar.activation(prob[:, 2 * (p % 4) + k, i * S:(i + 1) * S], psS[:, u, i * S:(i + 1) * S], ACT.Exp,
                                             bias=low[:, p % 2, BT * k + i:BT * k + i + 1], scale=-1.0).then_inc(exp_done, 1)

            def first():
                act.wait_ge(sel_loaded, 16)
                nc.scalar.copy(sel[:], sel_in[:]).then_inc(sel_ready, 1)
                copy_cur(0)
                act.wait_ge(bq_ready, 1)
                keep_qk(0)
                keep_q4(0, 0)

            def slots(b, new, prep, has_unit):
                for p in range(PAIRS):
                    old = has_unit(p, 8)
                    if has_unit(p, 2):
                        keep_t(b, p, 0)
                    if prep and p == 5:
                        keep_qk(b + 1)
                    if p == 7 and old:
                        ln.keep(act, b - 1, psM[:, 0:S])
                    if p in SCALAR_TURNS and has_unit(p, 2):
                        keep_t(b, p, 1)
                    if new:
                        exps(b, p, has_unit)
                    if new and p in (0, 2, 4):
                        keep_q4(b, p // 2 + 1)
                    if p % 2 == 0 and has_unit(p, 4):
                        gamma = b * G4 + (p - 4) // 2
                        if not (isinstance(b, int) and b == 0 and p == 4):
                            act.wait_ge(ot_done, gamma)
                        act.wait_ge(pv_done, gamma + 1)
                        nc.scalar.copy(oT[:], psO[:, 0:S]).then_inc(o_kept, 1)
                    if prep and p == 4:
                        act.wait_ge(v_done, b + 1)
                        copy_cur(b + 1)
                    if p == 3 and old:
                        act.wait_ge(oc_done, b)
                        nc.scalar.copy(o_cols[:], psM[:, 0:S]).then_inc(oc_kept, 1)
                    if prep and p == 7:
                        keep_q4(b + 1, 0)

            all_rounds(act, first, slots)

        @block.vector
        def _(dve):
            v = nc.vector

            def split(b):
                dve.wait_ge(qk_ready, b * 2 + 2)
                v.tensor_copy(qk_hi[:], qk[:]).then_inc(hi_done, 1)
                dve.wait_ge(hi_done, b + 1)
                v.tensor_tensor(qk_lo[:], qk[:], qk_hi[:].bitcast(F32), ALU.subtract).then_inc(lo_done, 1)

            def keep_k4(b, G):
                dve.wait_ge(spread_done, b * G4 + G + 1)
                if not (isinstance(b, int) and b == 0 and G < 2):
                    dve.wait_ge(s_done, b * H + 4 * G - 4)
                v.tensor_tensor(k4[:, G % 2, :, :], psA[:, S:2 * S].unsqueeze(1).to_broadcast([P, 4, S]),
                                g.head_mask[:].unsqueeze(2).to_broadcast([P, 4, S]), ALU.mult).then_inc(k4_kept, 1)

            def lows(b, p, has_unit):
                if has_unit(p, 2):
                    dve.wait_ge(exp_done, b * 32 + 4 * p - 4)
                for k in range(2):
                    dve.wait_ge(s_done, b * H + 2 * p + k + 1)
                    v.tensor_reduce(low[:, p % 2, BT * k:BT * k + BT], psS[:, 2 * (p % 2) + k, :].rearrange("p (i j) -> p i j", i=BT),
                                    AX.X, ALU.min).then_inc(low_done, 1)

            def keep_t(b, p):
                dve.wait_ge(t_done, b * H + 2 * p - 2)
                if not (isinstance(b, int) and b == 0 and p < 6):
                    dve.wait_ge(pv_done, b * G4 + (p - 4) // 2)
                v.tensor_copy(probT[:, (2 * (p - 2) + 1) % 8, :], psT[:]).then_inc(t1_kept, 1)

            def divide(gamma, G):
                dve.wait_ge(ot_done, gamma + 1)
                rows = psM[:, 0:S].rearrange("p (i h c) -> p i h c", i=BT, c=VW)
                v.reciprocal(inv[:], rows[:, :, :, DH1]).then_inc(inv_done, 1)
                dve.wait_ge(inv_done, gamma + 1)
                for i in range(BT):
                    x = v.tensor_tensor(o_rows[:, i, 4 * G * DH1:4 * (G + 1) * DH1].rearrange("p (h c) -> p h c", h=4),
                                        rows[:, i, :, 0:DH1], inv[:, i, :].unsqueeze(2).to_broadcast([P, 4, DH1]), ALU.mult)
                x.then_inc(o_norm, 1)

            def first():
                v.memset(v_aug[:], 0.0).then_inc(v_zero, 1)
                dve.wait_ge(v_zero, 1)
                v.memset(v_aug[:, :, :, DH1:DH1 + 1], 1.0).then_inc(v_one, 1)
                dve.wait_ge(v_one, 1)
                v.tensor_scalar(bq_scaled[:], g.bqk1[:, 0:1], -SCALE, None, ALU.mult).then_inc(bq_ready, 1)
                split(0)
                keep_k4(0, 0)

            def slots(b, new, prep, has_unit):
                for p in range(PAIRS):
                    old = has_unit(p, 8)
                    if new:
                        lows(b, p, has_unit)
                    if p == 5 and old:
                        dve.wait_ge(x_done, b)
                        dve.sem_inc(seen, 1)
                        ln.stats(dve, b - 1)
                        ln.stats_landed(dve, b - 1)
                        dve.sem_inc(seen, 1)
                        ln.aggregate(dve, b - 1)
                    if p == 3 and old:
                        divide(b * G4 - 1, 3)
                    if new and p in (0, 2, 4):
                        keep_k4(b, p // 2 + 1)
                    if prep and p == 6:
                        split(b + 1)
                    if p == 6 and old:
                        ln.apply(dve, b - 1)
                    if prep and p == 7:
                        keep_k4(b + 1, 0)
                    if has_unit(p, 2) and p not in SCALAR_TURNS:
                        keep_t(b, p)
                    if p == 0 and old:
                        divide(b * G4 - 3, 1)
                    if p == 1 and old:
                        divide(b * G4 - 2, 2)
                    if p == 4 and old:
                        dve.wait_ge(y_done, b)
                        v.tensor_tensor(resid[:], psM[:, 0:S].rearrange("p (t d) -> p t d", t=BT),
                                        g.x[:, bass.ds((b - 1) * BT, BT), :], ALU.add).then_inc(y_used, 1)
                    if p == 5 and new:
                        if old:
                            dve.wait_ge(oc_done, b)
                        divide(b * G4, 0)
                    if p == 3 and new:
                        dve.wait_ge(v_done, b + 1)
                        v.tensor_tensor(v_aug[:, :, :, 0:DH1], psA[:, 0:S].rearrange("p (j h c) -> p j h c", j=BT, h=H),
                                        g.bv1[:], ALU.add).then_inc(v_kept, 1)

            seen = ph.sem("seen")
            all_rounds(dve, first, slots)

        @block.gpsimd
        def _(pool):
            with pool.Fori(0, B) as b:
                pool.wait_ge(y_used, b + 1)
                pool.sem_inc(pool_seen, 1)
                nc.gpsimd.tensor_tensor(g.x[:, bass.ds(b * BT, BT), :], resid[:], g.bo1[:], ALU.add).then_inc(x_done, 1)
                ln.rstd(pool, b)


def layer1_context(nc, g, d):
    DH1 = D // H
    VW = 32
    SCALE = float(np.float32(DH1) ** np.float32(-0.5))
    with ExitStack() as ctx:
        ph = Phase(nc, ctx, "c1")
        psS = ph.ps("psS", [P, BT, H, L])
        psT = ph.ps("psT", [P, PAIRS, P])
        psO = ph.ps("psO", [P, 2, S])
        psM = ph.ps("psM", [P, 512])
        cur = ph.sb("cur", [P, 2, S])
        ctx2 = ph.sb("ctx2", [P, 2, 2, L])
        kT = ph.sb("kT", [P, B * L])
        q_sb = ph.sb("q", [P, 2, S])
        k_bd = ph.sb("k_bd", [P, 2, H, L])
        v_bd = ph.sb("v_bd", [P, 2, PAIRS, VW])
        low = ph.sb("low", [P, BT, H])
        above = ph.sb("above", [P, BT, H, L])
        prob = ph.sb("prob", [P, BT, H * L])
        probT = ph.sb("probT", [P, PAIRS, BT, P])
        oT = ph.sb("oT", [P, 2, S])
        inv = ph.sb("inv", [P, 2 * BT, 4, 2])
        o_rows = ph.sb("o_rows", [P, BT, D])
        o_cols = ph.sb("o_cols", [P, S])
        resid = ph.sb("resid", [P, BT, D])
        (k_done, kT_ready, v_zero, v_set, cur_ready, ctx_ready, q_done, v_done, q_kept, v_kept, k_bd_ready, s_done, low_done,
         above_done, exp_done, t_done, t_kept, pv_done, o_kept, ot_done, inv_done, o_norm, oc_done, oc_kept, y_done, y_used,
         x_done, seen, pool_seen) = (ph.sem(name) for name in (
            "k_done kT_ready v_zero v_set cur_ready ctx_ready q_done v_done q_kept v_kept k_bd_ready s_done low_done "
            "above_done exp_done t_done t_kept pv_done o_kept ot_done inv_done o_norm oc_done oc_kept y_done y_used "
            "x_done seen pool_seen").split())
        ln = LayerNorm(ph, g, "ln")
        block = ctx.enter_context(nc.Block())
        ROUNDS = B // 2

        @block.tensor
        def _(pe):
            ln.start_turned(pe)
            pe.sem_inc(oc_done, START)
            for c in range(2):
                mm = pe.matmul(psS[:, 0, c * 8:(c + 1) * 8, :], g.wk2[:], g.ctxT[:, c * 512:(c + 1) * 512], start=True, stop=True)
            mm.then_inc(k_done, 1)
            pe.wait_ge(kT_ready, 1)

            def turn_probs(n, i, p):
                pe.wait_ge(exp_done, n * BT - BT + i + 1)
                if i == 1:
                    pe.wait_ge(t_kept, n * BT - 1)
                for q in range(PAIRS):
                    mm = pe.transpose(psT[:, q, :], prob[:, i, q * P:(q + 1) * P], g.ident[:])
                mm.then_inc(t_done, 1)

            def slots(r, new, has_unit):
                for p in range(2):
                    n = r * 2 + p
                    if has_unit(p, 2):
                        pe.wait_ge(o_kept, n - 1)
                        for j in range(2 * BT):
                            mm = pe.transpose(psT[:, j, :], oT[:, j // BT, (j % BT) * P:(j % BT + 1) * P], g.ident[:])
                        mm.then_inc(ot_done, 1)
                    if new:
                        pe.wait_ge(cur_ready, n + 1)
                        pe.wait_ge(ctx_ready, n + 1)
                        if has_unit(p, 3):
                            ln.wait_kept(pe, n - 2)
                        pe.matmul(psM[:, 0:S], g.wq2[:], cur[:, p, :], start=True, stop=True).then_inc(q_done, 1)
                        pe.matmul(psM[:, S:S + D], ctx2[:, p, :, :], g.wv2[:], start=True, stop=True).then_inc(v_done, 1)
                    if has_unit(p, 2):
                        pe.wait_ge(o_norm, n - 1)
                        if new:
                            pe.wait_ge(v_kept, n + 1)
                            pe.wait_ge(q_kept, n + 1)
                        else:
                            ln.wait_kept(pe, n - 2)
                        for i in range(BT):
                            mm = pe.transpose(psM[:, i * P:(i + 1) * P], o_rows[:, i, :], g.ident[:])
                        mm.then_inc(oc_done, 1)
                    if has_unit(p, 1):
                        if has_unit(p, 2):
                            pe.wait_ge(o_norm, n - 1)
                        turn_probs(n, 0, p)
                    if has_unit(p, 2):
                        pe.wait_ge(oc_kept, n - 1)
                        for i in range(BT):
                            mm = pe.matmul(psM[:, i * P:(i + 1) * P], o_cols[:, i * P:(i + 1) * P], g.wo2[:], start=True, stop=True)
                        mm.then_inc(y_done, 1)
                    if new:
                        pe.wait_ge(q_kept, n + 1)
                        pe.wait_ge(k_bd_ready, n + 1)
                        for i in range(BT):
                            if has_unit(p, 1):
                                pe.wait_ge(above_done, n * BT - BT + i + 1)
                            for c in range(2):
                                mm = pe.matmul(psS[:, i, c * 8:(c + 1) * 8, :], q_sb[:, p, i * P:(i + 1) * P], k_bd[:, p, c * 8:(c + 1) * 8, :],
                                               start=True, stop=True)
                            mm.then_inc(s_done, 1)
                    if has_unit(p, 1):
                        turn_probs(n, 1, p)
                        pe.wait_ge(t_kept, n * BT)
                        pe.wait_ge(v_kept, n)
                        if has_unit(p, 2):
                            pe.wait_ge(o_kept, n - 1)
                        for q in range(2):
                            for c in range(4):
                                mm = pe.matmul(psO[c * VW:(c + 1) * VW, q, :], v_bd[:, 1 - p, 4 * q + c, :], probT[:, 4 * q + c, :, :],
                                               start=True, stop=True)
                        mm.then_inc(pv_done, 1)
                    if has_unit(p, 2):
                        pe.wait_ge(y_used, n - 1)
                        ln.turn(pe, n - 2, psM)

            rounds(pe, slots, ROUNDS)

        @block.scalar
        def _(act):
            ln.start_kept(act)
            act.wait_ge(k_done, 1)
            nc.scalar.copy(kT[:], psS[:, 0, :, :].rearrange("p h l -> p (h l)")).then_inc(kT_ready, 1)

            def exps(n, i):
                act.wait_ge(above_done, n * BT + i + 1)
                if not (isinstance(n, int) and n == 0):
                    act.wait_ge(t_done, n * BT - BT + i + 1)
                nc.scalar.activation(prob[:, i, :], above[:, i, :, :].rearrange("p h l -> p (h l)"), ACT.Exp, scale=-1.0).then_inc(exp_done, 1)

            def keep_t(n, i):
                act.wait_ge(t_done, n * BT - BT + i + 1)
                if not (isinstance(n, int) and n == 1):
                    act.wait_ge(pv_done, n - 1)
                nc.scalar.copy(probT[:, :, i, :], psT[:]).then_inc(t_kept, 1)

            def slots(r, new, has_unit):
                for p in range(2):
                    n = r * 2 + p
                    if new:
                        if has_unit(p, 2):
                            act.wait_ge(q_done, n - 1)
                        nc.scalar.copy(cur[:, p, :], g.xnT[:, bass.ds(n * S, S)]).then_inc(cur_ready, 1)
                        act.wait_ge(v_done, n + 1)
                        if has_unit(p, 2):
                            act.wait_ge(s_done, n * BT - BT)
                        nc.scalar.activation(q_sb[:, p, :], psM[:, 0:S], ACT.Copy, scale=-SCALE).then_inc(q_kept, 1)
                    if has_unit(p, 2):
                        act.wait_ge(oc_done, START + n - 1)
                        nc.scalar.copy(o_cols[:], psM[:, 0:S]).then_inc(oc_kept, 1)
                    if has_unit(p, 1):
                        keep_t(n, 0)
                    if new:
                        exps(n, 0)
                    if has_unit(p, 1):
                        keep_t(n, 1)
                    if new:
                        exps(n, 1)
                    if has_unit(p, 1):
                        act.wait_ge(pv_done, n)
                        if has_unit(p, 2):
                            act.wait_ge(ot_done, n - 1)
                        nc.scalar.copy(oT[:], psO[:]).then_inc(o_kept, 1)
                    if has_unit(p, 2):
                        ln.keep(act, n - 2, psM[:, 0:S])

            rounds(act, slots, ROUNDS)

        @block.gpsimd
        def _(pool):
            pool.wait_ge(kT_ready, 1)

            def slots(r, new, has_unit):
                for p in range(2):
                    n = r * 2 + p
                    if new:
                        if has_unit(p, 2):
                            pool.wait_ge(s_done, n * BT - BT)
                            pool.sem_inc(pool_seen, 1)
                        nc.gpsimd.tensor_tensor(k_bd[:, p, :, :], kT[:, bass.ds(n * L, L)].unsqueeze(1).to_broadcast([P, H, L]),
                                                g.head_mask16[:].unsqueeze(2).to_broadcast([P, H, L]), ALU.mult).then_inc(k_bd_ready, 1)
                    if has_unit(p, 2):
                        ln.rstd(pool, n - 2)

            rounds(pool, slots, ROUNDS)

        @block.vector
        def _(dve):
            v = nc.vector
            v.memset(v_bd[:], 0.0).then_inc(v_zero, 1)
            dve.wait_ge(v_zero, 1)
            v.memset(v_bd[0:L, :, :, 2 * DH1:2 * DH1 + 1], 1.0).then_inc(v_set, 1)
            v.memset(v_bd[L:P, :, :, 2 * DH1 + 1:2 * DH1 + 2], 1.0).then_inc(v_set, 1)
            dve.wait_ge(v_set, 2)

            def slots(r, new, has_unit):
                for p in range(2):
                    n = r * 2 + p
                    if new:
                        if has_unit(p, 2):
                            dve.wait_ge(v_done, n - 1)
                            dve.sem_inc(seen, 1)
                        for j in range(2):
                            i = v.tensor_copy(ctx2[:, p, j, :], g.ctxT[:, bass.ds(n * L, L)])
                        i.then_inc(ctx_ready, 1)
                    if has_unit(p, 2):
                        dve.wait_ge(ot_done, n - 1)
                        rows = psT[:, 0:2 * BT, :].rearrange("p j (c w) -> p j c w", w=VW)
                        v.reciprocal(inv[:], rows[:, :, :, 2 * DH1:2 * DH1 + 2]).then_inc(inv_done, 1)
                        dve.wait_ge(inv_done, n - 1)
                        if has_unit(p, 3):
                            dve.wait_ge(oc_done, START + n - 2)
                        for j in range(2 * BT):
                            q, i = j // BT, j % BT
                            x = v.tensor_tensor(o_rows[:, i, q * 64:(q + 1) * 64].rearrange("p (c h w) -> p c h w", c=4, h=2),
                                                rows[:, j, :, 0:2 * DH1].rearrange("p c (h w) -> p c h w", h=2),
                                                inv[:, j, :, :].unsqueeze(3).to_broadcast([P, 4, 2, DH1]), ALU.mult)
                        x.then_inc(o_norm, 1)
                    if new:
                        dve.wait_ge(v_done, n + 1)
                        dve.wait_ge(q_kept, n + 1)
                        if has_unit(p, 2):
                            dve.wait_ge(pv_done, n - 1)
                        for k in range(2):
                            half = slice(k * L, (k + 1) * L)
                            x = v.tensor_copy(v_bd[half, p, :, k * DH1:(k + 1) * DH1],
                                              psM[half, S:S + D].rearrange("p (q h w) -> p q h w", h=2, w=DH1)[:, :, k, :])
                        x.then_inc(v_kept, 1)
                    if has_unit(p, 2):
                        dve.wait_ge(y_done, n - 1)
                        rows = bass.ds((n - 2) * BT, BT)
                        v.tensor_tensor(resid[:], psM[:, 0:S].rearrange("p (t d) -> p t d", t=BT), g.x[:, rows, :], ALU.add).then_inc(y_used, 1)
                        dve.wait_ge(y_used, n - 1)
                        v.tensor_tensor(g.x[:, rows, :], resid[:], g.bo2[:], ALU.add).then_inc(x_done, 1)
                        dve.wait_ge(x_done, n - 1)
                        dve.sem_inc(seen, 1)
                        ln.stats(dve, n - 2)
                        ln.stats_landed(dve, n - 2)
                        if not new:
                            dve.sem_inc(seen, 1)
                    if new:
                        for i in range(BT):
                            dve.wait_ge(s_done, n * BT + i + 1)
                            if i == 0 and has_unit(p, 1):
                                dve.wait_ge(exp_done, n * BT)
                            v.tensor_reduce(low[:, i, :], psS[:, i, :, :], AX.X, ALU.min).then_inc(low_done, 1)
                            dve.wait_ge(low_done, n * BT + i + 1)
                            v.tensor_tensor(above[:, i, :, :], psS[:, i, :, :], low[:, i, :].unsqueeze(2).to_broadcast([P, H, L]),
                                            ALU.subtract).then_inc(above_done, 1)
                            if i == 0 and has_unit(p, 2):
                                ln.aggregate(dve, n - 2)
                    elif has_unit(p, 2):
                        ln.aggregate(dve, n - 2)
                    if has_unit(p, 2):
                        ln.apply(dve, n - 2)

            rounds(dve, slots, ROUNDS)


def layer1_route_and_shared(nc, g, d):
    with ExitStack() as ctx:
        ph = Phase(nc, ctx, "r1")
        psL = ph.ps("psL", [P, NT, E])
        parts = ph.sb("parts", [P, 2, NT, E])
        logits_done = ph.sem("logits_done")
        route = Routing(ph, g, "rt")
        shared = SharedExpert(ph, g, "sh", g.shared_in1, g.shared_out1[:], False)
        block = ctx.enter_context(nc.Block())

        @block.tensor
        def _(pe):
            for t in range(NT):
                mm = pe.matmul(psL[:, t, :], g.xnT[:, t * P:(t + 1) * P], g.router1[:], start=True, stop=True)
            mm.then_inc(logits_done, 1)
            rounds(pe, shared.slots(lambda *a: shared.tensor(pe, *a)), T // 1024)

        @block.scalar
        def _(act):
            route.exponent(act)
            rounds(act, shared.slots(lambda *a: shared.scalar(act, *a)), T // 1024)

        @block.vector
        def _(dve):
            v = nc.vector
            dve.wait_ge(logits_done, 1)
            route.choose(dve, psL[:], g.top, g.weight)
            for k in range(2):
                x = v.tensor_tensor(parts[:, k, :, :], g.top[:, k, :, :],
                                    g.weight[:, k, :].unsqueeze(2).to_broadcast([P, NT, E]), ALU.mult)
            route.then(dve, x)
            route.then(dve, v.tensor_tensor(g.share[:], parts[:, 0, :, :], parts[:, 1, :, :], ALU.add))
            rounds(dve, shared.slots(lambda *a: shared.vector(dve, *a)), T // 1024)


def layer1_experts(nc, g, d, out):
    FC = 4
    I1 = 512 // E
    with ExitStack() as ctx:
        ph = Phase(nc, ctx, "e1")
        psG = ph.ps("psG", [P, 2, 512])
        psU = ph.ps("psU", [P, 2, 512])
        psH = ph.ps("psH", [P, 512])
        psY = ph.ps("psY", [P, 512])
        cols = ph.sb("cols", [P, 2, P])
        act_sb = ph.sb("act", [P, 2, 512])
        wide = ph.sb("wide", [P, 2, 512])
        hid = ph.sb("hid", [P, 2, 512])
        hidT = ph.sb("hidT", [P, 512])
        (cols_ready, gate_in, in_done, silu_done, wide_done, hid_done, h_turned, h_kept, y_done, x_done, stored) = (
            ph.sem(name) for name in "cols_ready gate_in in_done silu_done wide_done hid_done h_turned h_kept y_done x_done stored".split())
        block = ctx.enter_context(nc.Block())

        def each(eng, slot):
            def body(r, new, has_unit):
                for p in range(4):
                    slot(r * 4 + p, p, new, has_unit(p, 2))
            rounds(eng, body, NT // 4)

        @block.tensor
        def _(pe):
            def slot(n, p, new, lagging):
                if lagging:
                    pe.wait_ge(hid_done, n - 1)
                    pe.wait_ge(h_kept, n - 2)
                    for c in range(FC):
                        mm = pe.transpose(psH[:, c * P:(c + 1) * P], hid[:, p % 2, c * P:(c + 1) * P], g.ident[:])
                    mm.then_inc(h_turned, 1)
                if new:
                    pe.wait_ge(cols_ready, n + 1)
                    if lagging:
                        pe.wait_ge(wide_done, n - 1)
                    pe.matmul(psG[:, p % 2, :], cols[:, p % 2, :], g.gate1[:], start=True, stop=True).then_inc(gate_in, 1)
                    pe.matmul(psU[:, p % 2, :], cols[:, p % 2, :], g.up1[:], start=True, stop=True).then_inc(in_done, 1)
                if lagging:
                    pe.wait_ge(h_kept, n - 1)
                    pe.wait_ge(x_done, n - 2)
                    for c in range(FC):
                        mm = pe.matmul(psY[:, 0:D], hidT[:, c * P:(c + 1) * P], g.down1[:, c, :], start=(c == 0), stop=(c == FC - 1))
                    mm.then_inc(y_done, 1)

            each(pe, slot)

        @block.scalar
        def _(act):
            def slot(n, p, new, lagging):
                if new:
                    if lagging:
                        act.wait_ge(in_done, n - 1)
                    nc.scalar.copy(cols[:, p % 2, :], g.xnT[:, bass.ds(n * P, P)]).then_inc(cols_ready, 1)
                if lagging:
                    act.wait_ge(h_turned, n - 1)
                    act.wait_ge(y_done, n - 2)
                    nc.scalar.copy(hidT[:], psH[:]).then_inc(h_kept, 1)
                if new:
                    act.wait_ge(gate_in, n + 1)
                    if lagging:
                        act.wait_ge(wide_done, n - 1)
                    nc.scalar.activation(act_sb[:, p % 2, :], psG[:, p % 2, :], ACT.Silu).then_inc(silu_done, 1)

            each(act, slot)

        @block.vector
        def _(dve):
            def slot(n, p, new, lagging):
                if new:
                    dve.wait_ge(silu_done, n + 1)
                    dve.wait_ge(in_done, n + 1)
                    if lagging:
                        dve.wait_ge(hid_done, n - 1)
                    nc.vector.tensor_tensor(wide[:, p % 2, :], act_sb[:, p % 2, :], psU[:, p % 2, :], ALU.mult).then_inc(wide_done, 1)
                if lagging:
                    dve.wait_ge(y_done, n - 1)
                    row = bass.ds(n - 2, 1)
                    nc.vector.tensor_tensor(g.x[:, row, :], g.x[:, row, :], psY[:, 0:D], ALU.add).then_inc(x_done, 1)

            each(dve, slot)

        @block.gpsimd
        def _(pool):
            def slot(n, p, new, lagging):
                if new:
                    pool.wait_ge(wide_done, n + 1)
                    if lagging:
                        pool.wait_ge(h_turned, n - 1)
                    pool.sem_inc(seen, 1)
                    nc.gpsimd.tensor_tensor(hid[:, p % 2, :].rearrange("p (e i) -> p e i", e=E),
                                            wide[:, p % 2, :].rearrange("p (e i) -> p e i", e=E),
                                            g.share[:, bass.ds(n, 1), :].rearrange("p t e -> p (t e)").unsqueeze(2).to_broadcast([P, E, I1]),
                                            ALU.mult).then_inc(hid_done, 1)

            seen = ph.sem("seen")
            each(pool, slot)

        @block.sync
        def _(sp):
            dst = out.rearrange("(t p) d -> p t d", p=P)
            with sp.Fori(0, NT // 4) as r:
                sp.wait_ge(x_done, r * 4 + 4)
                sp.dma_start(dst[:, bass.ds(r * 4, 4), :], g.x[:, bass.ds(r * 4, 4), :]).then_inc(stored, 16)
            sp.wait_ge(stored, 16 * (NT // 4))


class Globals:
    pass


def decoder(nc, d, out):
    g = Globals()
    loads = []

    def hold(ctx, name, shape, dt=F32, load=True):
        t = ctx.enter_context(nc.sbuf_tensor(name, shape, dt))
        if load:
            loads.append((t[:], d[name]))
        return t

    with ExitStack() as ctx:
        g.x = hold(ctx, "x", [P, NT, D], load=False)
        g.xnT = hold(ctx, "xnT", [P, T], load=False)
        g.ident = hold(ctx, "ident", [P, P], load=False)
        g.eps = hold(ctx, "eps", [P, BT], load=False)
        g.minus_half = hold(ctx, "minus_half", [P, BT], load=False)
        g.ctx = hold(ctx, "ctx", [P, B * L // P, D], load=False)
        g.ctxT = hold(ctx, "ctxT", [P, B * L], load=False)
        g.countdown = hold(ctx, "countdown", [P, NT, E])
        g.top = hold(ctx, "top", [P, 2, NT, E], load=False)
        g.weight = hold(ctx, "weight", [P, 2, NT], load=False)
        g.wqkv1 = hold(ctx, "wqkv1", [P, 3, D])
        g.bqk1 = hold(ctx, "bqk1", [P, 2])
        g.bv1 = hold(ctx, "bv1", [P, BT, H, D // H])
        g.wo1 = hold(ctx, "wo1", [P, D])
        g.bo1 = hold(ctx, "bo1", [P, BT, D])
        g.head_mask = hold(ctx, "head_mask", [P, 4])
        g.slopes = hold(ctx, "slopes", [P, H, P], BF16)
        g.distance = hold(ctx, "distance", [P, BT, S], BF16)
        g.wq2 = hold(ctx, "wq2", [P, D])
        g.wk2 = hold(ctx, "wk2", [P, D])
        g.wv2 = hold(ctx, "wv2", [P, D])
        g.wo2 = hold(ctx, "wo2", [P, D])
        g.bo2 = hold(ctx, "bo2", [P, BT, D])
        g.head_mask16 = hold(ctx, "head_mask16", [P, H])
        g.router1 = hold(ctx, "router1", [P, E])
        g.shared_in1 = hold(ctx, "shared_in1", [P, 2 * P])
        g.shared_out1 = hold(ctx, "shared_out1", [P, D])
        g.gate1 = hold(ctx, "gate1", [P, 512])
        g.up1 = hold(ctx, "up1", [P, 512])
        g.down1 = hold(ctx, "down1", [P, 4, D])
        g.share = hold(ctx, "share", [P, NT, E], load=False)
        g.sorted_in = nc.dram_tensor("sorted_in", (MOE_BLOCKS * P, D), F32, kind="Internal").ap()
        g.sorted_out = nc.dram_tensor("sorted_out", (MOE_BLOCKS * P, D), F32, kind="Internal").ap()
        with ExitStack() as layer0:
            g.rows = hold(layer0, "rows", [P, NT, D], load=False)
            g.wcat = hold(layer0, "wcat", [P, 2, 2 * D])
            g.bcat = hold(layer0, "bcat", [P, 2 * BT, 2 * D])
            g.gamma = hold(layer0, "gamma", [P, BT, D])
            g.beta = hold(layer0, "beta", [P, BT, D])
            g.router = hold(layer0, "router", [P, E])
            g.block_index = hold(layer0, "block_index", [P, MOE_BLOCKS])
            g.before_mask = hold(layer0, "before_mask", [P, P], BF16)
            g.ones_bf = hold(layer0, "ones_bf", [P, P], BF16)
            g.slot = hold(layer0, "slot", [P, 2, NT], I32, load=False)
            g.expert = hold(layer0, "expert", [P, MOE_BLOCKS], I32, load=False)
            g.shared_in0 = hold(layer0, "shared_in0", [P, 2 * P])
            g.shared_out0 = hold(layer0, "shared_out0", [P, D])
            with ExitStack() as attention0:
                g.G = hold(attention0, "G", [P, H, D], load=False)
                g.wv = hold(attention0, "wv", [P, H * DH0])
                g.wo = hold(attention0, "wo", [P, PAIRS, D])
                g.bias0 = hold(attention0, "bias0", [P, H, CAUSAL])
                g.bo = hold(attention0, "bo", [P, BT, D])
                load_and_prepare(nc, g, d, loads)
                layer0_attention(nc, g, d)
            g.gate_up = hold(layer0, "gate_up", [P, 2 * E, F0], load=False)
            g.down = hold(layer0, "down", [P, E * F0 // P, D], load=False)
            layer0_context(nc, g, d)
            layer0_route(nc, g, d)
            layer0_shared_and_dispatch(nc, g, d)
            layer0_experts(nc, g, d)
            layer0_combine(nc, g, d)
        layer1_attention(nc, g, d)
        layer1_context(nc, g, d)
        layer1_route_and_shared(nc, g, d)
        layer1_experts(nc, g, d, out)


def layout(a):
    c = np.ascontiguousarray
    bf16 = mybir.dt.np(BF16)
    pairs = lambda w: c(w.T.reshape(PAIRS, P, D).transpose(1, 0, 2))
    i = np.arange(S, dtype=np.float32)
    slope = (1.0 / np.power(np.float32((2.0 ** 8) ** (1.0 / H)), np.arange(1, H + 1, dtype=np.float32))).astype(np.float32)
    minus = -(slope[:, None, None] * (i[:, None] - i[None, :])).astype(np.float32)
    minus = np.where(i[:, None] >= i[None, :], minus, np.float32(MASKED))
    bias0 = np.concatenate([minus[:, :P, :P], minus[:, P:, :]], axis=2).transpose(1, 0, 2)
    dh = D // H
    part, head, at = np.meshgrid(np.arange(4), np.arange(4), np.arange(dh), indexing="ij")
    part, head, at = part.ravel(), head.ravel(), at.ravel()
    sel = np.zeros((P, 4, H // 4, P), np.float32)
    for kind, parts in enumerate(((0, 1), (2, 3), (0, 2), (1, 3))):
        for group in range(H // 4):
            for r in range(P):
                if part[r] in parts:
                    sel[(4 * group + head[r]) * dh + at[r], kind, group, r] = 1
    w1 = a["L1_attn_qkv_w"].reshape(H, 3, dh, D)
    b1 = a["L1_attn_qkv_b"].reshape(H, 3, dh)
    tok = np.arange(S).reshape(BT, P)
    return {
        "sel": sel,
        "wq2": c(a["L1_xattn_w_q"].T),
        "wk2": c(a["L1_xattn_w_kv"][:D].T),
        "wv2": c(a["L1_xattn_w_kv"][D:].T),
        "wo2": c(a["L1_xattn_w_out"].T),
        "bo2": c(np.broadcast_to(a["L1_xattn_b_out"], (P, BT, D))),
        "head_mask16": c((np.arange(P)[:, None] // dh == np.arange(H)).astype(np.float32)),
        "router1": c(a["L1_ffn_gate_w"]),
        "shared_in1": c(np.concatenate([a["L1_ffn_sg"], a["L1_ffn_su"]], axis=1)),
        "shared_out1": c(a["L1_ffn_sd"]),
        "gate1": c(a["L1_ffn_wg"].transpose(1, 0, 2).reshape(D, 512)),
        "up1": c(a["L1_ffn_wu"].transpose(1, 0, 2).reshape(D, 512)),
        "down1": c(a["L1_ffn_wd"].reshape(4, P, D).transpose(1, 0, 2)),
        "wqkv1": c(w1.transpose(3, 1, 0, 2).reshape(D, 3, D)),
        "bqk1": c(b1[:, :2].transpose(0, 2, 1).reshape(D, 2)),
        "bv1": c(np.broadcast_to(b1[:, 2], (P, BT, H, dh))),
        "wo1": c(a["L1_attn_out_w"].T),
        "bo1": c(np.broadcast_to(a["L1_attn_out_b"], (P, BT, D))),
        "head_mask": c((head[:, None] == np.arange(4)).astype(np.float32)),
        "slopes": c((np.eye(P)[:, None, :] * (0.5 ** np.arange(H))[None, :, None]).astype(bf16)),
        "distance": c(np.abs(tok.T[:, :, None] - np.arange(S)).astype(bf16)),
        "x": c(a["x"].reshape(T, D)),
        "ctx": c(a["ctx_1024"].reshape(B * L // P, P, D).transpose(1, 0, 2)),
        "ident": np.eye(P, dtype=np.float32),
        "wqT": pairs(a["L0_attn_Wq"]),
        "wkT": pairs(a["L0_attn_Wk"]),
        "wv": c(a["L0_attn_Wv"]),
        "wo": c(a["L0_attn_Wo"].reshape(PAIRS, P, D).transpose(1, 0, 2)),
        "bias0": c(bias0),
        "wcat": c(np.concatenate([a["L0_xattn_W_lin"].reshape(2, D, D), a["L0_xattn_W_gate"].reshape(2, D, D)], axis=2).transpose(1, 0, 2)),
        "bcat": c(np.broadcast_to(np.concatenate([a["L0_xattn_b_lin"], a["L0_xattn_b_gate"]]), (P, 2 * BT, 2 * D))),
        "gamma": c(np.broadcast_to(a["L0_ffn_ln_gamma"], (P, BT, D))),
        "beta": c(np.broadcast_to(a["L0_ffn_ln_beta"], (P, BT, D))),
        "router": c(a["L0_ffn_router_w"]),
        "countdown": c(np.broadcast_to(np.arange(E, 0, -1, dtype=np.float32), (P, NT, E))),
        "block_index": c(np.broadcast_to(np.arange(MOE_BLOCKS, dtype=np.float32), (P, MOE_BLOCKS))),
        "before_mask": np.triu(np.ones((P, P), np.float32), 1).astype(bf16),
        "ones_bf": np.ones((P, P), bf16),
        "gate_up": c(a["L0_ffn_gate_up_w"].reshape(E, D, 2, F0).transpose(1, 0, 2, 3).reshape(D, 2 * E, F0)),
        "down": c(a["L0_ffn_down_w"].reshape(E, F0 // P, P, D).transpose(2, 0, 1, 3).reshape(P, E * F0 // P, D)),
        "shared_in0": c(a["L0_ffn_shared_gate_up_w"]),
        "shared_out0": c(a["L0_ffn_shared_down_w"]),
        "bo": c(np.broadcast_to(a["L0_attn_bo"], (P, BT, D))),
    }


def kernel(**inputs):
    import concourse.bacc as bacc
    from concourse.bass_utils import run_bass_kernel_spmd

    nc = bacc.Bacc("TRN2", target_bir_lowering=False, num_devices=1)
    arrays = {f"in_{k}": v for k, v in layout({k: np.asarray(v) for k, v in inputs.items()}).items()}
    d = {k[3:]: nc.dram_tensor(k, v.shape, mybir.dt.from_np(v.dtype), kind="ExternalInput").ap() for k, v in arrays.items()}
    out = nc.dram_tensor("out", (T, D), F32, kind="ExternalOutput").ap()
    decoder(nc, d, out)
    r = run_bass_kernel_spmd(nc, [arrays], core_ids=[0])
    return np.asarray(r.results[0]["out"]).reshape(B, S, D)
```

```python
from contextlib import ExitStack

import numpy as np
import concourse.bass as bass
from concourse import mybir

F32 = mybir.dt.float32
F32R = mybir.dt.float32r
BF16 = mybir.dt.bfloat16
I32 = mybir.dt.int32
ALU = mybir.AluOpType
ACT = mybir.ActivationFunctionType
AX = mybir.AxisListType

P = 128
B = 16
S = 256
D = 128
L = 64
H = 16
T = B * S
NT = T // P
BT = S // P
DH0 = 64
PAIRS = H // 2
E = 8
F0 = 512
CAUSAL = P + 2 * P
MOE_BLOCKS = -(-(2 * T + E * (P - 1)) // P // 4) * 4
CLIP = 10.0
LN_EPS = 1e-5
MASKED = 1e30
LEAST = 3e38
START = 1


class Phase:

    def __init__(self, nc, ctx, tag):
        self.nc, self.ctx, self.tag = nc, ctx, tag
        self.sems = []
        ctx.callback(self.release)

    def sb(self, name, shape, dt=F32):
        return self.ctx.enter_context(self.nc.sbuf_tensor(f"{self.tag}_{name}", shape, dt))

    def ps(self, name, shape, dt=F32):
        return self.ctx.enter_context(self.nc.psum_tensor(f"{self.tag}_{name}", shape, dt))

    def sem(self, name):
        self.sems.append(self.nc.alloc_semaphore(f"{self.tag}_{name}"))
        return self.sems[-1]

    def release(self):
        self.nc.clear_and_free_semaphores(self.sems)
        self.nc.all_engine_barrier()


class LayerNorm:

    def __init__(self, ph, g, tag, keep_rows=False, source=None, scale=None, shift=None):
        self.g, self.keep_rows = g, keep_rows
        self.source, self.scale, self.shift = g.x if source is None else source, scale, shift
        if scale is not None:
            self.plain = ph.sb(f"{tag}_plain", [P, 2, BT, D])
            self.scaled = ph.sb(f"{tag}_scaled", [P, 2, BT, D])
            self.plain_done = ph.sem(f"{tag}_plain_done")
            self.scaled_done = ph.sem(f"{tag}_scaled_done")
        self.nc = ph.nc
        self.partial = ph.sb(f"{tag}_partial", [P, 2, BT, 6])
        self.moments = ph.sb(f"{tag}_moments", [P, 2, BT, 2])
        self.shifted = ph.sb(f"{tag}_shifted", [P, 2, BT])
        self.power = ph.sb(f"{tag}_power", [P, 2, BT])
        self.rows = ph.sb(f"{tag}_rows", [P, 2, BT, D])
        self.halves_done = ph.sem(f"{tag}_halves_done")
        self.moments_done = ph.sem(f"{tag}_moments_done")
        self.shift_done = ph.sem(f"{tag}_shift_done")
        self.rstd_done = ph.sem(f"{tag}_rstd_done")
        self.rows_done = ph.sem(f"{tag}_rows_done")
        self.turned = ph.sem(f"{tag}_turned")
        self.kept = ph.sem(f"{tag}_kept")

    def stats(self, dve, b, j=0):
        nc, g = self.nc, self.g
        for k in range(BT):
            nc.vector.bn_stats(self.partial[:, j, k, :], self.source[:, bass.ds(b * BT + k, 1), :]).then_inc(self.halves_done, 1)

    def stats_landed(self, dve, b):
        dve.wait_ge(self.halves_done, b * BT + BT)

    def aggregate(self, dve, b, j=0):
        nc = self.nc
        for k in range(BT):
            nc.vector.bn_aggr(self.moments[:, j, k, :], self.partial[:, j, k, :]).then_inc(self.moments_done, 1)

    def rstd(self, pool, b, j=0):
        nc, g = self.nc, self.g
        pool.wait_ge(self.moments_done, b * BT + BT)
        nc.gpsimd.tensor_tensor(self.shifted[:, j, :], self.moments[:, j, :, 1], g.eps[:, 0:BT],
                                ALU.add).then_inc(self.shift_done, 1)
        pool.wait_ge(self.shift_done, b + 1)
        nc.gpsimd.tensor_tensor(self.power[:, j, :], self.shifted[:, j, :], g.minus_half[:, 0:BT],
                                ALU.pow).then_inc(self.rstd_done, 1)

    def apply(self, dve, b, j=0, ahead=1):
        nc, g = self.nc, self.g
        dve.wait_ge(self.rstd_done, b + 1)
        if not (isinstance(b, int) and b < ahead):
            dve.wait_ge(self.turned, START + b - ahead + 1)
        out, done = (self.rows, self.rows_done) if self.scale is None else (self.plain, self.plain_done)
        kept = g.rows[:, bass.ds(b * BT, BT), :]
        for k in range(BT):
            args = (self.source[:, bass.ds(b * BT + k, 1), :], self.moments[:, j, k, 0:1], self.power[:, j, k:k + 1],
                    ALU.subtract, ALU.mult)
            nc.vector.tensor_scalar(out[:, j, k, :], *args).then_inc(done, 1)
            if self.keep_rows and self.scale is None:
                nc.vector.tensor_scalar(g.rows[:, bass.ds(b * BT + k, 1), :], *args)
        if self.scale is not None:
            dve.wait_ge(self.plain_done, b * BT + BT)
            nc.vector.tensor_tensor(self.scaled[:, j, :, :], self.plain[:, j, :, :], self.scale, ALU.mult).then_inc(self.scaled_done, 1)
            dve.wait_ge(self.scaled_done, b + 1)
            nc.vector.tensor_tensor(self.rows[:, j, :, :], self.scaled[:, j, :, :], self.shift, ALU.add).then_inc(self.rows_done, BT)
            if self.keep_rows:
                nc.vector.tensor_tensor(kept, self.scaled[:, j, :, :], self.shift, ALU.add)

    def turn(self, pe, b, out, j=0):
        pe.wait_ge(self.rows_done, b * BT + BT)
        for k in range(BT):
            mm = pe.transpose(out[:, k * P:(k + 1) * P], self.rows[:, j, k, :], self.g.ident[:])
        mm.then_inc(self.turned, 1)

    def start_turned(self, pe):
        pe.sem_inc(self.turned, START)

    def start_kept(self, act):
        act.sem_inc(self.kept, START)

    def wait_kept(self, pe, count):
        pe.wait_ge(self.kept, START + count)

    def keep(self, act, b, turned, seen=None):
        act.wait_ge(self.turned, START + b + 1)
        if seen is not None:
            act.sem_inc(seen, 1)
        self.nc.scalar.copy(self.g.xnT[:, bass.ds(b * S, S)], turned).then_inc(self.kept, 1)

    def all_turns(self, pe, psN):
        self.start_turned(pe)
        for j in range(2):
            self.turn(pe, j, psN[:, j, :], j)
        with pe.Fori(1, B // 2) as h:
            for j in range(2):
                self.wait_kept(pe, h * 2 + j - 1)
                self.turn(pe, h * 2 + j, psN[:, j, :], j)

    def all_keeps(self, act, psN):
        self.start_kept(act)
        with act.Fori(0, B // 2) as h:
            for j in range(2):
                self.keep(act, h * 2 + j, psN[:, j, 0:S])

    def all_rstds(self, pool):
        with pool.Fori(0, B // 2) as h:
            for j in range(2):
                self.rstd(pool, h * 2 + j, j)

    def all_rows(self, dve):
        def step(b, j):
            self.stats(dve, b + 1, 1 - j)
            self.stats_landed(dve, b + 1)
            self.apply(dve, b, j, 2)
            self.aggregate(dve, b + 1, 1 - j)

        self.stats(dve, 0, 0)
        self.stats_landed(dve, 0)
        self.aggregate(dve, 0, 0)
        for j in range(2):
            step(j, j)
        with dve.Fori(1, B // 2 - 1) as h:
            for j in range(2):
                step(h * 2 + j, j)
        step(B - 2, 0)
        self.apply(dve, B - 1, 1, 2)


def rounds(eng, new, count=B):
    new(0, True, lambda p, lag: p >= lag)
    with eng.Fori(1, count) as r:
        new(r, True, lambda p, lag: True)
    new(count, False, lambda p, lag: p < lag)


def rounds_ahead(eng, first, slots):
    first()
    slots(0, True, True, lambda p, lag: p >= lag)
    with eng.Fori(1, B - 1) as b:
        slots(b, True, True, lambda p, lag: True)
    slots(B - 1, True, False, lambda p, lag: True)
    slots(B, False, False, lambda p, lag: p < lag)


def load_and_prepare(nc, g, d, rest):
    with ExitStack() as ctx:
        ph = Phase(nc, ctx, "prep")
        wqT = ph.sb("wqT", [P, PAIRS, D])
        wkT = ph.sb("wkT", [P, PAIRS, D])
        psG = ph.ps("psG", [P, 4, 512])
        psC = ph.ps("psC", [P, 2, 512])
        x_in = [ph.sem(f"x_in{i}") for i in range(8)]
        qk_in = ph.sem("qk_in")
        ident_in = ph.sem("ident_in")
        ctx_in = ph.sem("ctx_in")
        rest_in = ph.sem("rest_in")
        g_done = ph.sem("g_done")
        c_done = ph.sem("c_done")
        block = ctx.enter_context(nc.Block())
        XB = NT // len(x_in)

        @block.sync
        def _(sp):
            sp.dma_start(wqT[:], d["wqT"]).then_inc(qk_in, 16)
            sp.dma_start(wkT[:], d["wkT"]).then_inc(qk_in, 16)
            sp.dma_start(g.ident[:], d["ident"]).then_inc(ident_in, 16)
            sp.dma_start(g.ctx[:], d["ctx"]).then_inc(ctx_in, 16)
            for i, sem in enumerate(x_in):
                sp.dma_start(g.x[:, i * XB:(i + 1) * XB, :],
                             d["x"][i * XB * P:(i + 1) * XB * P, :].rearrange("(t p) d -> p t d", p=P)).then_inc(sem, 16)
            for dst, src in rest:
                sp.dma_start(dst, src).then_inc(rest_in, 16)
            sp.wait_ge(rest_in, 16 * len(rest))
            for sem in x_in:
                sp.wait_ge(sem, 16)

        @block.tensor
        def _(pe):
            pe.wait_ge(ident_in, 16)
            pe.wait_ge(qk_in, 32)
            for h in range(H):
                k, q, j = h % 2, h // 8, (h % 8) // 2
                mm = pe.matmul(psG[:, 2 * q + k, j * P:(j + 1) * P], wqT[k * DH0:(k + 1) * DH0, h // 2, :],
                               wkT[k * DH0:(k + 1) * DH0, h // 2, :], start=True, stop=True)
                mm.then_inc(g_done, 1)
            pe.wait_ge(ctx_in, 16)
            for c in range(B * L // P):
                mm = pe.transpose(psC[:, c // 4, (c % 4) * P:(c % 4 + 1) * P], g.ctx[:, c, :], g.ident[:])
            mm.then_inc(c_done, 1)

        @block.scalar
        def _(act):
            for q in range(2):
                act.wait_ge(g_done, 8 * q + 8)
                for k in range(2):
                    nc.scalar.copy(g.G[:, 8 * q + k:8 * q + 8:2, :], psG[:, 2 * q + k, :].rearrange("p (h d) -> p h d", h=4))
            act.wait_ge(c_done, 1)
            nc.scalar.copy(g.ctxT[:].rearrange("p (a c) -> p a c", a=2), psC[:])


def layer0_attention(nc, g, d, rest):
    with ExitStack() as ctx:
        ph = Phase(nc, ctx, "a0")
        psA = ph.ps("psA", [P, 2, S])
        psS = ph.ps("psS", [P, 4, 512])
        psT = ph.ps("psT", [P, 512])
        psO = ph.ps("psO", [P, 512])
        psM = ph.ps("psM", [P, 512])
        cur = ph.sb("cur", [P, S])
        a_sb = ph.sb("a", [P, 2, 2, S])
        prob = ph.sb("prob", [P, 8, CAUSAL])
        probT = ph.sb("probT", [P, 4, CAUSAL])
        low = ph.sb("low", [P, 4, 2])
        total = ph.sb("total", [P, 4, 2])
        inv = ph.sb("inv", [P, 4, 2])
        v_sb = ph.sb("v", [P, BT, H * DH0])
        o_sb = ph.sb("o", [P, PAIRS, S])
        resid = ph.sb("resid", [P, BT, D])
        cur_ready = ph.sem("cur_ready")
        a_done = ph.sem("a_done")
        a_kept = ph.sem("a_kept")
        s_done = ph.sem("s_done")
        low_done = ph.sem("low_done")
        exp_done = ph.sem("exp_done")
        inv_done = ph.sem("inv_done")
        norm_done = ph.sem("norm_done")
        t_done = ph.sem("t_done")
        t_kept = ph.sem("t_kept")
        v_done = ph.sem("v_done")
        v_kept = ph.sem("v_kept")
        pv_done = ph.sem("pv_done")
        o_kept = ph.sem("o_kept")
        y_done = ph.sem("y_done")
        y_used = ph.sem("y_used")
        x_done = ph.sem("x_done")
        seen = ph.sem("seen")
        act_seen = ph.sem("act_seen")
        ln = LayerNorm(ph, g, "ln", keep_rows=True)
        ln_in = LayerNorm(ph, g, "ln_in")
        rest_in = ph.sem("rest_in")
        const_set = ph.sem("const_set")
        zero_set = ph.sem("zero_set")
        slots_cleared = ph.sem("slots_cleared")
        ZERO_PIECES = 16
        zero = ph.sb("zero", [P, MOE_BLOCKS * D // ZERO_PIECES])
        by_part = g.sorted_in.rearrange("(p r) d -> p (r d)", p=P)
        block = ctx.enter_context(nc.Block())
        blocks = [(0, 0, P), (1, P, 3 * P)]

        @block.sync
        def _(sp):
            for dst, src in rest:
                sp.dma_start(dst, src).then_inc(rest_in, 16)
            sp.wait_ge(zero_set, 1)
            w = MOE_BLOCKS * D // ZERO_PIECES
            for i in range(ZERO_PIECES):
                sp.dma_start(by_part[:, i * w:(i + 1) * w], zero[:]).then_inc(slots_cleared, 16)
            sp.wait_ge(rest_in, 16 * len(rest))
            sp.wait_ge(slots_cleared, 16 * ZERO_PIECES)

        @block.tensor
        def _(pe):
            ln_in.start_turned(pe)
            ln.start_turned(pe)
            def first():
                ln_in.turn(pe, 0, psM)

            def project(b, p):
                if p == 0:
                    ln_in.wait_kept(pe, b + 1)
                pe.wait_ge(a_kept, b * PAIRS + p)
                for k in range(2):
                    mm = pe.matmul(psA[:, k, :], g.G[:, 2 * p + k, :], g.xnT[:, bass.ds(b * S, S)], start=True, stop=True)
                mm.then_inc(a_done, 1)

            def scores(b, p, has_unit):
                pe.wait_ge(a_kept, b * PAIRS + p + 1)
                if has_unit(p, 2):
                    pe.wait_ge(exp_done, b * 32 + 4 * p - 4)
                for k in range(2):
                    for i, lo, hi in blocks:
                        mm = pe.matmul(psS[:, 2 * (p % 2) + k, lo:hi], a_sb[:, p % 2, k, i * P:(i + 1) * P],
                                       g.xnT[:, bass.ds(b * S, hi - lo)], start=True, stop=True)
                    mm.then_inc(s_done, 1)

            def values_in(b, p, prep, has_unit):
                if p == 4 and has_unit(p, 8):
                    pe.wait_ge(y_used, b)
                elif p == 6 and prep:
                    ln_in.wait_kept(pe, b + 2)
                elif p or has_unit(p, 8):
                    pe.wait_ge(v_kept, b * PAIRS + p)
                if p == 0 and has_unit(p, 8):
                    ln.wait_kept(pe, b - 1)
                if p == 0:
                    pe.wait_ge(cur_ready, b + 1)
                mm = pe.matmul(psM[:, 0:S], cur[:, (p % 2) * P:(p % 2 + 1) * P], g.wv[:, (p // 2) * S:(p // 2 + 1) * S],
                               start=True, stop=True)
                mm.then_inc(v_done, 1)

            def values(b, p):
                pe.wait_ge(t_kept, b * H + 2 * p - 4)
                pe.wait_ge(v_kept, b * PAIRS + 2 * ((p - 3) // 2) + 2)
                pe.wait_ge(o_kept, b * PAIRS + p - 3)
                q = (p - 3) % PAIRS
                for j, lo, hi in ((0, 0, S), (1, P, S)):
                    for k in range(2):
                        h = 2 * q + k
                        pt = probT[:, 2 * (q % 2) + k, 0:S] if j == 0 else probT[:, 2 * (q % 2) + k, S:CAUSAL]
                        mm = pe.matmul(psO[k * DH0:(k + 1) * DH0, lo:hi], v_sb[:, j, h * DH0:(h + 1) * DH0], pt,
                                       start=(j == 0), stop=(j == 1), skip_group_check=True)
                mm.then_inc(pv_done, 1)

            def turn(b, p, k):
                pe.wait_ge(norm_done, b * 32 + 4 * p - 6 + 2 * k)
                pe.wait_ge(t_kept, b * H + 2 * p - 4 + k)
                q = (p - 2) % PAIRS
                for c in range(3):
                    mm = pe.transpose(psT[:, c * P:(c + 1) * P], prob[:, 2 * (q % 4) + k, c * P:(c + 1) * P], g.ident[:])
                mm.then_inc(t_done, 1)

            def output(b):
                pe.wait_ge(o_kept, b * PAIRS)
                for i in range(BT):
                    for q in range(PAIRS):
                        mm = pe.matmul(psM[:, i * P:(i + 1) * P], o_sb[:, q, i * P:(i + 1) * P], g.wo[:, q, :],
                                       start=(q == 0), stop=(q == PAIRS - 1))
                mm.then_inc(y_done, 1)

            def tail_of_batch_before(b, p, new):
                if new:
                    pe.wait_ge(v_kept, b * PAIRS + p + 1)
                elif p == 7:
                    pe.wait_ge(y_used, b)
                else:
                    pe.wait_ge(v_kept, b * PAIRS)
                    ln.wait_kept(pe, b - 1)
                if p == 3:
                    output(b)
                else:
                    ln.turn(pe, b - 1, psM)

            def slots(b, new, prep, has_unit):
                for p in range(PAIRS):
                    if new and p == 0:
                        project(b, 0)
                    elif new:
                        scores(b, p, has_unit)
                    if has_unit(p, 2):
                        turn(b, p, 0)
                    if new and p == 0:
                        values_in(b, p, prep, has_unit)
                    if new and 0 < p < PAIRS - 1:
                        project(b, p + 1)
                    elif new and p == PAIRS - 1:
                        values_in(b, p, prep, has_unit)
                    if has_unit(p, 2):
                        turn(b, p, 1)
                    if new and p == 0:
                        project(b, 1)
                    elif new and p < PAIRS - 1:
                        values_in(b, p, prep, has_unit)
                    if has_unit(p, 3):
                        values(b, p)
                    if p == 3 and has_unit(p, 8):
                        tail_of_batch_before(b, p, new)
                    if p == 5 and prep:
                        pe.wait_ge(v_kept, b * PAIRS + 6)
                        ln_in.turn(pe, b + 1, psM)
                    if p == 7 and has_unit(p, 8):
                        tail_of_batch_before(b, p, new)
                    if new and p == 0:
                        scores(b, p, has_unit)

            rounds_ahead(pe, first, slots)

        @block.scalar
        def _(act):
            ln.start_kept(act)
            ln_in.start_kept(act)

            def first():
                ln_in.keep(act, 0, psM[:, 0:S])

            def keep_a(b, p):
                act.wait_ge(a_done, b * PAIRS + p + 1)
                if p >= 2:
                    act.wait_ge(s_done, b * H + 2 * p - 2)
                nc.scalar.activation(a_sb[:, p % 2, :, :], psA[:], ACT.Copy, scale=-(DH0 ** -0.5)).then_inc(a_kept, 1)

            def keep_t(b, p, k):
                q = (p - 2) % PAIRS
                if not (isinstance(b, int) and b == 0 and p < 4):
                    act.wait_ge(pv_done, b * PAIRS + p - 3)
                act.wait_ge(t_done, b * H + 2 * p - 3 + k)
                nc.scalar.copy(probT[:, 2 * (q % 2) + k, :], psT[:, 0:CAUSAL]).then_inc(t_kept, 1)

            def exps(b, p, has_unit):
                if has_unit(p, 4):
                    act.wait_ge(t_done, b * H + 2 * p - 6)
                for k in range(2):
                    u = 2 * (p % 2) + k
                    act.wait_ge(low_done, b * 32 + 4 * p + 2 * k + 2)
                    for i, lo, hi in blocks:
                        nc.scalar.activation(prob[:, 2 * (p % 4) + k, lo:hi], psS[:, u, lo:hi], ACT.Exp, bias=low[:, u, i:i + 1],
                                             scale=-1.0, accum_out=total[:, u, i:i + 1]).then_inc(exp_done, 1)

            def slots(b, new, prep, has_unit):
                for p in range(PAIRS):
                    if new and p == 0:
                        if has_unit(p, 8):
                            act.wait_ge(v_done, b * PAIRS)
                        act.wait_ge(ln_in.kept, START + b + 1)
                        act.sem_inc(act_seen, 1)
                        nc.scalar.copy(cur[:], g.xnT[:, bass.ds(b * S, S)]).then_inc(cur_ready, 1)
                    if prep and p == 6:
                        ln_in.keep(act, b + 1, psM[:, 0:S], act_seen)
                    if new and p == 0:
                        keep_a(b, 0)
                    if has_unit(p, 2):
                        keep_t(b, p, 0)
                    if new and 0 < p < PAIRS - 1:
                        keep_a(b, p + 1)
                    if has_unit(p, 2):
                        keep_t(b, p, 1)
                    if new and p == 0:
                        keep_a(b, 1)
                    if new:
                        exps(b, p, has_unit)
                    if p == 7 and has_unit(p, 8):
                        ln.keep(act, b - 1, psM[:, 0:S], act_seen)

            rounds_ahead(act, first, slots)

        @block.vector
        def _(dve):
            def lows(b, p, has_unit):
                if has_unit(p, 2):
                    dve.wait_ge(exp_done, b * 32 + 4 * p - 4)
                for k in range(2):
                    u = 2 * (p % 2) + k
                    dve.wait_ge(s_done, b * H + 2 * p + k + 1)
                    dve.sem_inc(seen, 1)
                    for i, lo, hi in blocks:
                        nc.vector.tensor_tensor_reduce(psS[:, u, lo:hi], psS[:, u, lo:hi], g.bias0[:, 2 * p + k, lo:hi],
                                                       1.0, LEAST, ALU.add, ALU.min, low[:, u, i:i + 1]).then_inc(low_done, 1)

            def norm(b, p):
                q = (p - 1) % PAIRS
                u = slice(2 * (q % 2), 2 * (q % 2) + 2)
                dve.wait_ge(exp_done, b * 32 + 4 * p)
                nc.vector.reciprocal(inv[:, u, :], total[:, u, :]).then_inc(inv_done, 1)
                dve.wait_ge(inv_done, b * PAIRS + p)
                for k in range(2):
                    for i, lo, hi in blocks:
                        w = prob[:, 2 * (q % 4) + k, lo:hi]
                        nc.vector.tensor_scalar(w, w, inv[:, 2 * (q % 2) + k, i:i + 1], None, ALU.mult).then_inc(norm_done, 1)

            def keep_o(b, p):
                q = (p - 3) % PAIRS
                if p == 3 and not (isinstance(b, int) and b == 0):
                    dve.wait_ge(y_done, b)
                dve.wait_ge(pv_done, b * PAIRS + p - 2)
                nc.vector.tensor_copy(o_sb[:, q, :], psO[:, 0:S]).then_inc(o_kept, 1)

            def slots(b, new, prep, has_unit):
                for p in range(PAIRS):
                    if prep and p == 2:
                        ln_in.stats_landed(dve, b + 1)
                    if p == 5 and has_unit(p, 8):
                        ln.stats_landed(dve, b - 1)
                        dve.sem_inc(seen, 1)
                        ln.aggregate(dve, b - 1)
                    if new:
                        lows(b, p, has_unit)
                    if has_unit(p, 1):
                        norm(b, p)
                    if new:
                        dve.wait_ge(v_done, b * PAIRS + p + 1)
                        nc.vector.tensor_copy(v_sb[:, p % 2, (p // 2) * S:(p // 2 + 1) * S], psM[:, 0:S]).then_inc(v_kept, 1)
                    if p == 3 and has_unit(p, 8):
                        dve.wait_ge(y_done, b)
                        nc.vector.tensor_tensor(resid[:], psM[:, 0:S].rearrange("p (t d) -> p t d", t=BT),
                                                g.x[:, bass.ds((b - 1) * BT, BT), :], ALU.add).then_inc(y_used, 1)
                        dve.wait_ge(y_used, b)
                        nc.vector.tensor_tensor(g.x[:, bass.ds((b - 1) * BT, BT), :], resid[:], g.bo[:], ALU.add).then_inc(x_done, 1)
                    if has_unit(p, 3):
                        keep_o(b, p)
                    if prep and p == 1:
                        ln_in.stats(dve, b + 1)
                    if prep and p == 2:
                        dve.sem_inc(seen, 1)
                        ln_in.aggregate(dve, b + 1)
                    if prep and p == 3:
                        ln_in.apply(dve, b + 1)
                    if p == 4 and has_unit(p, 8):
                        dve.wait_ge(x_done, b)
                        dve.sem_inc(seen, 1)
                        ln.stats(dve, b - 1)
                    if p == 5 and has_unit(p, 8):
                        ln.apply(dve, b - 1)

            def first():
                dve.wait_ge(const_set, 2)
                ln_in.stats(dve, 0)
                ln_in.stats_landed(dve, 0)
                ln_in.aggregate(dve, 0)
                ln_in.apply(dve, 0)

            rounds_ahead(dve, first, slots)

        @block.gpsimd
        def _(pool):
            nc.gpsimd.memset(zero[:], 0.0).then_inc(zero_set, 1)
            nc.gpsimd.memset(g.eps[:], LN_EPS).then_inc(const_set, 1)
            nc.gpsimd.memset(g.minus_half[:], -0.5).then_inc(const_set, 1)
            pool.wait_ge(const_set, 2)

            def slots(b, new, prep, has_unit):
                if prep:
                    ln_in.rstd(pool, b + 1)
                if has_unit(0, 8):
                    ln.rstd(pool, b - 1)

            rounds_ahead(pool, lambda: ln_in.rstd(pool, 0), slots)


def layer0_context(nc, g, d):
    UQ = 2 * S
    UB = UQ // P
    EPS = 1e-8
    SMOOTH = 9.0
    with ExitStack() as ctx:
        ph = Phase(nc, ctx, "c0")
        psX = ph.ps("psX", [P, 512])
        psW = ph.ps("psW", [P, 2, 512])
        psV = ph.ps("psV", [P, 512])
        psC = ph.ps("psC", [P, UB, 2 * D])
        psN = ph.ps("psN", [P, 2, 512])
        q_cur = ph.sb("q_cur", [P, 4, UQ])
        ctxT_cur = ph.sb("ctxT_cur", [P, 2, 2 * L])
        ctx1_cur = ph.sb("ctx1_cur", [P, 2, D + 1])
        tenth = ph.sb("tenth", [P, S])
        leaky = ph.sb("leaky", [P, 2, S])
        square = ph.sb("square", [P, S])
        norm2 = ph.sb("norm2", [P, 1])
        norm2e = ph.sb("norm2e", [P, 1])
        root = ph.sb("root", [P, 1])
        length = ph.sb("length", [P, 1])
        inv = ph.sb("inv", [P, 1])
        sharp = ph.sb("sharp", [P, 1])
        consts = ph.sb("consts", [P, 2])
        e_bd = ph.sb("e_bd", [P, 2, UQ])
        invz = ph.sb("invz", [P, UB])
        w_rows = ph.sb("w_rows", [P, UB, D])
        w_sb = ph.sb("w", [P, UQ])
        pre = ph.sb("pre", [P, UB, 2 * D])
        hid = ph.sb("hid", [P, UB, D])
        gate = ph.sb("gate", [P, UB, D])
        diff = ph.sb("diff", [P, UB, D])
        part = ph.sb("part", [P, UB, D])
        mix = ph.sb("mix", [P, UB, D])
        consts_set = ph.sem("consts_set")
        cur_ready = ph.sem("cur_ready")
        ctx_ready = ph.sem("ctx_ready")
        x_scores = ph.sem("x_scores")
        tenth_done = ph.sem("tenth_done")
        leaky_done = ph.sem("leaky_done")
        square_done = ph.sem("square_done")
        root_steps = ph.sem("root_steps")
        sharp_steps = ph.sem("sharp_steps")
        e_done = ph.sem("e_done")
        w_done = ph.sem("w_done")
        invz_done = ph.sem("invz_done")
        rows_done = ph.sem("rows_done")
        w_turned = ph.sem("w_turned")
        w_kept = ph.sem("w_kept")
        c_done = ph.sem("c_done")
        pre_done = ph.sem("pre_done")
        tanh_done = ph.sem("tanh_done")
        diff_done = ph.sem("diff_done")
        mix_steps = ph.sem("mix_steps")
        pool_seen = ph.sem("pool_seen")
        x_done = ph.sem("x_done")
        ln = LayerNorm(ph, g, "ln", keep_rows=True)
        block = ctx.enter_context(nc.Block())
        ROUNDS = B // 8
        experts_in = ph.sem("experts_in")

        @block.sync
        def _(sp):
            for i in range(4):
                n = 2 * E // 4
                sp.dma_start(g.in_lo[:, i * n:(i + 1) * n, :].bitcast(F32), d["gate_up"][:, i * n:(i + 1) * n, :]).then_inc(experts_in, 16)
            sp.dma_start(g.down[:], d["down"]).then_inc(experts_in, 16)
            sp.wait_ge(experts_in, 16 * 5)

        @block.tensor
        def _(pe):
            ln.start_turned(pe)
            pe.wait_ge(consts_set, 4)
            def slots(r, new, has_unit):
                for p in range(4):
                    n, now, last = r * 4 + p, p % 2, 1 - p % 2
                    if new:
                        pe.wait_ge(cur_ready, n + 1)
                        pe.wait_ge(ctx_ready, n * 2 + 2)
                        if has_unit(p, 1):
                            pe.wait_ge(leaky_done, n)
                        for j in range(2):
                            mm = pe.matmul(psX[j * L:(j + 1) * L, 0:S], ctxT_cur[:, now, j * L:(j + 1) * L],
                                           q_cur[:, p, j * S:(j + 1) * S], start=True, stop=True)
                        mm.then_inc(x_scores, 1)
                    if has_unit(p, 1):
                        pe.wait_ge(e_done, n * 2)
                        pe.wait_ge(rows_done, n - 1)
                        for k in range(UB):
                            mm = pe.matmul(psW[:, k // 2, (k % 2) * 256:(k % 2) * 256 + D + 1], e_bd[:, last, k * P:(k + 1) * P],
                                           ctx1_cur[:, last, :], start=True, stop=True)
                        mm.then_inc(w_done, 1)
                        pe.wait_ge(pre_done, n - 1)
                        for k in range(UB):
                            if k % 2 == 0:
                                pe.matmul(psC[:, k, :], q_cur[:, (p + 3) % 4, k * P:(k + 1) * P], g.wcat[:, 0, :], start=True, stop=False)
                            if k == 0:
                                pe.wait_ge(rows_done, n)
                                for c in range(UB):
                                    mm = pe.transpose(psV[:, c * P:(c + 1) * P], w_rows[:, c, :], g.ident[:])
                                mm.then_inc(w_turned, 1)
                            if k % 2 == 1:
                                pe.matmul(psC[:, k, :], q_cur[:, (p + 3) % 4, k * P:(k + 1) * P], g.wcat[:, 0, :], start=True, stop=False)
                            if k == 0:
                                pe.wait_ge(w_kept, n)
                            mm = pe.matmul(psC[:, k, :], w_sb[:, k * P:(k + 1) * P], g.wcat[:, 1, :], start=False, stop=True)
                        mm.then_inc(c_done, 1)
                    if has_unit(p, 3):
                        ln.wait_kept(pe, n * 2 - 6)
                        for j in range(2):
                            ln.turn(pe, n * 2 - 6 + j, psN[:, j, :], j)

            rounds(pe, slots, ROUNDS)

        @block.scalar
        def _(act):
            ln.start_kept(act)

            def slots(r, new, has_unit):
                for p in range(4):
                    n, now = r * 4 + p, p % 2
                    if new:
                        if has_unit(p, 4):
                            act.wait_ge(c_done, n - 3)
                        nc.scalar.copy(q_cur[:, p, :], g.xnT[:, bass.ds(n * UQ, UQ)]).then_inc(cur_ready, 1)
                    if has_unit(p, 2):
                        act.wait_ge(pre_done, n - 1)
                        nc.scalar.activation(hid[:], pre[:, :, 0:D], ACT.Tanh).then_inc(tanh_done, 1)
                        nc.scalar.activation(gate[:], pre[:, :, D:2 * D], ACT.Tanh, scale=0.5).then_inc(tanh_done, 1)
                    if has_unit(p, 1):
                        act.wait_ge(w_turned, n)
                        if has_unit(p, 2):
                            act.wait_ge(c_done, n - 1)
                        nc.scalar.copy(w_sb[:], psV[:]).then_inc(w_kept, 1)
                    if new:
                        act.wait_ge(sharp_steps, n * 3 + 3)
                        if has_unit(p, 2):
                            act.wait_ge(w_done, n - 1)
                        for j in range(2):
                            rows = slice(j * L, (j + 1) * L)
                            nc.scalar.activation(e_bd[rows, now, j * S:(j + 1) * S], leaky[rows, now, :], ACT.Exp,
                                                 scale=sharp[rows, 0:1]).then_inc(e_done, 1)
                    if has_unit(p, 3):
                        for j in range(2):
                            ln.keep(act, n * 2 - 6 + j, psN[:, j, 0:S])

            rounds(act, slots, ROUNDS)

        @block.gpsimd
        def _(pool):
            nc.gpsimd.memset(ctx1_cur[:, :, D:D + 1], 1.0).then_inc(consts_set, 1)
            nc.gpsimd.memset(consts[:, 0:1], EPS).then_inc(consts_set, 1)
            nc.gpsimd.memset(consts[:, 1:2], 0.5).then_inc(consts_set, 1)
            nc.gpsimd.memset(e_bd[:], 0.0).then_inc(consts_set, 1)
            pool.wait_ge(consts_set, 4)

            def slots(r, new, has_unit):
                for p in range(4):
                    n = r * 4 + p
                    if new:
                        pool.wait_ge(square_done, n + 1)
                        nc.gpsimd.tensor_tensor(norm2e[:], norm2[:], consts[:, 0:1], ALU.add).then_inc(root_steps, 1)
                        pool.wait_ge(root_steps, n * 2 + 1)
                        nc.gpsimd.tensor_tensor(root[:], norm2e[:], consts[:, 1:2], ALU.pow).then_inc(root_steps, 1)
                    if has_unit(p, 2):
                        rows = bass.ds((n - 2) * UB, UB)
                        pool.wait_ge(tanh_done, n * 2 - 3)
                        pool.sem_inc(pool_seen, 1)
                        nc.gpsimd.tensor_tensor(diff[:], g.rows[:, rows, :], hid[:], ALU.subtract).then_inc(diff_done, 1)
                        pool.wait_ge(mix_steps, n * 2 - 2)
                        pool.sem_inc(pool_seen, 1)
                        nc.gpsimd.tensor_tensor(g.x[:, rows, :], g.x[:, rows, :], mix[:], ALU.add).then_inc(x_done, 1)
                        for j in range(2):
                            ln.rstd(pool, n * 2 - 4 + j, j)

            rounds(pool, slots, ROUNDS)

        @block.vector
        def _(dve):
            dve.wait_ge(consts_set, 4)

            def slots(r, new, has_unit):
                for p in range(4):
                    n, now = r * 4 + p, p % 2
                    if new:
                        if has_unit(p, 2):
                            dve.wait_ge(w_done, n - 1)
                        nc.vector.tensor_copy(ctxT_cur[:, now, :], g.ctxT[:, bass.ds(n * 2 * L, 2 * L)]).then_inc(ctx_ready, 1)
                        nc.vector.tensor_copy(ctx1_cur[:, now, 0:D], g.ctx[:, bass.ds(n, 1), :]).then_inc(ctx_ready, 1)
                    if has_unit(p, 2):
                        dve.wait_ge(c_done, n - 1)
                        nc.vector.tensor_tensor(pre[:], psC[:], g.bcat[:], ALU.add).then_inc(pre_done, 1)
                    if new:
                        dve.wait_ge(x_scores, n + 1)
                        nc.vector.tensor_scalar(tenth[:], psX[:, 0:S], 0.1, None, ALU.mult).then_inc(tenth_done, 1)
                        dve.wait_ge(tenth_done, n + 1)
                        if has_unit(p, 2):
                            dve.wait_ge(e_done, n * 2 - 2)
                        nc.vector.tensor_tensor(leaky[:, now, :], psX[:, 0:S], tenth[:], ALU.max).then_inc(leaky_done, 1)
                        dve.wait_ge(leaky_done, n + 1)
                        nc.vector.tensor_tensor_reduce(square[:], leaky[:, now, :], leaky[:, now, :], 1.0, 0.0, ALU.mult, ALU.add,
                                                       norm2[:]).then_inc(square_done, 1)
                    if has_unit(p, 1):
                        dve.wait_ge(w_done, n)
                        nc.vector.reciprocal(invz[:], psW[:].rearrange("p b (k c) -> p (b k) c", c=256)[:, :, D]).then_inc(invz_done, 1)
                        dve.wait_ge(invz_done, n)
                        if has_unit(p, 2):
                            dve.wait_ge(w_turned, n - 1)
                        for k in range(UB):
                            at = psW[:, k // 2, (k % 2) * 256:(k % 2) * 256 + D]
                            i = nc.vector.tensor_scalar(w_rows[:, k, :], at, invz[:, k:k + 1], None, ALU.mult)
                        i.then_inc(rows_done, 1)
                    if new:
                        dve.wait_ge(root_steps, n * 2 + 2)
                        if has_unit(p, 1):
                            dve.wait_ge(e_done, n * 2)
                        nc.vector.tensor_scalar(length[:], root[:], EPS, None, ALU.add).then_inc(sharp_steps, 1)
                        dve.wait_ge(sharp_steps, n * 3 + 1)
                        nc.vector.reciprocal(inv[:], length[:]).then_inc(sharp_steps, 1)
                        dve.wait_ge(sharp_steps, n * 3 + 2)
                        nc.vector.tensor_scalar(sharp[:], inv[:], SMOOTH, None, ALU.mult).then_inc(sharp_steps, 1)
                    if has_unit(p, 2):
                        dve.wait_ge(tanh_done, n * 2 - 2)
                        dve.wait_ge(diff_done, n - 1)
                        nc.vector.scalar_tensor_tensor(out=part[:], in0=gate[:], scalar=1.0, in1=diff[:], op0=ALU.add,
                                                       op1=ALU.mult).then_inc(mix_steps, 1)
                        dve.wait_ge(mix_steps, n * 2 - 3)
                        nc.vector.scalar_tensor_tensor(out=mix[:], in0=part[:], scalar=0.5, in1=hid[:], op0=ALU.mult,
                                                       op1=ALU.add).then_inc(mix_steps, 1)
                    if has_unit(p, 3):
                        for j in range(2):
                            ln.apply(dve, n * 2 - 6 + j, j, 2)
                    if has_unit(p, 2):
                        dve.wait_ge(x_done, n - 1)
                        dve.sem_inc(seen, 1)
                        for j in range(2):
                            ln.stats(dve, n * 2 - 4 + j, j)
                        ln.stats_landed(dve, n * 2 - 3)
                        dve.sem_inc(seen, 1)
                        for j in range(2):
                            ln.aggregate(dve, n * 2 - 4 + j, j)

            seen = ph.sem("seen")
            rounds(dve, slots, ROUNDS)


class Routing:

    def __init__(self, ph, g, tag):
        self.g, self.nc = g, ph.nc
        full = lambda name: ph.sb(f"{tag}_{name}", [P, NT, E])
        col = lambda name: ph.sb(f"{tag}_{name}", [P, NT])
        self.logits, self.hit, self.score, self.rest = full("logits"), full("hit"), full("score"), full("rest")
        self.best, self.first, self.second, self.pick = col("best"), col("first"), col("second"), col("pick")
        self.gap, self.e_gap, self.one_plus = col("gap"), col("e_gap"), col("one_plus")
        self.step = ph.sem(f"{tag}_step")
        self.gap_done = ph.sem(f"{tag}_gap_done")
        self.exp_done = ph.sem(f"{tag}_exp_done")
        self.count = 0
        self.meanwhile = None

    def then(self, dve, instruction):
        instruction.then_inc(self.step, 1)
        self.count += 1
        if self.meanwhile:
            self.meanwhile(self.count)
        dve.wait_ge(self.step, self.count)

    def choose(self, dve, psum, top, weight):
        v, g = self.nc.vector, self.g
        wide = lambda t: t[:].unsqueeze(2).to_broadcast([P, NT, E])
        self.then(dve, v.tensor_copy(self.logits[:], psum))
        source, bests = self.logits, (self.first, self.second)
        for k in range(2):
            self.then(dve, v.tensor_reduce(bests[k][:], source[:], AX.X, ALU.max))
            self.then(dve, v.tensor_tensor(self.hit[:], source[:], wide(bests[k]), ALU.is_ge))
            self.then(dve, v.tensor_tensor(self.score[:], self.hit[:], g.countdown[:], ALU.mult))
            self.then(dve, v.tensor_reduce(self.pick[:], self.score[:], AX.X, ALU.max))
            self.then(dve, v.tensor_tensor(top[:, k, :, :], g.countdown[:], wide(self.pick), ALU.is_equal))
            if k == 0:
                self.then(dve, v.tensor_scalar(self.hit[:], top[:, 0, :, :], -LEAST, None, ALU.mult))
                self.then(dve, v.tensor_tensor(self.rest[:], self.logits[:], self.hit[:], ALU.add))
                source = self.rest
        v.tensor_tensor(self.gap[:], self.second[:], self.first[:], ALU.subtract).then_inc(self.gap_done, 1)
        dve.wait_ge(self.exp_done, 1)
        self.then(dve, v.tensor_scalar(self.one_plus[:], self.e_gap[:], 1.0, None, ALU.add))
        self.then(dve, v.reciprocal(weight[:, 0, :], self.one_plus[:]))
        self.then(dve, v.tensor_tensor(weight[:, 1, :], self.e_gap[:], weight[:, 0, :], ALU.mult))

    def exponent(self, act):
        act.wait_ge(self.gap_done, 1)
        self.nc.scalar.activation(self.e_gap[:], self.gap[:], ACT.Exp).then_inc(self.exp_done, 1)


def layer0_route(nc, g, d):
    with ExitStack() as ctx:
        ph = Phase(nc, ctx, "r0")
        psN = ph.ps("psN", [P, 2, 512])
        psL = ph.ps("psL", [P, NT, E])
        psR = ph.ps("psR", [P, NT, E])
        psK = ph.ps("psK", [P, NT, E])
        top_sum = ph.sb("top_sum", [P, NT, E], BF16)
        zeros = ph.sb("zeros", [P, NT])
        upto = ph.sb("upto", [P, NT, E])
        before = ph.sb("before", [P, NT, E])
        rank = ph.sb("rank", [P, NT, E])
        padded = ph.sb("padded", [P, E])
        padded_i = ph.sb("padded_i", [P, E], I32)
        blocks_i = ph.sb("blocks_i", [P, E], I32)
        blocks = ph.sb("blocks", [P, E])
        ends = ph.sb("ends", [P, E])
        base = ph.sb("base", [P, E])
        place = ph.sb("place", [P, NT, E])
        chosen = ph.sb("chosen", [P, NT, E])
        slot_f = ph.sb("slot_f", [P, NT])
        late = ph.sb("late", [P, MOE_BLOCKS, E])
        expert_f = ph.sb("expert_f", [P, MOE_BLOCKS])
        expert_c = ph.sb("expert_c", [P, MOE_BLOCKS])
        logits_done = ph.sem("logits_done")
        top_ready = ph.sem("top_ready")
        ranks_done = ph.sem("ranks_done")
        ln = LayerNorm(ph, g, "ln", keep_rows=True, source=g.rows, scale=g.gamma[:], shift=g.beta[:])
        route = Routing(ph, g, "rt")
        block = ctx.enter_context(nc.Block())

        @block.tensor
        def _(pe):
            ln.all_turns(pe, psN)
            ln.wait_kept(pe, B)
            for t in range(NT):
                mm = pe.matmul(psL[:, t, :], g.xnT[:, t * P:(t + 1) * P], g.router[:], start=True, stop=True)
            mm.then_inc(logits_done, 1)
            pe.wait_ge(top_ready, 1)
            pe.matmul(psR[:], g.before_mask[:], top_sum[:], start=True, stop=True)
            pe.matmul(psK[:], g.ones_bf[:], top_sum[:], start=True, stop=True).then_inc(ranks_done, 1)

        @block.scalar
        def _(act):
            ln.all_keeps(act, psN)
            route.exponent(act)

        @block.gpsimd
        def _(pool):
            ln.all_rstds(pool)

        @block.vector
        def _(dve):
            v = nc.vector
            v.memset(zeros[:], 0.0)
            ln.all_rows(dve)
            dve.wait_ge(logits_done, 1)
            route.choose(dve, psL[:], g.top, g.weight)
            then = lambda i: route.then(dve, i)
            v.tensor_tensor(top_sum[:], g.top[:, 0, :, :], g.top[:, 1, :, :], ALU.add).then_inc(top_ready, 1)
            dve.wait_ge(ranks_done, 1)
            for e in range(E):
                i = v.tensor_tensor_scan(upto[:, :, e], psK[:, :, e], zeros[:], 0.0, ALU.add, ALU.add)
            then(i)
            then(v.tensor_tensor(before[:], upto[:], psK[:], ALU.subtract))
            then(v.tensor_tensor(rank[:], before[:], psR[:], ALU.add))
            then(v.tensor_scalar(padded[:], upto[:, NT - 1, :], float(P - 1), None, ALU.add))
            then(v.tensor_copy(padded_i[:], padded[:]))
            then(v.tensor_scalar(blocks_i[:], padded_i[:], 7, None, ALU.logical_shift_right))
            then(v.tensor_copy(blocks[:], blocks_i[:]))
            then(v.tensor_tensor_scan(ends[:], blocks[:], zeros[:, 0:E], 0.0, ALU.add, ALU.add))
            then(v.tensor_tensor(padded[:], ends[:], blocks[:], ALU.subtract))
            then(v.tensor_scalar(base[:], padded[:], float(P), None, ALU.mult))
            then(v.tensor_tensor(place[:], rank[:], base[:].unsqueeze(1).to_broadcast([P, NT, E]), ALU.add))
            for k in range(2):
                then(v.tensor_tensor(chosen[:], place[:], g.top[:, k, :, :], ALU.mult))
                then(v.tensor_reduce(slot_f[:], chosen[:], AX.X, ALU.add))
                then(v.tensor_copy(g.slot[:, k, :], slot_f[:]))
            then(v.tensor_tensor(late[:], g.block_index[:].unsqueeze(2).to_broadcast([P, MOE_BLOCKS, E]),
                                 ends[:].unsqueeze(1).to_broadcast([P, MOE_BLOCKS, E]), ALU.is_ge))
            then(v.tensor_reduce(expert_f[:], late[:], AX.X, ALU.add))
            then(v.tensor_scalar(expert_c[:], expert_f[:], float(E - 1), None, ALU.min))
            then(v.tensor_copy(g.expert[:], expert_c[:]))


class SharedExpert:

    def __init__(self, ph, g, tag, w_in, w_out, clip):
        self.g, self.nc, self.w_in, self.w_out, self.clip = g, ph.nc, w_in, w_out, clip
        self.psG = ph.ps(f"{tag}_psG", [P, 512])
        self.psU = ph.ps(f"{tag}_psU", [P, 512])
        self.psY = ph.ps(f"{tag}_psY", [P, 4, D])
        self.gate = ph.sb(f"{tag}_gate", [P, 2, 512])
        self.act = ph.sb(f"{tag}_act", [P, 2, 512])
        self.hid = ph.sb(f"{tag}_hid", [P, 2, 512])
        self.in_done, self.clipped = ph.sem(f"{tag}_in_done"), ph.sem(f"{tag}_clipped")
        self.silu_done, self.hid_done = ph.sem(f"{tag}_silu_done"), ph.sem(f"{tag}_hid_done")
        self.y_done, self.x_done = ph.sem(f"{tag}_y_done"), ph.sem(f"{tag}_x_done")

    def tensor(self, pe, n, p, new, lagging):
        g = self.g
        if new:
            pe.wait_ge(self.hid_done, n)
            pe.matmul(self.psG[:], self.w_in[:, 0:P], g.xnT[:, bass.ds(n * 512, 512)], start=True, stop=True)
            pe.matmul(self.psU[:], self.w_in[:, P:2 * P], g.xnT[:, bass.ds(n * 512, 512)], start=True, stop=True).then_inc(self.in_done, 1)
        if lagging:
            pe.wait_ge(self.hid_done, n)
            pe.wait_ge(self.x_done, n - 1)
            for k in range(4):
                mm = pe.matmul(self.psY[:, k, :], self.hid[:, 1 - p, k * P:(k + 1) * P], self.w_out, start=True, stop=True)
            mm.then_inc(self.y_done, 1)

    def scalar(self, act, n, p, new, lagging):
        if new:
            act.wait_ge(self.clipped if self.clip else self.in_done, n + 1)
            src = self.gate[:, p, :] if self.clip else self.psG[:]
            self.nc.scalar.activation(self.act[:, p, :], src, ACT.Silu).then_inc(self.silu_done, 1)

    def vector(self, dve, n, p, new, lagging):
        v, g = self.nc.vector, self.g
        if new:
            dve.wait_ge(self.in_done, n + 1)
            if self.clip:
                v.tensor_scalar(self.gate[:, p, :], self.psG[:], CLIP, -CLIP, ALU.min, ALU.max).then_inc(self.clipped, 1)
            dve.wait_ge(self.silu_done, n + 1)
            v.tensor_tensor(self.hid[:, p, :], self.act[:, p, :], self.psU[:], ALU.mult).then_inc(self.hid_done, 1)
        if lagging:
            rows = bass.ds((n - 1) * 4, 4)
            dve.wait_ge(self.y_done, n)
            v.tensor_tensor(g.x[:, rows, :], g.x[:, rows, :], self.psY[:], ALU.add).then_inc(self.x_done, 1)

    def slots(self, step):
        def body(r, new, has_unit):
            for p in range(2):
                step(r * 2 + p, p, new, has_unit(p, 1))
        return body


def layer0_shared_and_dispatch(nc, g, d):
    PIECE = 4
    with ExitStack() as ctx:
        ph = Phase(nc, ctx, "s0")
        shared = SharedExpert(ph, g, "sh", g.shared_in0, g.shared_out0[:], True)
        sent = ph.sem("sent")
        hi_done = ph.sem("hi_done")
        lo_done = ph.sem("lo_done")
        block = ctx.enter_context(nc.Block())

        @block.gpsimd
        def _(pool):
            for k in range(2):
                for t in range(NT):
                    nc.gpsimd.indirect_dma_start(out=g.sorted_in, out_offset=bass.IndirectOffsetOnAxis(ap=g.slot[:, k, t:t + 1], axis=0),
                                                 in_=g.rows[:, t, :], in_offset=None).then_inc(sent, 16)
            pool.wait_ge(sent, 16 * 2 * NT)

        @block.tensor
        def _(pe):
            rounds(pe, shared.slots(lambda *a: shared.tensor(pe, *a)), T // 1024)

        @block.scalar
        def _(act):
            rounds(act, shared.slots(lambda *a: shared.scalar(act, *a)), T // 1024)
            for i in range(0, 2 * E, PIECE):
                nc.scalar.copy(g.in_hi[:, i:i + PIECE, :], g.in_lo[:, i:i + PIECE, :].bitcast(F32)).then_inc(hi_done, 1)

        @block.vector
        def _(dve):
            rounds(dve, shared.slots(lambda *a: shared.vector(dve, *a)), T // 1024)
            for i in range(0, 2 * E, PIECE):
                dve.wait_ge(hi_done, i // PIECE + 1)
                nc.vector.tensor_tensor(g.in_lo[:, i:i + PIECE, :], g.in_lo[:, i:i + PIECE, :].bitcast(F32),
                                        g.in_hi[:, i:i + PIECE, :].bitcast(F32), ALU.subtract).then_inc(lo_done, 1)
            dve.wait_ge(lo_done, 2 * E // PIECE)


def layer0_experts(nc, g, d):
    FC = F0 // P
    with ExitStack() as ctx:
        ph = Phase(nc, ctx, "e0")
        psX = ph.ps("psX", [P, 512])
        psG = ph.ps("psG", [P, 2, 512])
        psU = ph.ps("psU", [P, 2, 512])
        psH = ph.ps("psH", [P, 512])
        psY = ph.ps("psY", [P, 512])
        rows = ph.sb("rows", [P, 4, D])
        cols_hi = ph.sb("cols_hi", [P, 2, P], F32R)
        cols_lo = ph.sb("cols_lo", [P, 2, P], F32R)
        gate = ph.sb("gate", [P, F0])
        act_sb = ph.sb("act", [P, F0])
        hid = ph.sb("hid", [P, 4, F0])
        hidT = ph.sb("hidT", [P, F0])
        y_sb = ph.sb("y", [P, 2, D])
        rows_in = [ph.sem(f"rows_in{i}") for i in range(4)]
        turned = ph.sem("turned")
        hi_done = ph.sem("hi_done")
        lo_done = ph.sem("lo_done")
        gate_in = ph.sem("gate_in")
        in_done = ph.sem("in_done")
        clipped = ph.sem("clipped")
        silu_done = ph.sem("silu_done")
        hid_done = ph.sem("hid_done")
        h_turned = ph.sem("h_turned")
        h_kept = ph.sem("h_kept")
        y_done = ph.sem("y_done")
        y_kept = ph.sem("y_kept")
        y_free = ph.sem("y_free")
        y_out = [ph.sem(f"y_out{i}") for i in range(2)]
        block = ctx.enter_context(nc.Block())
        N = MOE_BLOCKS
        src = g.sorted_in.rearrange("(n p) d -> p n d", p=P)
        dst = g.sorted_out.rearrange("(n p) d -> p n d", p=P)

        @block.sync
        def _(sp):
            for n in range(4):
                sp.dma_start(rows[:, n, :], src[:, n, :]).then_inc(rows_in[n], 16)
            with sp.Fori(0, N // 4 - 1) as r:
                for k in range(4):
                    n = r * 4 + k
                    sp.wait_ge(turned, n + 1)
                    sp.dma_start(rows[:, k, :], src[:, bass.ds(n + 4, 1), :]).then_inc(rows_in[k], 16)

        @block.gpsimd
        def _(pool):
            pool.sem_inc(y_free, START)

            def store(r, later):
                for k in range(2):
                    pool.wait_ge(y_kept, r * 2 + k + 1)
                    nc.gpsimd.dma_start(dst[:, bass.ds(r * 2 + k, 1), :], y_sb[:, k, :]).then_inc(y_out[k], 16)
                    if k or later:
                        pool.wait_ge(y_out[1 - k], (r + k) * 16)
                        pool.sem_inc(y_free, 1)

            store(0, False)
            with pool.Fori(1, N // 2) as r:
                store(r, True)
            for k in range(2):
                pool.wait_ge(y_out[k], 16 * (N // 2))

        def each(eng, slot):
            def body(r, new, has_unit):
                for p in range(4):
                    slot(r * 4 + p, p, new, has_unit(p, 1), has_unit(p, 2), has_unit(p, 3))
            rounds(eng, body, N // 4)

        @block.tensor
        def _(pe):
            def slot(n, p, new, one, two, three):
                if new:
                    pe.wait_ge(rows_in[p], (n - p) * 4 + 16)
                    pe.wait_ge(lo_done, n)
                    pe.transpose(psX[:, 0:P], rows[:, p, :], g.ident[:]).then_inc(turned, 1)
                if three:
                    pe.wait_ge(hid_done, n - 2)
                    pe.wait_ge(h_kept, n - 3)
                    for c in range(FC):
                        mm = pe.transpose(psH[:, c * P:(c + 1) * P], hid[:, (p + 1) % 4, c * P:(c + 1) * P], g.ident[:])
                    mm.then_inc(h_turned, 1)
                if one:
                    e = pe.value_load(g.expert[0:1, bass.ds(n - 1, 1)], min_val=0, max_val=E - 1)
                    pe.wait_ge(lo_done, n)
                    q = (p + 1) % 2
                    for ps, row, done in ((psG, e * 2, gate_in), (psU, e * 2 + 1, in_done)):
                        pe.matmul(ps[:, q, :], cols_hi[:, q, :], g.in_hi[:, bass.ds(row, 1), :], start=True, stop=False)
                        pe.matmul(ps[:, q, :], cols_hi[:, q, :], g.in_lo[:, bass.ds(row, 1), :], start=False, stop=False)
                        pe.matmul(ps[:, q, :], cols_lo[:, q, :], g.in_hi[:, bass.ds(row, 1), :], start=False, stop=True).then_inc(done, 1)
                if three:
                    e = pe.value_load(g.expert[0:1, bass.ds(n - 3, 1)], min_val=0, max_val=E - 1)
                    pe.wait_ge(h_kept, n - 2)
                    pe.wait_ge(y_kept, n - 3)
                    for c in range(FC):
                        mm = pe.matmul(psY[:, 0:D], hidT[:, c * P:(c + 1) * P], g.down[:, bass.ds(e * FC + c, 1), :],
                                       start=(c == 0), stop=(c == FC - 1))
                    mm.then_inc(y_done, 1)

            each(pe, slot)

        @block.scalar
        def _(act):
            def slot(n, p, new, one, two, three):
                if new:
                    act.wait_ge(turned, n + 1)
                    if two:
                        act.wait_ge(in_done, n - 1)
                    nc.scalar.copy(cols_hi[:, p % 2, :], psX[:, 0:P]).then_inc(hi_done, 1)
                if three:
                    act.wait_ge(h_turned, n - 2)
                    act.wait_ge(y_done, n - 3)
                    nc.scalar.copy(hidT[:], psH[:]).then_inc(h_kept, 1)
                if one:
                    act.wait_ge(clipped, n)
                    nc.scalar.activation(act_sb[:], gate[:], ACT.Silu).then_inc(silu_done, 1)

            each(act, slot)

        @block.vector
        def _(dve):
            def slot(n, p, new, one, two, three):
                if new:
                    dve.wait_ge(hi_done, n + 1)
                    nc.vector.tensor_tensor(cols_lo[:, p % 2, :], psX[:, 0:P], cols_hi[:, p % 2, :].bitcast(F32), ALU.subtract).then_inc(lo_done, 1)
                if one:
                    q = (p + 1) % 2
                    dve.wait_ge(gate_in, n)
                    nc.vector.tensor_scalar(gate[:], psG[:, q, :], CLIP, -CLIP, ALU.min, ALU.max).then_inc(clipped, 1)
                    dve.wait_ge(silu_done, n)
                    dve.wait_ge(in_done, n)
                    nc.vector.tensor_tensor(hid[:, (p + 3) % 4, :], act_sb[:], psU[:, q, :], ALU.mult).then_inc(hid_done, 1)
                if three:
                    q = (p + 1) % 2
                    dve.wait_ge(y_done, n - 2)
                    if not (isinstance(n, int) and n < 5):
                        dve.wait_ge(y_free, START + n - 4)
                    nc.vector.tensor_copy(y_sb[:, q, :], psY[:, 0:D]).then_inc(y_kept, 1)

            each(dve, slot)


def layer1_attention(nc, g, d):
    G4 = H // 4
    DH1 = D // H
    SCALAR_TURNS = (1, 2, 6)
    VW = 32
    SCALE = float(np.float32(DH1) ** np.float32(-0.5))
    with ExitStack() as ctx:
        ph = Phase(nc, ctx, "a1")
        psA = ph.ps("psA", [P, 512])
        psS = ph.ps("psS", [P, 4, 512])
        psT = ph.ps("psT", [P, 512])
        psO = ph.ps("psO", [P, 512])
        psM = ph.ps("psM", [P, 512])
        cur = ph.sb("cur", [P, S])
        sel = ph.sb("sel", [P, 4, G4, P], F32R)
        sel_in = ph.sb("sel_in", [P, 4, G4, P])
        qk = ph.sb("qk", [P, 2, S])
        qk_hi = ph.sb("qk_hi", [P, 2, S], F32R)
        qk_lo = ph.sb("qk_lo", [P, 2, S], F32R)
        q4 = ph.sb("q4", [P, 2, S], F32R)
        k4 = ph.sb("k4", [P, 2, 4, S], F32R)
        prob = ph.sb("prob", [P, 8, BT * S])
        probT = ph.sb("probT", [P, 8, BT * S])
        low = ph.sb("low", [P, 2, 4])
        v_aug = ph.sb("v_aug", [P, BT, H, VW])
        oT = ph.sb("oT", [P, S])
        inv = ph.sb("inv", [P, BT, 4])
        o_rows = ph.sb("o_rows", [P, BT, D])
        o_cols = ph.sb("o_cols", [P, S])
        resid = ph.sb("resid", [P, BT, D])
        sem = {name: ph.sem(name) for name in (
            "sel_loaded", "sel_ready", "v_zero", "v_one", "cur_ready", "proj_done", "qk_ready", "hi_done", "lo_done",
            "spread_done", "k4_kept", "q4_kept", "s_done", "low_done", "exp_done", "t_done", "t0_kept", "t1_kept",
            "v_done", "v_kept", "pv_done", "o_kept", "ot_done", "inv_done", "o_norm", "oc_done", "oc_kept", "y_done",
            "y_used", "x_done")}
        (sel_loaded, sel_ready, v_zero, v_one, cur_ready, proj_done, qk_ready, hi_done, lo_done, spread_done, k4_kept,
         q4_kept, s_done, low_done, exp_done, t_done, t0_kept, t1_kept, v_done, v_kept, pv_done, o_kept, ot_done,
         inv_done, o_norm, oc_done, oc_kept, y_done, y_used, x_done) = sem.values()
        bq_scaled = ph.sb("bq_scaled", [P, 1])
        bq_ready = ph.sem("bq_ready")
        act_seen = ph.sem("act_seen")
        back = ph.sb("back", [P, NT, 2, D])
        fetched = [ph.sem(f"fetched{i}") for i in range(4)]
        gathered = ph.sem("gathered")
        added = ph.sem("added")
        ln_in = LayerNorm(ph, g, "ln_in")
        ln = LayerNorm(ph, g, "ln")
        block = ctx.enter_context(nc.Block())

        @block.sync
        def _(sp):
            sp.dma_start(sel_in[:], d["sel"]).then_inc(sel_loaded, 16)

        @block.tensor
        def _(pe):
            ln.start_turned(pe)
            ln_in.start_turned(pe)
            def project(b):
                pe.wait_ge(cur_ready, b + 1)
                for k in range(2):
                    mm = pe.matmul(psA[:, k * S:(k + 1) * S], g.wqkv1[:, k, :], cur[:], start=True, stop=True)
                mm.then_inc(proj_done, 1)

            def spread_parts(b, G):
                pe.wait_ge(lo_done, b + 1)
                for k in range(2):
                    for j, part in enumerate((qk_hi, qk_lo)):
                        mm = pe.matmul(psA[:, k * S:(k + 1) * S], sel[:, 2 * k + j, G, :], part[:, k, :], start=(j == 0), stop=(j == 1))
                mm.then_inc(spread_done, 1)

            def scores(b, p, k, has_unit):
                G = p // 2
                if k == 0:
                    pe.wait_ge(q4_kept, b * G4 + G + 1)
                if has_unit(p, 2):
                    pe.wait_ge(exp_done, b * 32 + 4 * p - 6 + 2 * k)
                for i in range(BT):
                    at = psS[:, 2 * (p % 2) + k, i * S:(i + 1) * S]
                    pe.matmul(at, q4[:, G % 2, i * P:(i + 1) * P], k4[:, G % 2, (2 * p + k) % 4, :], start=True, stop=False)
                    mm = pe.matmul(at, g.slopes[:, 2 * p + k, :], g.distance[:, i, :], start=False, stop=True)
                mm.then_inc(s_done, 1)

            def turn(b, p, k):
                pe.wait_ge(exp_done, b * 32 + 4 * p - 6 + 2 * k)
                if k == 0:
                    pe.wait_ge(t1_kept, b * PAIRS + p - 2)
                else:
                    pe.wait_ge(t0_kept, b * PAIRS + p - 1)
                u = 2 * ((p - 2) % 4) + k
                for j in range(BT):
                    for i in range(BT):
                        mm = pe.transpose(psT[:, j * S + i * P:j * S + (i + 1) * P], prob[:, u, i * S + j * P:i * S + (j + 1) * P], g.ident[:])
                mm.then_inc(t_done, 1)

            def values(b, p):
                gamma = b * G4 + (p - 4) // 2
                pe.wait_ge(t0_kept, gamma * 2 + 2)
                pe.wait_ge(t1_kept, gamma * 2 + 2)
                pe.wait_ge(v_kept, b + 1 if p >= 4 else b)
                pe.wait_ge(o_kept, gamma)
                for j in range(BT):
                    for hh in range(4):
                        h = 4 * (((p - 4) // 2) % G4) + hh
                        mm = pe.matmul(psO[hh * VW:(hh + 1) * VW, 0:S], v_aug[:, j, h, :], probT[:, h % 8, j * S:(j + 1) * S],
                                       start=(j == 0), stop=(j == BT - 1))
                mm.then_inc(pv_done, 1)

            def values_to_rows(gamma):
                pe.wait_ge(o_kept, gamma + 1)
                for i in range(BT):
                    mm = pe.transpose(psM[:, i * P:(i + 1) * P], oT[:, i * P:(i + 1) * P], g.ident[:])
                mm.then_inc(ot_done, 1)

            def first():
                ln_in.turn(pe, 0, psM)
                project(0)
                spread_parts(0, 0)

            def slots(b, new, prep, has_unit):
                for p in range(PAIRS):
                    old = has_unit(p, 8)
                    if new:
                        scores(b, p, 0, has_unit)
                    if has_unit(p, 2):
                        turn(b, p, 0)
                    if new:
                        scores(b, p, 1, has_unit)
                    if prep and p == 3:
                        if old:
                            pe.wait_ge(o_norm, b * G4 - 1)
                        else:
                            ln_in.wait_kept(pe, 1)
                        ln_in.turn(pe, b + 1, psM)
                    if p == 4 and old:
                        pe.wait_ge(o_norm, b * G4)
                        for i in range(BT):
                            mm = pe.transpose(psM[:, i * P:(i + 1) * P], o_rows[:, i, :], g.ident[:])
                        mm.then_inc(oc_done, 1)
                    if p == 7 and old:
                        if new:
                            pe.wait_ge(o_norm, b * G4 + 1)
                        else:
                            pe.wait_ge(y_used, b)
                        ln.turn(pe, b - 1, psM)
                    if new and p in (0, 2, 4):
                        pe.wait_ge(v_kept, b + 1) if p == 4 else pe.wait_ge(q4_kept, b * G4 + p // 2 + 1)
                        spread_parts(b, p // 2 + 1)
                    if prep and p == 5:
                        pe.wait_ge(q4_kept, b * G4 + 4)
                        project(b + 1)
                    if has_unit(p, 2):
                        turn(b, p, 1)
                    if p == 1 and old:
                        pe.wait_ge(o_norm, b * G4 - 2)
                        values_to_rows(b * G4 - 2)
                    if p == 4 and old:
                        pe.wait_ge(oc_kept, b)
                        for i in range(BT):
                            mm = pe.matmul(psM[:, i * P:(i + 1) * P], o_cols[:, i * P:(i + 1) * P], g.wo1[:], start=True, stop=True)
                        mm.then_inc(y_done, 1)
                    if p == 5 and new:
                        if old:
                            pe.wait_ge(y_used, b)
                        else:
                            ln_in.wait_kept(pe, 2)
                        values_to_rows(b * G4)
                    if p % 2 == 0 and has_unit(p, 4):
                        values(b, p)
                    if new and p == 3:
                        pe.wait_ge(q4_kept, b * G4 + 3)
                        for j in range(BT):
                            mm = pe.matmul(psA[:, j * P:(j + 1) * P], cur[:, j * P:(j + 1) * P], g.wqkv1[:, 2, :], start=True, stop=True)
                        mm.then_inc(v_done, 1)
                    if p == 3 and old:
                        if prep:
                            ln_in.wait_kept(pe, b + 2)
                        else:
                            pe.wait_ge(o_norm, b * G4 - 1)
                        values_to_rows(b * G4 - 1)
                    if p == 7 and new:
                        if old:
                            ln.wait_kept(pe, b)
                        else:
                            pe.wait_ge(o_norm, 1)
                        values_to_rows(b * G4 + 1)
                    if prep and p == 6:
                        spread_parts(b + 1, 0)

            pe.wait_ge(sel_ready, 1)
            rounds_ahead(pe, first, slots)

        @block.scalar
        def _(act):
            ln.start_kept(act)
            ln_in.start_kept(act)
            def keep_in(b):
                ln_in.keep(act, b, psM[:, 0:S], act_seen)

            def copy_cur(b):
                act.wait_ge(ln_in.kept, START + b + 1)
                act.sem_inc(act_seen, 1)
                nc.scalar.copy(cur[:], g.xnT[:, bass.ds(b * S, S)]).then_inc(cur_ready, 1)

            def keep_qk(b):
                act.wait_ge(proj_done, b + 1)
                nc.scalar.activation(qk[:, 0, :], psA[:, 0:S], ACT.Identity, bias=bq_scaled[:], scale=-SCALE).then_inc(qk_ready, 1)
                nc.scalar.activation(qk[:, 1, :], psA[:, S:2 * S], ACT.Identity, bias=g.bqk1[:, 1:2]).then_inc(qk_ready, 1)

            def keep_q4(b, G):
                act.wait_ge(k4_kept, b * G4 + G + 1)
                nc.scalar.copy(q4[:, G % 2, :], psA[:, 0:S]).then_inc(q4_kept, 1)

            def keep_t(b, p, k):
                if not (isinstance(b, int) and b == 0 and p < 6):
                    act.wait_ge(pv_done, b * G4 + (p - 4) // 2)
                act.wait_ge(t_done, b * H + 2 * p - 3 + k)
                nc.scalar.copy(probT[:, (2 * (p - 2) + k) % 8, :], psT[:]).then_inc(t1_kept if k else t0_kept, 1)

            def exps(b, p, has_unit):
                if has_unit(p, 4):
                    act.wait_ge(t_done, b * H + 2 * p - 6)
                for k in range(2):
                    act.wait_ge(low_done, b * H + 2 * p + k + 1)
                    for i in range(BT):
                        u = 2 * (p % 2) + k
                        nc.scalar.activation(prob[:, 2 * (p % 4) + k, i * S:(i + 1) * S], psS[:, u, i * S:(i + 1) * S], ACT.Exp,
                                             bias=low[:, p % 2, BT * k + i:BT * k + i + 1], scale=-1.0).then_inc(exp_done, 1)

            def first():
                act.wait_ge(sel_loaded, 16)
                nc.scalar.copy(sel[:], sel_in[:]).then_inc(sel_ready, 1)
                keep_in(0)
                copy_cur(0)
                act.wait_ge(bq_ready, 1)
                keep_qk(0)
                keep_q4(0, 0)

            def slots(b, new, prep, has_unit):
                for p in range(PAIRS):
                    old = has_unit(p, 8)
                    if has_unit(p, 2):
                        keep_t(b, p, 0)
                    if prep and p == 3:
                        keep_in(b + 1)
                    if p == 4 and old:
                        act.wait_ge(oc_done, b)
                        nc.scalar.copy(o_cols[:], psM[:, 0:S]).then_inc(oc_kept, 1)
                    if prep and p == 5:
                        keep_qk(b + 1)
                    if p == 7 and old:
                        ln.keep(act, b - 1, psM[:, 0:S], act_seen)
                    if p in SCALAR_TURNS and has_unit(p, 2):
                        keep_t(b, p, 1)
                    if prep and p == 7:
                        keep_q4(b + 1, 0)
                    if new:
                        exps(b, p, has_unit)
                    if new and p in (0, 2, 4):
                        keep_q4(b, p // 2 + 1)
                    if p % 2 == 0 and has_unit(p, 4):
                        gamma = b * G4 + (p - 4) // 2
                        if not (isinstance(b, int) and b == 0 and p == 4):
                            act.wait_ge(ot_done, gamma)
                        act.wait_ge(pv_done, gamma + 1)
                        nc.scalar.copy(oT[:], psO[:, 0:S]).then_inc(o_kept, 1)
                    if prep and p == 4:
                        act.wait_ge(v_done, b + 1)
                        copy_cur(b + 1)

            rounds_ahead(act, first, slots)

        @block.vector
        def _(dve):
            v = nc.vector
            seen = ph.sem("seen")

            def add_choice(b, k):
                if k == 0:
                    dve.wait_ge(gathered, b + 1)
                else:
                    dve.wait_ge(added, b * 2 * BT + BT)
                dve.sem_inc(seen, 1)
                for t in range(BT):
                    row = bass.ds(b * BT + t, 1)
                    v.scalar_tensor_tensor(out=g.x[:, row, :], in0=back[:, row, k, :], scalar=g.weight[:, k, row],
                                           in1=g.x[:, row, :], op0=ALU.mult, op1=ALU.add).then_inc(added, 1)

            def statistics(b):
                dve.wait_ge(added, b * 2 * BT + 2 * BT)
                dve.sem_inc(seen, 1)
                ln_in.stats(dve, b)
                ln_in.stats_landed(dve, b)
                dve.sem_inc(seen, 1)
                ln_in.aggregate(dve, b)

            def split(b):
                dve.wait_ge(qk_ready, b * 2 + 2)
                v.tensor_copy(qk_hi[:], qk[:]).then_inc(hi_done, 1)
                dve.wait_ge(hi_done, b + 1)
                v.tensor_tensor(qk_lo[:], qk[:], qk_hi[:].bitcast(F32), ALU.subtract).then_inc(lo_done, 1)

            def keep_k4(b, G):
                dve.wait_ge(spread_done, b * G4 + G + 1)
                if not (isinstance(b, int) and b == 0 and G < 2):
                    dve.wait_ge(s_done, b * H + 4 * G - 4)
                v.tensor_tensor(k4[:, G % 2, :, :], psA[:, S:2 * S].unsqueeze(1).to_broadcast([P, 4, S]),
                                g.head_mask[:].unsqueeze(2).to_broadcast([P, 4, S]), ALU.mult).then_inc(k4_kept, 1)

            def lows(b, p, has_unit):
                if has_unit(p, 2):
                    dve.wait_ge(exp_done, b * 32 + 4 * p - 4)
                for k in range(2):
                    dve.wait_ge(s_done, b * H + 2 * p + k + 1)
                    v.tensor_reduce(low[:, p % 2, BT * k:BT * k + BT], psS[:, 2 * (p % 2) + k, :].rearrange("p (i j) -> p i j", i=BT),
                                    AX.X, ALU.min).then_inc(low_done, 1)

            def keep_t(b, p):
                dve.wait_ge(t_done, b * H + 2 * p - 2)
                if not (isinstance(b, int) and b == 0 and p < 6):
                    dve.wait_ge(pv_done, b * G4 + (p - 4) // 2)
                v.tensor_copy(probT[:, (2 * (p - 2) + 1) % 8, :], psT[:]).then_inc(t1_kept, 1)

            def divide(gamma, G):
                dve.wait_ge(ot_done, gamma + 1)
                rows = psM[:, 0:S].rearrange("p (i h c) -> p i h c", i=BT, c=VW)
                v.reciprocal(inv[:], rows[:, :, :, DH1]).then_inc(inv_done, 1)
                dve.wait_ge(inv_done, gamma + 1)
                for i in range(BT):
                    x = v.tensor_tensor(o_rows[:, i, 4 * G * DH1:4 * (G + 1) * DH1].rearrange("p (h c) -> p h c", h=4),
                                        rows[:, i, :, 0:DH1], inv[:, i, :].unsqueeze(2).to_broadcast([P, 4, DH1]), ALU.mult)
                x.then_inc(o_norm, 1)

            def first():
                v.memset(v_aug[:], 0.0).then_inc(v_zero, 1)
                dve.wait_ge(v_zero, 1)
                v.memset(v_aug[:, :, :, DH1:DH1 + 1], 1.0).then_inc(v_one, 1)
                dve.wait_ge(v_one, 1)
                add_choice(0, 0)
                add_choice(0, 1)
                statistics(0)
                ln_in.apply(dve, 0)
                v.tensor_scalar(bq_scaled[:], g.bqk1[:, 0:1], -SCALE, None, ALU.mult).then_inc(bq_ready, 1)
                split(0)
                keep_k4(0, 0)

            def slots(b, new, prep, has_unit):
                for p in range(PAIRS):
                    old = has_unit(p, 8)
                    if prep and p == 7:
                        keep_k4(b + 1, 0)
                    if new:
                        lows(b, p, has_unit)
                    if p == 5 and old:
                        dve.wait_ge(x_done, b)
                        dve.sem_inc(seen, 1)
                        ln.stats(dve, b - 1)
                        ln.stats_landed(dve, b - 1)
                        dve.sem_inc(seen, 1)
                        ln.aggregate(dve, b - 1)
                    if new and p in (0, 2, 4):
                        keep_k4(b, p // 2 + 1)
                    if prep and p == 6:
                        split(b + 1)
                    if p == 6 and old:
                        ln.apply(dve, b - 1)
                    if has_unit(p, 2) and p not in SCALAR_TURNS:
                        keep_t(b, p)
                    if p == 0 and old:
                        divide(b * G4 - 3, 1)
                    if p == 1 and old:
                        divide(b * G4 - 2, 2)
                    if prep and p == 0:
                        add_choice(b + 1, 0)
                    if prep and p == 1:
                        add_choice(b + 1, 1)
                        statistics(b + 1)
                    if prep and p == 2:
                        ln_in.apply(dve, b + 1)
                    if p == 4 and old:
                        dve.wait_ge(y_done, b)
                        v.tensor_tensor(resid[:], psM[:, 0:S].rearrange("p (t d) -> p t d", t=BT),
                                        g.x[:, bass.ds((b - 1) * BT, BT), :], ALU.add).then_inc(y_used, 1)
                    if p == 5 and new:
                        if old:
                            dve.wait_ge(oc_done, b)
                        divide(b * G4, 0)
                    if p == 3 and new:
                        dve.wait_ge(v_done, b + 1)
                        v.tensor_tensor(v_aug[:, :, :, 0:DH1], psA[:, 0:S].rearrange("p (j h c) -> p j h c", j=BT, h=H),
                                        g.bv1[:], ALU.add).then_inc(v_kept, 1)
                    if p == 3 and old:
                        divide(b * G4 - 1, 3)

            rounds_ahead(dve, first, slots)

        @block.gpsimd
        def _(pool):
            def add_bias(b):
                pool.wait_ge(y_used, b + 1)
                nc.gpsimd.tensor_tensor(g.x[:, b * BT:(b + 1) * BT, :], resid[:], g.bo1[:], ALU.add).then_inc(x_done, 1)
                ln.rstd(pool, b)

            def fetch(b):
                for t in range(b * BT, b * BT + BT):
                    for k in range(2):
                        nc.gpsimd.indirect_dma_start(out=back[:, t, k, :], out_offset=None, in_=g.sorted_out,
                                                     in_offset=bass.IndirectOffsetOnAxis(ap=g.slot[:, k, t:t + 1], axis=0)).then_inc(fetched[b % 4], 16)

            def hand_over(b):
                pool.wait_ge(fetched[b % 4], 16 * 2 * BT * (b // 4 + 1))
                pool.sem_inc(gathered, 1)
                ln_in.rstd(pool, b)

            fetch(0)
            fetch(1)
            hand_over(0)
            for b in range(B):
                if b + 1 < B:
                    hand_over(b + 1)
                if b + 2 < B:
                    fetch(b + 2)
                if b:
                    add_bias(b - 1)
            add_bias(B - 1)


def layer1_context(nc, g, d):
    DH1 = D // H
    VW = 32
    SCALE = float(np.float32(DH1) ** np.float32(-0.5))
    with ExitStack() as ctx:
        ph = Phase(nc, ctx, "c1")
        psS = ph.ps("psS", [P, BT, H, L])
        psT = ph.ps("psT", [P, PAIRS, P])
        psO = ph.ps("psO", [P, 2, S])
        psM = ph.ps("psM", [P, 512])
        v_rows = ph.sb("v_rows", [P, B, D])
        kT = ph.sb("kT", [P, B * L])
        q_sb = ph.sb("q", [P, 2, S])
        k_bd = ph.sb("k_bd", [P, 2, H, L])
        v_bd = ph.sb("v_bd", [P, 2, PAIRS, VW])
        low = ph.sb("low", [P, BT, H])
        above = ph.sb("above", [P, BT, H, L])
        prob = ph.sb("prob", [P, BT, H * L])
        probT = ph.sb("probT", [P, PAIRS, BT, P])
        oT = ph.sb("oT", [P, 2, S])
        inv = ph.sb("inv", [P, 2 * BT, 4, 2])
        o_rows = ph.sb("o_rows", [P, BT, D])
        o_cols = ph.sb("o_cols", [P, S])
        resid = ph.sb("resid", [P, BT, D])
        (k_done, kT_ready, v_zero, v_set, v_ready, q_done, v_done, q_kept, v_kept, k_bd_ready, s_done, low_done,
         above_done, exp_done, t_done, t_kept, pv_done, o_kept, ot_done, inv_done, o_norm, oc_done, oc_kept, y_done, y_used,
         x_done, seen, pool_seen, act_seen) = (ph.sem(name) for name in (
            "k_done kT_ready v_zero v_set v_ready q_done v_done q_kept v_kept k_bd_ready s_done low_done "
            "above_done exp_done t_done t_kept pv_done o_kept ot_done inv_done o_norm oc_done oc_kept y_done y_used "
            "x_done seen pool_seen act_seen").split())
        ln = LayerNorm(ph, g, "ln")
        block = ctx.enter_context(nc.Block())
        ROUNDS = B // 4

        @block.tensor
        def _(pe):
            ln.start_turned(pe)
            pe.sem_inc(oc_done, START)
            for c in range(2):
                mm = pe.matmul(psT[:, 4 * c:4 * c + 4, :], g.wk2[:], g.ctxT[:, c * 512:(c + 1) * 512], start=True, stop=True)
            mm.then_inc(k_done, 1)
            for b in range(B):
                for j in range(2):
                    mm = pe.matmul(psS[j * L:(j + 1) * L, b // 8, b % 8 * 2:b % 8 * 2 + 2, :], g.ctxT[:, b * L:(b + 1) * L],
                                   g.wv2[:], start=True, stop=True)
            mm.then_inc(v_done, 1)
            pe.wait_ge(kT_ready, 1)
            pe.wait_ge(v_ready, 1)

            def turn_probs(n, i):
                pe.wait_ge(exp_done, n * BT - BT + i + 1)
                if not (isinstance(n, int) and n == 1 and i == 0):
                    pe.wait_ge(t_kept, n * BT - BT + i)
                for q in range(PAIRS):
                    mm = pe.transpose(psT[:, q, :], prob[:, i, q * P:(q + 1) * P], g.ident[:])
                mm.then_inc(t_done, 1)

            def scores(n, i, p, has_unit):
                if i == 0:
                    pe.wait_ge(q_kept, n + 1)
                    pe.wait_ge(k_bd_ready, n + 1)
                if has_unit(p, 1):
                    pe.wait_ge(above_done, n * BT - BT + i + 1)
                for c in range(2):
                    mm = pe.matmul(psS[:, i, c * 8:(c + 1) * 8, :], q_sb[:, p % 2, i * P:(i + 1) * P], k_bd[:, p % 2, c * 8:(c + 1) * 8, :],
                                   start=True, stop=True)
                mm.then_inc(s_done, 1)

            def slots(r, new, has_unit):
                for p in range(4):
                    n, last = r * 4 + p, 1 - p % 2
                    if new:
                        if has_unit(p, 4):
                            ln.wait_kept(pe, n - 3)
                        elif has_unit(p, 3):
                            pe.wait_ge(y_used, 1)
                        elif p:
                            pe.wait_ge(q_kept, p)
                        pe.matmul(psM[:, 0:S], g.wq2[:], g.xnT[:, bass.ds(n * S, S)], start=True, stop=True).then_inc(q_done, 1)
                    if has_unit(p, 2):
                        pe.wait_ge(o_kept, n - 1)
                        for j in range(2 * BT):
                            mm = pe.transpose(psO[:, j // BT, (j % BT) * P:(j % BT + 1) * P], oT[:, j // BT, (j % BT) * P:(j % BT + 1) * P], g.ident[:])
                        mm.then_inc(ot_done, 1)
                    if has_unit(p, 1):
                        turn_probs(n, 0)
                    if new:
                        scores(n, 0, p, has_unit)
                    if has_unit(p, 2):
                        pe.wait_ge(o_norm, n - 1)
                        if new:
                            pe.wait_ge(q_kept, n + 1)
                        else:
                            ln.wait_kept(pe, n - 3)
                        for i in range(BT):
                            mm = pe.transpose(psM[:, i * P:(i + 1) * P], o_rows[:, i, :], g.ident[:])
                        mm.then_inc(oc_done, 1)
                    if has_unit(p, 1):
                        turn_probs(n, 1)
                    if has_unit(p, 2):
                        pe.wait_ge(oc_kept, n - 1)
                        for i in range(BT):
                            mm = pe.matmul(psM[:, i * P:(i + 1) * P], o_cols[:, i * P:(i + 1) * P], g.wo2[:], start=True, stop=True)
                        mm.then_inc(y_done, 1)
                    if new:
                        scores(n, 1, p, has_unit)
                    if has_unit(p, 3):
                        if has_unit(p, 2):
                            pe.wait_ge(y_used, n - 1)
                        else:
                            ln.wait_kept(pe, n - 3)
                        ln.turn(pe, n - 3, psM)
                    if has_unit(p, 1):
                        pe.wait_ge(t_kept, n * BT)
                        pe.wait_ge(v_kept, n)
                        if has_unit(p, 2):
                            pe.wait_ge(o_norm, n - 1)
                        for q in range(2):
                            for c in range(4):
                                mm = pe.matmul(psO[c * VW:(c + 1) * VW, q, :], v_bd[:, last, 4 * q + c, :], probT[:, 4 * q + c, :, :],
                                               start=True, stop=True)
                        mm.then_inc(pv_done, 1)

            rounds(pe, slots, ROUNDS)

        @block.scalar
        def _(act):
            ln.start_kept(act)
            act.wait_ge(k_done, 1)
            nc.scalar.copy(kT[:], psT[:].rearrange("p q c -> p (q c)")).then_inc(kT_ready, 1)

            def exps(n, i):
                act.wait_ge(above_done, n * BT + i + 1)
                if not (isinstance(n, int) and n == 0):
                    act.wait_ge(t_done, n * BT - BT + i + 1)
                nc.scalar.activation(prob[:, i, :], above[:, i, :, :].rearrange("p h l -> p (h l)"), ACT.Exp, scale=-1.0).then_inc(exp_done, 1)

            def keep_t(n, i):
                act.wait_ge(t_done, n * BT - BT + i + 1)
                if not (isinstance(n, int) and n == 1):
                    act.wait_ge(pv_done, n - 1)
                nc.scalar.copy(probT[:, :, i, :], psT[:]).then_inc(t_kept, 1)

            def slots(r, new, has_unit):
                for p in range(4):
                    n, now = r * 4 + p, p % 2
                    if new:
                        act.wait_ge(q_done, n + 1)
                        if has_unit(p, 2):
                            act.wait_ge(s_done, n * BT - BT)
                        nc.scalar.activation(q_sb[:, now, :], psM[:, 0:S], ACT.Copy, scale=-SCALE).then_inc(q_kept, 1)
                    if has_unit(p, 1):
                        keep_t(n, 0)
                    if has_unit(p, 2):
                        act.wait_ge(oc_done, START + n - 1)
                        nc.scalar.copy(o_cols[:], psM[:, 0:S]).then_inc(oc_kept, 1)
                    if has_unit(p, 1):
                        keep_t(n, 1)
                    if new:
                        exps(n, 0)
                    if has_unit(p, 3):
                        ln.keep(act, n - 3, psM[:, 0:S], act_seen)
                    if has_unit(p, 1):
                        act.wait_ge(pv_done, n)
                        if has_unit(p, 2):
                            act.wait_ge(ot_done, n - 1)
                        nc.scalar.copy(oT[:], psO[:]).then_inc(o_kept, 1)
                    if new:
                        exps(n, 1)

            rounds(act, slots, ROUNDS)

        @block.gpsimd
        def _(pool):
            pool.wait_ge(kT_ready, 1)

            def slots(r, new, has_unit):
                for p in range(4):
                    n, now = r * 4 + p, p % 2
                    if new:
                        if has_unit(p, 2):
                            pool.wait_ge(s_done, n * BT - BT)
                            pool.sem_inc(pool_seen, 1)
                        nc.gpsimd.tensor_tensor(k_bd[:, now, :, :], kT[:, bass.ds(n * L, L)].unsqueeze(1).to_broadcast([P, H, L]),
                                                g.head_mask16[:].unsqueeze(2).to_broadcast([P, H, L]), ALU.mult).then_inc(k_bd_ready, 1)
                    if has_unit(p, 3):
                        ln.rstd(pool, n - 3)

            rounds(pool, slots, ROUNDS)

        @block.vector
        def _(dve):
            v = nc.vector
            v.memset(v_bd[:], 0.0).then_inc(v_zero, 1)
            dve.wait_ge(v_zero, 1)
            v.memset(v_bd[0:L, :, :, 2 * DH1:2 * DH1 + 1], 1.0).then_inc(v_set, 1)
            v.memset(v_bd[L:P, :, :, 2 * DH1 + 1:2 * DH1 + 2], 1.0).then_inc(v_set, 1)
            dve.wait_ge(v_set, 2)
            dve.wait_ge(v_done, 1)
            v.tensor_copy(v_rows[:], psS[:].rearrange("p i (c h) l -> p (i c) (h l)", h=2)).then_inc(v_ready, 1)
            dve.wait_ge(v_ready, 1)

            def scores_less_minimum(n, i, has_last):
                dve.wait_ge(s_done, n * BT + i + 1)
                if i == 0 and has_last:
                    dve.wait_ge(exp_done, n * BT)
                v.tensor_reduce(low[:, i, :], psS[:, i, :, :], AX.X, ALU.min).then_inc(low_done, 1)
                dve.wait_ge(low_done, n * BT + i + 1)
                v.tensor_tensor(above[:, i, :, :], psS[:, i, :, :], low[:, i, :].unsqueeze(2).to_broadcast([P, H, L]),
                                ALU.subtract).then_inc(above_done, 1)

            def slots(r, new, has_unit):
                for p in range(4):
                    n, now = r * 4 + p, p % 2
                    if has_unit(p, 2):
                        dve.wait_ge(ot_done, n - 1)
                        rows = psO[:].rearrange("p q (i c w) -> p (q i) c w", i=BT, w=VW)
                        v.reciprocal(inv[:], rows[:, :, :, 2 * DH1:2 * DH1 + 2]).then_inc(inv_done, 1)
                        dve.wait_ge(inv_done, n - 1)
                        if has_unit(p, 3):
                            dve.wait_ge(oc_done, START + n - 2)
                        for j in range(2 * BT):
                            q, i = j // BT, j % BT
                            x = v.tensor_tensor(o_rows[:, i, q * 64:(q + 1) * 64].rearrange("p (c h w) -> p c h w", c=4, h=2),
                                                rows[:, j, :, 0:2 * DH1].rearrange("p c (h w) -> p c h w", h=2),
                                                inv[:, j, :, :].unsqueeze(3).to_broadcast([P, 4, 2, DH1]), ALU.mult)
                        x.then_inc(o_norm, 1)
                    if new:
                        if has_unit(p, 2):
                            dve.wait_ge(pv_done, n - 1)
                            dve.sem_inc(seen, 1)
                        for k in range(2):
                            half = slice(k * L, (k + 1) * L)
                            x = v.tensor_copy(v_bd[half, now, :, k * DH1:(k + 1) * DH1],
                                              v_rows[half, bass.ds(n, 1), :].rearrange("p b (q h w) -> p (b q) h w", h=2, w=DH1)[:, :, k, :])
                        x.then_inc(v_kept, 1)
                    if has_unit(p, 3):
                        ln.apply(dve, n - 3)
                    if new:
                        scores_less_minimum(n, 0, has_unit(p, 1))
                    if has_unit(p, 2):
                        dve.wait_ge(y_done, n - 1)
                        rows = bass.ds((n - 2) * BT, BT)
                        v.tensor_tensor(resid[:], psM[:, 0:S].rearrange("p (t d) -> p t d", t=BT), g.x[:, rows, :], ALU.add).then_inc(y_used, 1)
                    if new:
                        scores_less_minimum(n, 1, False)
                    if has_unit(p, 2):
                        dve.wait_ge(y_used, n - 1)
                        v.tensor_tensor(g.x[:, rows, :], resid[:], g.bo2[:], ALU.add).then_inc(x_done, 1)
                        dve.wait_ge(x_done, n - 1)
                        dve.sem_inc(seen, 1)
                        ln.stats(dve, n - 2)
                        ln.stats_landed(dve, n - 2)
                        dve.sem_inc(seen, 1)
                        ln.aggregate(dve, n - 2)

            rounds(dve, slots, ROUNDS)


def layer1_route_and_shared(nc, g, d):
    UNITS = T // 512
    EVERY = 3
    EARLY = 4
    with ExitStack() as ctx:
        ph = Phase(nc, ctx, "r1")
        psL = ph.ps("psL", [P, NT, E])
        parts = ph.sb("parts", [P, 2, NT, E])
        logits_done = ph.sem("logits_done")
        route = Routing(ph, g, "rt")
        shared = SharedExpert(ph, g, "sh", g.shared_in1, g.shared_out1[:], False)
        block = ctx.enter_context(nc.Block())

        @block.tensor
        def _(pe):
            for t in range(NT):
                mm = pe.matmul(psL[:, t, :], g.xnT[:, t * P:(t + 1) * P], g.router1[:], start=True, stop=True)
            mm.then_inc(logits_done, 1)
            rounds(pe, shared.slots(lambda *a: shared.tensor(pe, *a)), T // 1024)

        @block.scalar
        def _(act):
            for n in range(UNITS):
                if n == EARLY:
                    route.exponent(act)
                shared.scalar(act, n, n % 2, True, n > 0)

        @block.vector
        def _(dve):
            v = nc.vector
            def meanwhile(step):
                n = step // EVERY - 1
                if step % EVERY == 0 and n < UNITS:
                    shared.vector(dve, n, n % 2, True, n > 0)

            route.meanwhile = meanwhile
            dve.wait_ge(logits_done, 1)
            route.choose(dve, psL[:], g.top, g.weight)
            for k in range(2):
                x = v.tensor_tensor(parts[:, k, :, :], g.top[:, k, :, :],
                                    g.weight[:, k, :].unsqueeze(2).to_broadcast([P, NT, E]), ALU.mult)
            route.then(dve, x)
            route.then(dve, v.tensor_tensor(g.share[:], parts[:, 0, :, :], parts[:, 1, :, :], ALU.add))
            for n in range(route.count // EVERY, UNITS):
                shared.vector(dve, n, n % 2, True, n > 0)
            shared.vector(dve, UNITS, UNITS % 2, False, True)


def layer1_experts(nc, g, d, out):
    FC = 4
    I1 = 512 // E
    with ExitStack() as ctx:
        ph = Phase(nc, ctx, "e1")
        psG = ph.ps("psG", [P, 2, 512])
        psU = ph.ps("psU", [P, 2, 512])
        psH = ph.ps("psH", [P, 512])
        psY = ph.ps("psY", [P, 512])
        cols = ph.sb("cols", [P, 2, P])
        act_sb = ph.sb("act", [P, 2, 512])
        wide = ph.sb("wide", [P, 2, 512])
        hid = ph.sb("hid", [P, 2, 512])
        hidT = ph.sb("hidT", [P, 512])
        (cols_ready, gate_in, in_done, silu_done, wide_done, hid_done, h_turned, h_kept, y_done, x_done, stored) = (
            ph.sem(name) for name in "cols_ready gate_in in_done silu_done wide_done hid_done h_turned h_kept y_done x_done stored".split())
        block = ctx.enter_context(nc.Block())

        def each(eng, slot):
            def body(r, new, has_unit):
                for p in range(4):
                    slot(r * 4 + p, p, new, has_unit(p, 2))
            rounds(eng, body, NT // 4)

        @block.tensor
        def _(pe):
            def slot(n, p, new, lagging):
                if lagging:
                    pe.wait_ge(hid_done, n - 1)
                    pe.wait_ge(h_kept, n - 2)
                    for c in range(FC):
                        mm = pe.transpose(psH[:, c * P:(c + 1) * P], hid[:, p % 2, c * P:(c + 1) * P], g.ident[:])
                    mm.then_inc(h_turned, 1)
                if new:
                    pe.wait_ge(cols_ready, n + 1)
                    if lagging:
                        pe.wait_ge(wide_done, n - 1)
                    pe.matmul(psG[:, p % 2, :], cols[:, p % 2, :], g.gate1[:], start=True, stop=True).then_inc(gate_in, 1)
                    pe.matmul(psU[:, p % 2, :], cols[:, p % 2, :], g.up1[:], start=True, stop=True).then_inc(in_done, 1)
                if lagging:
                    pe.wait_ge(h_kept, n - 1)
                    pe.wait_ge(x_done, n - 2)
                    for c in range(FC):
                        mm = pe.matmul(psY[:, 0:D], hidT[:, c * P:(c + 1) * P], g.down1[:, c, :], start=(c == 0), stop=(c == FC - 1))
                    mm.then_inc(y_done, 1)

            each(pe, slot)

        @block.scalar
        def _(act):
            def slot(n, p, new, lagging):
                if new:
                    if lagging:
                        act.wait_ge(in_done, n - 1)
                    nc.scalar.copy(cols[:, p % 2, :], g.xnT[:, bass.ds(n * P, P)]).then_inc(cols_ready, 1)
                if lagging:
                    act.wait_ge(h_turned, n - 1)
                    act.wait_ge(y_done, n - 2)
                    nc.scalar.copy(hidT[:], psH[:]).then_inc(h_kept, 1)
                if new:
                    act.wait_ge(gate_in, n + 1)
                    if lagging:
                        act.wait_ge(wide_done, n - 1)
                    nc.scalar.activation(act_sb[:, p % 2, :], psG[:, p % 2, :], ACT.Silu).then_inc(silu_done, 1)

            each(act, slot)

        @block.vector
        def _(dve):
            def slot(n, p, new, lagging):
                if new:
                    dve.wait_ge(silu_done, n + 1)
                    dve.wait_ge(in_done, n + 1)
                    if lagging:
                        dve.wait_ge(hid_done, n - 1)
                    nc.vector.tensor_tensor(wide[:, p % 2, :], act_sb[:, p % 2, :], psU[:, p % 2, :], ALU.mult).then_inc(wide_done, 1)
                if lagging:
                    dve.wait_ge(y_done, n - 1)
                    row = bass.ds(n - 2, 1)
                    nc.vector.tensor_tensor(g.x[:, row, :], g.x[:, row, :], psY[:, 0:D], ALU.add).then_inc(x_done, 1)

            each(dve, slot)

        @block.gpsimd
        def _(pool):
            def slot(n, p, new, lagging):
                if new:
                    pool.wait_ge(wide_done, n + 1)
                    if lagging:
                        pool.wait_ge(h_turned, n - 1)
                    pool.sem_inc(seen, 1)
                    nc.gpsimd.tensor_tensor(hid[:, p % 2, :].rearrange("p (e i) -> p e i", e=E),
                                            wide[:, p % 2, :].rearrange("p (e i) -> p e i", e=E),
                                            g.share[:, bass.ds(n, 1), :].rearrange("p t e -> p (t e)").unsqueeze(2).to_broadcast([P, E, I1]),
                                            ALU.mult).then_inc(hid_done, 1)

            seen = ph.sem("seen")
            each(pool, slot)

        @block.sync
        def _(sp):
            dst = out.rearrange("(t p) d -> p t d", p=P)
            with sp.Fori(0, NT // 4) as r:
                sp.wait_ge(x_done, r * 4 + 4)
                sp.dma_start(dst[:, bass.ds(r * 4, 4), :], g.x[:, bass.ds(r * 4, 4), :]).then_inc(stored, 16)
            sp.wait_ge(stored, 16 * (NT // 4))


class Globals:
    pass


def decoder(nc, d, out):
    g = Globals()
    first_loads, later_loads = [], []

    def hold(ctx, name, shape, dt=F32, load=True, first=False):
        t = ctx.enter_context(nc.sbuf_tensor(name, shape, dt))
        if load:
            (first_loads if first else later_loads).append((t[:], d[name]))
        return t

    with ExitStack() as ctx:
        g.x = hold(ctx, "x", [P, NT, D], load=False)
        g.xnT = hold(ctx, "xnT", [P, T], load=False)
        g.ident = hold(ctx, "ident", [P, P], load=False)
        g.eps = hold(ctx, "eps", [P, BT], load=False)
        g.minus_half = hold(ctx, "minus_half", [P, BT], load=False)
        g.ctx = hold(ctx, "ctx", [P, B * L // P, D], load=False)
        g.ctxT = hold(ctx, "ctxT", [P, B * L], load=False)
        g.countdown = hold(ctx, "countdown", [P, NT, E])
        g.top = hold(ctx, "top", [P, 2, NT, E], load=False)
        g.slot = hold(ctx, "slot", [P, 2, NT], I32, load=False)
        g.weight = hold(ctx, "weight", [P, 2, NT], load=False)
        g.wqkv1 = hold(ctx, "wqkv1", [P, 3, D])
        g.bqk1 = hold(ctx, "bqk1", [P, 2])
        g.bv1 = hold(ctx, "bv1", [P, BT, H, D // H])
        g.wo1 = hold(ctx, "wo1", [P, D])
        g.bo1 = hold(ctx, "bo1", [P, BT, D])
        g.head_mask = hold(ctx, "head_mask", [P, 4])
        g.slopes = hold(ctx, "slopes", [P, H, P], BF16)
        g.distance = hold(ctx, "distance", [P, BT, S], BF16)
        g.wq2 = hold(ctx, "wq2", [P, D])
        g.wk2 = hold(ctx, "wk2", [P, D])
        g.wv2 = hold(ctx, "wv2", [P, D])
        g.wo2 = hold(ctx, "wo2", [P, D])
        g.bo2 = hold(ctx, "bo2", [P, BT, D])
        g.head_mask16 = hold(ctx, "head_mask16", [P, H])
        g.router1 = hold(ctx, "router1", [P, E])
        g.shared_in1 = hold(ctx, "shared_in1", [P, 2 * P])
        g.shared_out1 = hold(ctx, "shared_out1", [P, D])
        g.gate1 = hold(ctx, "gate1", [P, 512])
        g.up1 = hold(ctx, "up1", [P, 512])
        g.down1 = hold(ctx, "down1", [P, 4, D])
        g.share = hold(ctx, "share", [P, NT, E], load=False)
        g.sorted_in = nc.dram_tensor("sorted_in", (MOE_BLOCKS * P, D), F32, kind="Internal").ap()
        g.sorted_out = nc.dram_tensor("sorted_out", (MOE_BLOCKS * P, D), F32, kind="Internal").ap()
        with ExitStack() as layer0:
            g.rows = hold(layer0, "rows", [P, NT, D], load=False)
            g.wcat = hold(layer0, "wcat", [P, 2, 2 * D])
            g.bcat = hold(layer0, "bcat", [P, 2 * BT, 2 * D])
            g.gamma = hold(layer0, "gamma", [P, BT, D])
            g.beta = hold(layer0, "beta", [P, BT, D])
            g.router = hold(layer0, "router", [P, E])
            g.block_index = hold(layer0, "block_index", [P, MOE_BLOCKS])
            g.before_mask = hold(layer0, "before_mask", [P, P], BF16)
            g.ones_bf = hold(layer0, "ones_bf", [P, P], BF16)
            g.expert = hold(layer0, "expert", [P, MOE_BLOCKS], I32, load=False)
            g.shared_in0 = hold(layer0, "shared_in0", [P, 2 * P])
            g.shared_out0 = hold(layer0, "shared_out0", [P, D])
            with ExitStack() as attention0:
                g.G = hold(attention0, "G", [P, H, D], load=False)
                g.wv = hold(attention0, "wv", [P, H * DH0], first=True)
                g.wo = hold(attention0, "wo", [P, PAIRS, D], first=True)
                g.bias0 = hold(attention0, "bias0", [P, H, CAUSAL], first=True)
                g.bo = hold(attention0, "bo", [P, BT, D], first=True)
                load_and_prepare(nc, g, d, first_loads)
                layer0_attention(nc, g, d, later_loads)
            g.in_lo = hold(layer0, "in_lo", [P, 2 * E, F0], F32R, load=False)
            g.down = hold(layer0, "down", [P, E * F0 // P, D], load=False)
            layer0_context(nc, g, d)
            layer0_route(nc, g, d)
            with ExitStack() as experts0:
                g.in_hi = hold(experts0, "in_hi", [P, 2 * E, F0], F32R, load=False)
                layer0_shared_and_dispatch(nc, g, d)
                layer0_experts(nc, g, d)
        layer1_attention(nc, g, d)
        layer1_context(nc, g, d)
        layer1_route_and_shared(nc, g, d)
        layer1_experts(nc, g, d, out)


def layout(a):
    c = np.ascontiguousarray
    bf16 = mybir.dt.np(BF16)
    pairs = lambda w: c(w.T.reshape(PAIRS, P, D).transpose(1, 0, 2))
    i = np.arange(S, dtype=np.float32)
    slope = (1.0 / np.power(np.float32((2.0 ** 8) ** (1.0 / H)), np.arange(1, H + 1, dtype=np.float32))).astype(np.float32)
    minus = -(slope[:, None, None] * (i[:, None] - i[None, :])).astype(np.float32)
    minus = np.where(i[:, None] >= i[None, :], minus, np.float32(MASKED))
    bias0 = np.concatenate([minus[:, :P, :P], minus[:, P:, :]], axis=2).transpose(1, 0, 2)
    dh = D // H
    part, head, at = np.meshgrid(np.arange(4), np.arange(4), np.arange(dh), indexing="ij")
    part, head, at = part.ravel(), head.ravel(), at.ravel()
    sel = np.zeros((P, 4, H // 4, P), np.float32)
    for kind, parts in enumerate(((0, 1), (2, 3), (0, 2), (1, 3))):
        for group in range(H // 4):
            for r in range(P):
                if part[r] in parts:
                    sel[(4 * group + head[r]) * dh + at[r], kind, group, r] = 1
    w1 = a["L1_attn_qkv_w"].reshape(H, 3, dh, D)
    b1 = a["L1_attn_qkv_b"].reshape(H, 3, dh)
    tok = np.arange(S).reshape(BT, P)
    return {
        "sel": sel,
        "wq2": c(a["L1_xattn_w_q"].T),
        "wk2": c(a["L1_xattn_w_kv"][:D].T),
        "wv2": c(a["L1_xattn_w_kv"][D:].T),
        "wo2": c(a["L1_xattn_w_out"].T),
        "bo2": c(np.broadcast_to(a["L1_xattn_b_out"], (P, BT, D))),
        "head_mask16": c((np.arange(P)[:, None] // dh == np.arange(H)).astype(np.float32)),
        "router1": c(a["L1_ffn_gate_w"]),
        "shared_in1": c(np.concatenate([a["L1_ffn_sg"], a["L1_ffn_su"]], axis=1)),
        "shared_out1": c(a["L1_ffn_sd"]),
        "gate1": c(a["L1_ffn_wg"].transpose(1, 0, 2).reshape(D, 512)),
        "up1": c(a["L1_ffn_wu"].transpose(1, 0, 2).reshape(D, 512)),
        "down1": c(a["L1_ffn_wd"].reshape(4, P, D).transpose(1, 0, 2)),
        "wqkv1": c(w1.transpose(3, 1, 0, 2).reshape(D, 3, D)),
        "bqk1": c(b1[:, :2].transpose(0, 2, 1).reshape(D, 2)),
        "bv1": c(np.broadcast_to(b1[:, 2], (P, BT, H, dh))),
        "wo1": c(a["L1_attn_out_w"].T),
        "bo1": c(np.broadcast_to(a["L1_attn_out_b"], (P, BT, D))),
        "head_mask": c((head[:, None] == np.arange(4)).astype(np.float32)),
        "slopes": c((np.eye(P)[:, None, :] * (0.5 ** np.arange(H))[None, :, None]).astype(bf16)),
        "distance": c(np.abs(tok.T[:, :, None] - np.arange(S)).astype(bf16)),
        "x": c(a["x"].reshape(T, D)),
        "ctx": c(a["ctx_1024"].reshape(B * L // P, P, D).transpose(1, 0, 2)),
        "ident": np.eye(P, dtype=np.float32),
        "wqT": pairs(a["L0_attn_Wq"]),
        "wkT": pairs(a["L0_attn_Wk"]),
        "wv": c(a["L0_attn_Wv"]),
        "wo": c(a["L0_attn_Wo"].reshape(PAIRS, P, D).transpose(1, 0, 2)),
        "bias0": c(bias0),
        "wcat": c(np.concatenate([a["L0_xattn_W_lin"].reshape(2, D, D), a["L0_xattn_W_gate"].reshape(2, D, D)], axis=2).transpose(1, 0, 2)),
        "bcat": c(np.broadcast_to(np.concatenate([a["L0_xattn_b_lin"], a["L0_xattn_b_gate"]]), (P, 2 * BT, 2 * D))),
        "gamma": c(np.broadcast_to(a["L0_ffn_ln_gamma"], (P, BT, D))),
        "beta": c(np.broadcast_to(a["L0_ffn_ln_beta"], (P, BT, D))),
        "router": c(a["L0_ffn_router_w"]),
        "countdown": c(np.broadcast_to(np.arange(E, 0, -1, dtype=np.float32), (P, NT, E))),
        "block_index": c(np.broadcast_to(np.arange(MOE_BLOCKS, dtype=np.float32), (P, MOE_BLOCKS))),
        "before_mask": np.triu(np.ones((P, P), np.float32), 1).astype(bf16),
        "ones_bf": np.ones((P, P), bf16),
        "gate_up": c(a["L0_ffn_gate_up_w"].reshape(E, D, 2, F0).transpose(1, 0, 2, 3).reshape(D, 2 * E, F0)),
        "down": c(a["L0_ffn_down_w"].reshape(E, F0 // P, P, D).transpose(2, 0, 1, 3).reshape(P, E * F0 // P, D)),
        "shared_in0": c(a["L0_ffn_shared_gate_up_w"]),
        "shared_out0": c(a["L0_ffn_shared_down_w"]),
        "bo": c(np.broadcast_to(a["L0_attn_bo"], (P, BT, D))),
    }


def kernel(**inputs):
    import concourse.bacc as bacc
    from concourse.bass_utils import run_bass_kernel_spmd

    nc = bacc.Bacc("TRN2", target_bir_lowering=False, num_devices=1)
    arrays = {f"in_{k}": v for k, v in layout({k: np.asarray(v) for k, v in inputs.items()}).items()}
    d = {k[3:]: nc.dram_tensor(k, v.shape, mybir.dt.from_np(v.dtype), kind="ExternalInput").ap() for k, v in arrays.items()}
    out = nc.dram_tensor("out", (T, D), F32, kind="ExternalOutput").ap()
    decoder(nc, d, out)
    r = run_bass_kernel_spmd(nc, [arrays], core_ids=[0])
    return np.asarray(r.results[0]["out"]).reshape(B, S, D)
```
